# Optimizing a Trainium2 kernel written in Bass

```python
import numpy as np
import jax
import jax.numpy as jnp

def _softmax(x, axis=-1):
    return jax.nn.softmax(x, axis=axis)

def _gelu(x):
    return jax.nn.gelu(x, approximate=True)

def _silu(x):
    return jax.nn.silu(x)

def _sigmoid(x):
    return jax.nn.sigmoid(x)

def _layernorm(x, axis=-1, eps=1e-05):
    m = jnp.mean(x, axis=axis, keepdims=True)
    v = jnp.var(x, axis=axis, keepdims=True)
    return (x - m) / jnp.sqrt(v + eps)

def _scatter_add(tgt, idx, src, axis=0):
    return tgt.at[idx].add(src)

def _segment_sum(src, seg, n):
    return jax.ops.segment_sum(src, seg, n)
kernel_name = 'mk_gnn_preln_d4_gnn_r64_479575'

def setup_inputs(seed: int=0):
    np.random.seed(seed)
    _w = jnp.asarray

    def _rec_inputs():
        import jax
        import jax.numpy as jnp
        _gk = jax.random.key(seed)
        x = -0.0001006 + 1 * jax.random.normal(jax.random.fold_in(_gk, 1), (100000, 96), jnp.float32)
        src = jax.random.randint(jax.random.fold_in(_gk, 2), (50000,), 0, 100000, jnp.int32)
        dst = jnp.minimum((100000 * jax.random.uniform(jax.random.fold_in(_gk, 3), (50000,)) ** 2.0).astype(jnp.int32), 99999)
        _o = jnp.argsort(dst, stable=True)
        src = src[_o]
        dst = dst[_o]
        edge_attr_32 = 0.000196303 + 1.00016 * jax.random.normal(jax.random.fold_in(_gk, 12), (50000, 32), jnp.float32)
        edge_attr_96 = jax.random.uniform(jax.random.fold_in(_gk, 13), (50000, 96), jnp.float32, 0.0, 1.11111)
        return (x, src, dst, edge_attr_32, edge_attr_96)
    x, src, dst, edge_attr_32, edge_attr_96 = _rec_inputs()

    def _L0_gnn_setup():
        import jax, jax.numpy as jnp
        import numpy as np
        N, E = (50000, 12500)
        ND, ED = (96, 32)

        def _gelu(x):
            return jax.nn.gelu(x, approximate=False)
        key = jax.random.key(seed)
        ks = jax.random.split(key, 16)
        s = lambda fan_in: 1.0 / np.sqrt(fan_in)
        inp = {'x': jax.random.normal(ks[0], (N, ND), jnp.float32), 'edge_index': jax.random.randint(ks[1], (2, E), 0, N, jnp.int32), 'edge_attr': jax.random.normal(ks[2], (E, ED), jnp.float32), 'mW1': jax.random.uniform(ks[3], (ND + ED, ND), jnp.float32, -s(ND + ED), s(ND + ED)), 'mb1': jnp.zeros((ND,), jnp.float32), 'mW2': jax.random.uniform(ks[4], (ND, ND), jnp.float32, -s(ND), s(ND)), 'mb2': jnp.zeros((ND,), jnp.float32), 'gW1': jax.random.uniform(ks[5], (ND + ED, ND), jnp.float32, -s(ND + ED), s(ND + ED)), 'gb1': jnp.zeros((ND,), jnp.float32), 'gW2': jax.random.uniform(ks[6], (ND, 1), jnp.float32, -s(ND), s(ND)), 'gb2': jnp.zeros((1,), jnp.float32), 'uW1': jax.random.uniform(ks[7], (2 * ND, ND), jnp.float32, -s(2 * ND), s(2 * ND)), 'ub1': jnp.zeros((ND,), jnp.float32), 'uW2': jax.random.uniform(ks[8], (ND, ND), jnp.float32, -s(ND), s(ND)), 'ub2': jnp.zeros((ND,), jnp.float32), 'ln_g': jnp.ones((ND,), jnp.float32), 'ln_b': jnp.zeros((ND,), jnp.float32)}
        return inp
    _L0_gnn_all = _L0_gnn_setup()
    _L0_gnn_in = {k: v for k, v in _L0_gnn_all.items() if k in ('mW1', 'mb1', 'mW2', 'mb2', 'gW1', 'gb1', 'gW2', 'gb2', 'uW1', 'ub1', 'uW2', 'ub2', 'ln_g', 'ln_b')}
    del _L0_gnn_all

    def _L1_gnn_setup():
        import jax, jax.numpy as jnp
        import numpy as np
        N_NODES = 50000
        N_EDGES = 12500
        D = 96
        EDGE_DROP = 0.1
        key = jax.random.key(seed)
        ks = jax.random.split(key, 12)
        d2 = 2 * D
        s1 = 1.0 / np.sqrt(d2)
        s2 = 1.0 / np.sqrt(D)
        h = jax.random.normal(ks[0], (N_NODES, D), dtype=jnp.float32)
        src = jax.random.randint(ks[1], (N_EDGES,), 0, N_NODES, dtype=jnp.int32)
        dst = jax.random.randint(ks[2], (N_EDGES,), 0, N_NODES, dtype=jnp.int32)
        Wm1 = jax.random.uniform(ks[3], (d2, D), jnp.float32, -s1, s1)
        bm1 = jnp.zeros((D,), jnp.float32)
        Wm2 = jax.random.uniform(ks[4], (D, D), jnp.float32, -s2, s2)
        bm2 = jnp.zeros((D,), jnp.float32)
        Wu1 = jax.random.uniform(ks[5], (d2, D), jnp.float32, -s1, s1)
        bu1 = jnp.zeros((D,), jnp.float32)
        Wu2 = jax.random.uniform(ks[6], (D, D), jnp.float32, -s2, s2)
        bu2 = jnp.zeros((D,), jnp.float32)
        keep = 1.0 - EDGE_DROP
        drop_mask = (jax.random.uniform(ks[7], (N_EDGES, D)) < keep).astype(jnp.float32) / keep
        return {'h': h, 'Wm1': Wm1, 'bm1': bm1, 'Wm2': Wm2, 'bm2': bm2, 'Wu1': Wu1, 'bu1': bu1, 'Wu2': Wu2, 'bu2': bu2, 'drop_mask': drop_mask, 'src': src, 'dst': dst}
    _L1_gnn_all = _L1_gnn_setup()
    _L1_gnn_in = {k: v for k, v in _L1_gnn_all.items() if k in ('Wm1', 'bm1', 'Wm2', 'bm2', 'Wu1', 'bu1', 'Wu2', 'bu2')}
    del _L1_gnn_all

    def _L2_gnn_setup():
        import jax, jax.numpy as jnp
        import numpy as np
        N_NODES = 50000
        N_EDGES = 12500
        D_IN = 96
        D_OUT = 96
        key = jax.random.key(seed)
        k1, k2, k3, k4 = jax.random.split(key, 4)
        x = jax.random.normal(k1, (N_NODES, D_IN), dtype=jnp.float32)
        edge_index = jax.random.randint(k2, (2, N_EDGES), 0, N_NODES, dtype=jnp.int64)
        W = jax.random.normal(k3, (D_IN, D_OUT), dtype=jnp.float32) * (1.0 / np.sqrt(D_IN))
        b = jax.random.normal(k4, (D_OUT,), dtype=jnp.float32) * 0.01
        return {'x': x, 'edge_index': edge_index, 'W': W, 'b': b}
    _L2_gnn_all = _L2_gnn_setup()
    _L2_gnn_in = {k: v for k, v in _L2_gnn_all.items() if k in ('W', 'b')}
    del _L2_gnn_all

    def _L3_gnn_setup():
        import jax, jax.numpy as jnp
        import numpy as np
        N_NODES = 50000
        N_EDGES = 12500
        D = 96
        N_LAYERS = 3

        def _gnn_forward(h, src, dst, weights, biases):
            N = h.shape[0]
            ones = jnp.ones(src.shape[0], dtype=h.dtype)
            out_deg = jnp.clip(jax.ops.segment_sum(ones, src, num_segments=N), 1.0)
            in_deg = jnp.clip(jax.ops.segment_sum(ones, dst, num_segments=N), 1.0)
            norm_src = (out_deg ** (-0.5))[:, None]
            norm_dst = (in_deg ** (-0.5))[:, None]
            for W, b in zip(weights, biases):
                x = h * norm_src
                m = jax.ops.segment_sum(x[src], dst, num_segments=N)
                m = m * norm_dst
                h = jax.nn.relu(m @ W + b)
            return h
        key = jax.random.key(seed)
        ks = jax.random.split(key, 3 + 2 * N_LAYERS)
        h = jax.random.normal(ks[0], (N_NODES, D), dtype=jnp.float32)
        src = jax.random.randint(ks[1], (N_EDGES,), 0, N_NODES, dtype=jnp.int64)
        dst = jax.random.randint(ks[2], (N_EDGES,), 0, N_NODES, dtype=jnp.int64)
        inp = {'h': h, 'src': src, 'dst': dst}
        scale = 1.0 / np.sqrt(D)
        for i in range(N_LAYERS):
            inp[f'W{i}'] = jax.random.normal(ks[3 + 2 * i], (D, D), dtype=jnp.float32) * scale
            inp[f'b{i}'] = jnp.zeros((D,), dtype=jnp.float32)
        return inp
    _L3_gnn_all = _L3_gnn_setup()
    _L3_gnn_in = {k: v for k, v in _L3_gnn_all.items() if k in ('W0', 'b0', 'W1', 'b1', 'W2', 'b2')}
    del _L3_gnn_all
    return {'x': x, 'src': src, 'dst': dst, 'edge_attr_32': edge_attr_32, 'edge_attr_96': edge_attr_96, 'L0_gnn_mW1': _L0_gnn_in['mW1'], 'L0_gnn_mb1': _L0_gnn_in['mb1'], 'L0_gnn_mW2': _L0_gnn_in['mW2'], 'L0_gnn_mb2': _L0_gnn_in['mb2'], 'L0_gnn_gW1': _L0_gnn_in['gW1'], 'L0_gnn_gb1': _L0_gnn_in['gb1'], 'L0_gnn_gW2': _L0_gnn_in['gW2'], 'L0_gnn_gb2': _L0_gnn_in['gb2'], 'L0_gnn_uW1': _L0_gnn_in['uW1'], 'L0_gnn_ub1': _L0_gnn_in['ub1'], 'L0_gnn_uW2': _L0_gnn_in['uW2'], 'L0_gnn_ub2': _L0_gnn_in['ub2'], 'L0_gnn_ln_g': _L0_gnn_in['ln_g'], 'L0_gnn_ln_b': _L0_gnn_in['ln_b'], 'L1_gnn_Wm1': _L1_gnn_in['Wm1'], 'L1_gnn_bm1': _L1_gnn_in['bm1'], 'L1_gnn_Wm2': _L1_gnn_in['Wm2'], 'L1_gnn_bm2': _L1_gnn_in['bm2'], 'L1_gnn_Wu1': _L1_gnn_in['Wu1'], 'L1_gnn_bu1': _L1_gnn_in['bu1'], 'L1_gnn_Wu2': _L1_gnn_in['Wu2'], 'L1_gnn_bu2': _L1_gnn_in['bu2'], 'L2_gnn_W': _L2_gnn_in['W'], 'L2_gnn_b': _L2_gnn_in['b'], 'L3_gnn_W0': _L3_gnn_in['W0'], 'L3_gnn_b0': _L3_gnn_in['b0'], 'L3_gnn_W1': _L3_gnn_in['W1'], 'L3_gnn_b1': _L3_gnn_in['b1'], 'L3_gnn_W2': _L3_gnn_in['W2'], 'L3_gnn_b2': _L3_gnn_in['b2']}

def reference(x, src, dst, edge_attr_32, edge_attr_96, L0_gnn_mW1, L0_gnn_mb1, L0_gnn_mW2, L0_gnn_mb2, L0_gnn_gW1, L0_gnn_gb1, L0_gnn_gW2, L0_gnn_gb2, L0_gnn_uW1, L0_gnn_ub1, L0_gnn_uW2, L0_gnn_ub2, L0_gnn_ln_g, L0_gnn_ln_b, L1_gnn_Wm1, L1_gnn_bm1, L1_gnn_Wm2, L1_gnn_bm2, L1_gnn_Wu1, L1_gnn_bu1, L1_gnn_Wu2, L1_gnn_bu2, L2_gnn_W, L2_gnn_b, L3_gnn_W0, L3_gnn_b0, L3_gnn_W1, L3_gnn_b1, L3_gnn_W2, L3_gnn_b2):
    import jax
    import jax.numpy as jnp

    def _L0_gnn_ref(x, edge_index, edge_attr, mW1, mb1, mW2, mb2, gW1, gb1, gW2, gb2, uW1, ub1, uW2, ub2, ln_g, ln_b):
        import jax, jax.numpy as jnp
        import numpy as np
        N, E = (50000, 12500)
        ND, ED = (96, 32)

        def _gelu(x):
            return jax.nn.gelu(x, approximate=False)
        src, dst = (edge_index[0], edge_index[1])
        edge_input = jnp.concatenate([x[src], edge_attr], axis=-1)
        messages = _gelu(edge_input @ mW1 + mb1) @ mW2 + mb2
        gates = jax.nn.sigmoid(_gelu(edge_input @ gW1 + gb1) @ gW2 + gb2)
        aggregated = jax.ops.segment_sum(messages * gates, dst, num_segments=x.shape[0])
        combined = jnp.concatenate([x, aggregated], axis=-1)
        update = _gelu(combined @ uW1 + ub1) @ uW2 + ub2
        h = x + update
        mu = jnp.mean(h, axis=-1, keepdims=True)
        var = jnp.mean(jnp.square(h - mu), axis=-1, keepdims=True)
        return (h - mu) * jax.lax.rsqrt(var + 1e-05) * ln_g + ln_b

    def _L1_gnn_ref(h, Wm1, bm1, Wm2, bm2, Wu1, bu1, Wu2, bu2, drop_mask, src, dst):
        import jax, jax.numpy as jnp
        import numpy as np
        N_NODES = 50000
        N_EDGES = 12500
        D = 96
        EDGE_DROP = 0.1
        n = h.shape[0]
        e = jnp.concatenate([h[src], h[dst]], axis=-1)
        e = jax.nn.relu(e @ Wm1 + bm1) @ Wm2 + bm2
        e = e * drop_mask
        m = jax.ops.segment_sum(e, dst, num_segments=n)
        z = jnp.concatenate([h, m], axis=-1)
        h_new = jax.nn.relu(z @ Wu1 + bu1) @ Wu2 + bu2
        return h_new

    def _L2_gnn_ref(x, edge_index, W, b):
        import jax, jax.numpy as jnp
        import numpy as np
        N_NODES = 50000
        N_EDGES = 12500
        D_IN = 96
        D_OUT = 96
        num_nodes = x.shape[0]
        src, dst = (edge_index[0], edge_index[1])
        messages = x[src] @ W + b
        out = jax.ops.segment_sum(messages, dst, num_segments=num_nodes)
        deg = jax.ops.segment_sum(jnp.ones((dst.shape[0],), dtype=x.dtype), dst, num_segments=num_nodes)
        deg = jnp.clip(deg, 1.0, None)
        return out / deg[:, None]

    def _L3_gnn_ref(h, src, dst, W0, b0, W1, b1, W2, b2):
        import jax, jax.numpy as jnp
        import numpy as np
        N_NODES = 50000
        N_EDGES = 12500
        D = 96
        N_LAYERS = 3

        def _gnn_forward(h, src, dst, weights, biases):
            N = h.shape[0]
            ones = jnp.ones(src.shape[0], dtype=h.dtype)
            out_deg = jnp.clip(jax.ops.segment_sum(ones, src, num_segments=N), 1.0)
            in_deg = jnp.clip(jax.ops.segment_sum(ones, dst, num_segments=N), 1.0)
            norm_src = (out_deg ** (-0.5))[:, None]
            norm_dst = (in_deg ** (-0.5))[:, None]
            for W, b in zip(weights, biases):
                x = h * norm_src
                m = jax.ops.segment_sum(x[src], dst, num_segments=N)
                m = m * norm_dst
                h = jax.nn.relu(m @ W + b)
            return h
        return _gnn_forward(h, src, dst, (W0, W1, W2), (b0, b1, b2))
    edge_index = jnp.stack([src, dst])
    h = jnp.maximum(_layernorm(x, axis=-1), 0.0)
    x = x + _L0_gnn_ref(h, edge_index, edge_attr_32, L0_gnn_mW1, L0_gnn_mb1, L0_gnn_mW2, L0_gnn_mb2, L0_gnn_gW1, L0_gnn_gb1, L0_gnn_gW2, L0_gnn_gb2, L0_gnn_uW1, L0_gnn_ub1, L0_gnn_uW2, L0_gnn_ub2, L0_gnn_ln_g, L0_gnn_ln_b)
    h = jnp.maximum(_layernorm(x, axis=-1), 0.0)
    x = x + _L1_gnn_ref(h, L1_gnn_Wm1, L1_gnn_bm1, L1_gnn_Wm2, L1_gnn_bm2, L1_gnn_Wu1, L1_gnn_bu1, L1_gnn_Wu2, L1_gnn_bu2, edge_attr_96, src, dst)
    h = jnp.maximum(_layernorm(x, axis=-1), 0.0)
    x = x + _L2_gnn_ref(h, edge_index, L2_gnn_W, L2_gnn_b)
    h = jnp.maximum(_layernorm(x, axis=-1), 0.0)
    x = x + _L3_gnn_ref(h, src, dst, L3_gnn_W0, L3_gnn_b0, L3_gnn_W1, L3_gnn_b1, L3_gnn_W2, L3_gnn_b2)
    return x

_drawn_inputs = setup_inputs


def setup_inputs(seed=0):
    import zlib

    import numpy as np

    out = dict(_drawn_inputs(seed))
    spreads = {'L0_gnn_mb1': (0.0, 2.0),
     'L0_gnn_mb2': (0.0, 2.0),
     'L0_gnn_gb1': (0.0, 0.8),
     'L0_gnn_ub1': (0.0, 0.268),
     'L0_gnn_ub2': (0.0, 0.1),
     'L0_gnn_ln_g': (1.0, 0.2),
     'L0_gnn_ln_b': (0.0, 0.1),
     'L1_gnn_bm1': (0.0, 0.8),
     'L1_gnn_bm2': (0.0, 0.8),
     'L1_gnn_bu1': (0.0, 1.215),
     'L1_gnn_bu2': (0.0, 0.499),
     'L3_gnn_b0': (0.0, 0.8),
     'L3_gnn_b1': (0.0, 0.794),
     'L3_gnn_b2': (0.0, 0.8)}
    factors = {'edge_attr_32': 8.0,
     'edge_attr_96': 8.0,
     'L0_gnn_mW1': 8.0,
     'L0_gnn_mW2': 6.809,
     'L0_gnn_gW1': 8.0,
     'L0_gnn_gW2': 8.0,
     'L1_gnn_Wm1': 7.422,
     'L1_gnn_Wm2': 5.83,
     'L2_gnn_b': 64.0,
     'L3_gnn_W0': 4.653,
     'L3_gnn_W1': 3.896,
     'L3_gnn_W2': 2.676}
    for name, (base, spread) in spreads.items():
        noise = np.random.default_rng([zlib.crc32(name.encode()), seed]).standard_normal(out[name].shape)
        drawn = base * np.exp(spread * noise) if base else spread * noise
        out[name] = jnp.asarray(drawn.astype(out[name].dtype))
    for name, factor in factors.items():
        out[name] = (out[name] * factor).astype(out[name].dtype)
    return out
```

```python
from contextlib import ExitStack

import concourse.bass as bass
from concourse import mybir

F32 = mybir.dt.float32
F16 = mybir.dt.float16
I32 = mybir.dt.int32
ALU = mybir.AluOpType
ACT = mybir.ActivationFunctionType

P = 128
D = 96
DA = 32
N = 100000
E = 50000
G = 4
GE = G * P
EG = 98
ET = EG * G
E_PAD = EG * GE
NG = (N + GE - 1) // GE
SL = 4
HI, LO = 98, 1024
LB = EG
FAR = float(1 << 20)
EPS = 1e-5
NO_NODE, NO_EDGE = -1, -2
assert HI * LO >= N and E_PAD >= E


class Count:

    def __init__(self, sem, base=0):
        self.sem, self.base = sem, base


def need(eng, count, value):
    sem, base = (count.sem, count.base) if isinstance(count, Count) else (count, 0)
    if not isinstance(value, int) or value > 0:
        eng.wait_ge(sem, value + base)


def uses(n, s):
    return (n - s + SL - 1) // SL


def landed(j, s, dmas=1):
    return dmas * ((16 // SL) * (j - s) + 16)


def ended(n, s, dmas=1):
    return 16 * dmas * uses(n, s)


def pipelined(eng, n, stages):
    most = max(lag for _, lag in stages)
    first = (most + 2 * SL - 1) // SL * SL
    steady = (n - 1 - first) // SL * SL

    def step(i, s):
        for stage, lag in stages:
            if not isinstance(i, int) or 0 <= i - lag < n:
                stage(i - lag, (s - lag) % SL)

    for i in range(first):
        step(i, i % SL)
    with eng.Fori(0, steady // SL) as turn:
        for s in range(SL):
            step(turn * SL + (first + s), s)
    for i in range(first + steady, n + most):
        step(i, i % SL)


def build(nc, a, out):
    with ExitStack() as ctx:
        def sb(name, shape, dt=F32):
            return ctx.enter_context(nc.sbuf_tensor(name, shape, dt))

        def sem(name):
            return ctx.enter_context(nc.semaphore(name))

        def sems(name, n):
            return [sem(f"{name}{i}") for i in range(n)]

        def dram(name, shape, dt=F32):
            return nc.dram_tensor(name, shape, dt, kind="Internal").ap()

        srcp = dram("srcp", (E_PAD,), I32)
        dstp = dram("dstp", (E_PAD + 2,), I32)
        info_d = dram("info_d", (HI * LO, 2))
        t1 = dram("t1", (E_PAD + N, D))
        t2 = dram("t2", (E_PAD + N + E_PAD, D))
        c1 = dram("c1", (E_PAD + 1, D))
        c2 = dram("c2", (E_PAD + 1, D))

        ident = sb("ident", [P, P])
        before = sb("before", [HI, HI])
        iota_lo = sb("iota_lo", [P, LO])
        iota_hi_i = sb("iota_hi_i", [P, P], I32)
        iota_hi = sb("iota_hi", [P, P])
        home_i = sb("home_i", [HI, LO], I32)
        mw1 = sb("mw1", [D + DA, D])
        gw1 = sb("gw1", [D + DA, D])
        mw2 = sb("mw2", [D + 1, D])
        gw2 = sb("gw2", [D + 1, 1])
        uw1 = sb("uw1", [D, 2, D])
        uw2 = sb("uw2", [D + 1, D])
        wm1 = sb("wm1", [D, 2, D])
        wm2 = sb("wm2", [D + 1, D])
        wu1 = sb("wu1", [D, 2, D])
        wu2 = sb("wu2", [D + 1, D])
        w2 = sb("w2", [D + 1, D + 1])
        w3 = sb("w3", [D, 3, D])
        bias = sb("bias", [D, 5])
        rows = sb("rows", [P, 5, D])
        relu_b2 = sb("relu_b2", [P, D])

        st_s = sb("st_s", [P, ET], I32)
        st_d = sb("st_d", [P, ET], I32)
        edge_pad = sb("edge_pad", [1, 2], I32)
        blk_i = sb("blk_i", [LB, 3, 4, P], I32)
        cols = sb("cols", [P, 3, ET])
        src_at = sb("src_at", [P, ET])
        dst_at = sb("dst_at", [P, ET])
        out_at = sb("out_at", [P, ET])
        is_last = sb("is_last", [P, ET])
        in_tab = sb("in_tab", [P, ET])
        lo_of = sb("lo_of", [P, 2, ET])
        hi_of = sb("hi_of", [P, 2, ET])
        row_src = sb("row_src", [P, ET])
        row_dst = sb("row_dst", [P, ET])
        row_src3 = sb("row_src3", [P, ET])
        row_srcc = sb("row_srcc", [P, ET])
        ns = sb("ns", [P, ET])
        nd = sb("nd", [P, ET])
        hot_hi = sb("hot_hi", [P, 2, 2, P], F16)
        hot_lo = sb("hot_lo", [P, 2, 2, LO], F16)
        degi = sb("degi", [HI, LO])
        deg = sb("deg", [P, ET])
        cum = sb("cum", [HI, LO])
        home = sb("home", [HI, LO])
        has = sb("has", [HI, LO])
        off = sb("off", [HI, 1])
        info = sb("info", [HI, LO, 2])

        idx = sb("idx", [P, SL, 2, G], I32)
        got = sb("got", [P, SL, 2, G, 2])
        xs = sb("xs", [P, SL, G, D])
        xd = sb("xd", [P, SL, G, D])
        hs = sb("hs", [P, SL, G, P])
        hd = sb("hd", [P, SL, G, D])
        stats = sb("stats", [P, 3, G, 6])
        mv = sb("mv", [P, SL, 3, G, 2])
        var = sb("var", [P, SL, 3, G])
        rstd = sb("rstd", [P, SL, 3, G])
        neg_half = sb("neg_half", [P, 1])
        hsT = sb("hsT", [P, 2, GE])
        hdT = sb("hdT", [D, 2, GE])
        m1 = sb("m1", [D + 1, 2, GE])
        g1 = sb("g1", [D + 1, 2, GE])
        u1 = sb("u1", [D + 1, 2, GE])
        v1 = sb("v1", [D + 1, 2, GE])
        gate = sb("gate", [P, SL, 2, G])
        msg = sb("msg", [P, 2, G, D + 1])
        same = sb("same", [P, 2, G, P])
        iota_lo_i = same[:, 0:2, :, :].rearrange("p s c e -> p (s c e)").bitcast(I32)
        goes_on = sb("goes_on", [P, 2, G, P])
        dst_row = sb("dst_row", [P, SL, GE + 1], I32)
        drop = sb("drop", [P, SL, G, D])
        aggT = sb("aggT", [D + 1, SL, GE])
        y = sb("y", [P, SL, G, D])
        blk = y[0:LB, :, :, :].rearrange("p s c d -> p (s c d)").rearrange("p (k b e) -> p k b e", k=3, b=4)
        yg = sb("yg", [P, SL, G, D])
        xb = sb("xb", [P, SL, G, D])
        dego = xb[0:HI, :, :, :].rearrange("p s c d -> p (s c d)")[:, 0:LO]
        xn = sb("xn", [P, SL, G, D])
        xo = sb("xo", [P, SL, G, D])

        bank = [ctx.enter_context(nc.psum_tensor(f"bank{i}", [P, 512], F32)) for i in range(8)]

        ns_now = gate[:, :, 0, :]
        nd_now = gate[:, :, 1, :]

        def tok(b, w=D):
            return b[:, 0:G * w].rearrange("p (a c) -> p a c", c=w)

        weights_in = sem("weights_in")
        consts = sem("consts")
        const_step = sem("const_step")
        pad_set = sem("pad_set")
        staged = sem("staged")
        scratch_out = sem("scratch_out")
        blocks_in = sem("blocks_in")
        blk_f = sem("blk_f")
        blk_t = sem("blk_t")
        col_step = sem("col_step")
        hot = sem("hot")
        counted = sem("counted")
        table_step = sem("table_step")
        offs = sem("offs")
        info_out = sem("info_out")
        pool_turn = sem("pool_turn")
        sp_turn = sem("sp_turn")
        nd_made = sem("nd_made")
        ns_made = sem("ns_made")
        dve_turn = sem("dve_turn")
        rows_ready = sem("rows_ready")
        idx_step = sem("idx_step")
        n_weights = [0]

        def Phase(tag, n, counts, slots, after=None):
            made = {}
            for name in counts:
                made[name] = Count(sem(f"{tag}_{name}")) if after is None else \
                    Count(after[name].sem, after[name].base + after["n"] * after["counts"][name])
            for name in slots:
                made[name] = []
                for s in range(SL):
                    if after is None:
                        made[name].append(Count(sem(f"{tag}_{name}{s}")))
                        continue
                    extra = 16 if name == "attr" and s == (EG - 1) % SL else 0
                    last = after[name][s]
                    made[name].append(Count(last.sem, last.base + 16 * after["slots"][name] * uses(after["n"], s) + extra))
            return dict(made, n=n, counts=counts, slots=slots)

        info_p = Phase("info", EG, dict(idx=1, kept=1), dict(got=2 * G))
        dn = Phase("dense", NG, dict(root_a=1, root_y=1, root_x=1, norm=4, t1=1, r1=1, z1=1, g1=1, u1=1, upd=10, t2=1, r2=1, z2=1, g2=1,
                                     u2=1, fin=2), dict(x_in=1, x1_out=1, x2_out=1, o_out=1))
        e0 = Phase("edge", EG, dict(idx=1, root_a=1, root_y=1, norm=4, same=2, tr=1, trr=1, hid=1, act=1, tok=1, msg=3, seg=1, agg=G,
                                    z=1, g=1, u=1, upd=6), dict(xs=G, xd=G, attr=1, dst=1, x_out=1))
        e1 = Phase("edge", EG, dict(e0["counts"], msg=1, upd=1, root_y=0), e0["slots"], after=e0)
        conv = []
        for k in range(4):
            conv.append(Phase(
                "conv", EG, dict(idx=1, root_a=1 if k < 2 else 0, norm=4 if k < 2 else 0, same=2, h=1, seg=1, agg=G, u=1, upd=3),
                dict(xs=G, dst=1, res=1 if k in (0, 3) else 0, x_out=1 if k < 3 else 0,
                     scattered=G if k == 3 else 0),
                after=conv[k - 1] if k else None))

        xd_rows = a["x"]

        def node_start(j):
            return min(j * GE, N - GE) if isinstance(j, int) else j * GE

        def node_view(t, first):
            return t[bass.ds(first, GE), :].rearrange("(p c) d -> p c d", c=G)

        def edge_view(t, first):
            return t[bass.ds(first, GE), :].rearrange("(c p) d -> p c d", p=P)

        attr_dmas_last = 2

        def attr_landed(j, s):
            if isinstance(j, int) and j == EG - 1:
                return landed(j, s) + 16 * (attr_dmas_last - 1)
            return landed(j, s)

        block = ctx.enter_context(nc.Block())

        @block.sync
        def _(sp):
            def load(dst, src):
                sp.dma_start(dst, src).then_inc(weights_in, 16)
                n_weights[0] += 1

            sp.wait_ge(pad_set, 3)
            whole = E // ET
            for st, name in ((st_s, "src"), (st_d, "dst")):
                sp.dma_start(st[0:whole, :], a[name][0:whole * ET].rearrange("(p t) -> p t", t=ET)).then_inc(staged, 16)
                sp.dma_start(st[whole:whole + 1, 0:E - whole * ET],
                             a[name][whole * ET:E].rearrange("(p t) -> p t", p=1)).then_inc(staged, 16)
            sp.wait_ge(staged, 64)
            sp.dma_start(srcp.rearrange("(p t) -> p t", t=ET), st_s[:]).then_inc(scratch_out, 16)
            sp.dma_start(dstp[1:1 + E_PAD].rearrange("(p t) -> p t", t=ET), st_d[:]).then_inc(scratch_out, 16)
            sp.dma_start(dstp[0:1].rearrange("(p t) -> p t", p=1), edge_pad[:, 0:1]).then_inc(scratch_out, 16)
            sp.dma_start(dstp[E_PAD + 1:E_PAD + 2].rearrange("(p t) -> p t", p=1), edge_pad[:, 1:2]).then_inc(scratch_out, 16)
            sp.wait_ge(scratch_out, 64)
            for k, flat in enumerate((srcp, dstp[1:1 + E_PAD], dstp[2:2 + E_PAD])):
                sp.dma_start(blk_i[:, k, :, :], flat.rearrange("(b t p) -> t b p", t=LB, p=P)).then_inc(blocks_in, 16)

            load(mw1[:], a["L0_gnn_mW1"][:, :])
            load(gw1[:], a["L0_gnn_gW1"][:, :])
            for w, name, b in ((mw2, "L0_gnn_mW2", "L0_gnn_mb2"), (gw2, "L0_gnn_gW2", "L0_gnn_gb2"),
                               (uw2, "L0_gnn_uW2", "L0_gnn_ub2"), (wm2, "L1_gnn_Wm2", "L1_gnn_bm2"),
                               (wu2, "L1_gnn_Wu2", "L1_gnn_bu2")):
                load(w[0:D, :], a[name][:, :])
                load(w[D:D + 1, :], a[b].rearrange("(p c) -> p c", p=1))
            for w, name in ((uw1, "L0_gnn_uW1"), (wm1, "L1_gnn_Wm1"), (wu1, "L1_gnn_Wu1")):
                load(w[:], a[name].rearrange("(h p) c -> p h c", p=D))
            sp.wait_ge(const_step, 1)
            load(w2[0:D, 0:D], a["L2_gnn_W"][:, :])
            load(w2[D:D + 1, 0:D], a["L2_gnn_b"].rearrange("(p c) -> p c", p=1))
            for k in range(3):
                load(w3[:, k, :], a[f"L3_gnn_W{k}"][:, :])
            for k, name in enumerate(("L0_gnn_mb1", "L0_gnn_gb1", "L0_gnn_ub1", "L1_gnn_bm1", "L1_gnn_bu1")):
                load(bias[:, k:k + 1], a[name].rearrange("(p c) -> p c", c=1))
            for k, name in enumerate(("L0_gnn_ln_g", "L0_gnn_ln_b", "L3_gnn_b0", "L3_gnn_b1", "L3_gnn_b2")):
                load(rows[:, k, :], a[name].partition_broadcast(P))
            sp.wait_ge(weights_in, 16 * n_weights[0])
            for c, k in ((c1, 2), (c2, 3)):
                sp.dma_start(c[E_PAD:E_PAD + 1, :], rows[0:1, k, :]).then_inc(rows_ready, 16)

            sp.wait_ge(table_step, 7)
            sp.wait_ge(ns_made, 1)
            sp.dma_start(info_d.rearrange("(h l) c -> h (l c)", l=LO), info[:].rearrange("h l c -> h (l c)"))\
                .then_inc(info_out, 16)

            def dense_load(j, s):
                need(sp, dn["upd"], 10 * (j - SL + 1))
                sp.sem_inc(sp_turn, 1)
                sp.dma_start(xd[:, s, :, :], node_view(xd_rows, node_start(j))).then_inc(dn["x_in"][s].sem, 16)

            def dense_store_x1(j, s):
                need(sp, dn["upd"], 10 * (j + 1))
                if isinstance(j, int) and j == NG - 1:
                    need(sp, dn["x1_out"][(s - 1) % SL], landed(j - 1, (s - 1) % SL))
                sp.sem_inc(sp_turn, 1)
                sp.dma_start(node_view(t1, node_start(j) + E_PAD), xn[:, s, :, :]).then_inc(dn["x1_out"][s].sem, 16)

            def dense_store_x2(j, s):
                need(sp, dn["fin"], 2 * (j + 1))
                if isinstance(j, int) and j == NG - 1:
                    need(sp, dn["x2_out"][(s - 1) % SL], landed(j - 1, (s - 1) % SL))
                    need(sp, dn["o_out"][(s - 1) % SL], landed(j - 1, (s - 1) % SL))
                sp.sem_inc(sp_turn, 1)
                sp.dma_start(node_view(t2, node_start(j) + E_PAD), xo[:, s, :, :]).then_inc(dn["x2_out"][s].sem, 16)
                sp.sem_inc(sp_turn, 1)
                sp.dma_start(node_view(out, node_start(j)), yg[:, s, :, :]).then_inc(dn["o_out"][s].sem, 16)

            pipelined(sp, NG, [(dense_load, 0), (dense_store_x1, 3), (dense_store_x2, 5)])

            def edge_phase(ph, t, last):
                attr = a["edge_attr_32"] if ph is e0 else a["edge_attr_96"]
                width = DA if ph is e0 else D
                into = hs[:, :, :, D:D + DA] if ph is e0 else drop[:, :, :, :]

                def edge_load(j, s):
                    if ph is e0:
                        need(sp, ph["tr"], j - SL + 1)
                    else:
                        need(sp, ph["msg"], j - SL + 1)
                    if isinstance(j, int) and j == EG - 1:
                        full = (E - j * GE) // P
                        rest = E - j * GE - full * P
                        sp.sem_inc(sp_turn, 1)
                        sp.dma_start(into[:, s, 0:full, :], attr[j * GE:j * GE + full * P, :]
                                     .rearrange("(c p) d -> p c d", p=P)).then_inc(ph["attr"][s].sem, 16)
                        sp.dma_start(into[0:rest, s, full, :], attr[E - rest:E, :]).then_inc(ph["attr"][s].sem, 16)
                    else:
                        sp.sem_inc(sp_turn, 1)
                        sp.dma_start(into[:, s, :, :], edge_view(attr, j * GE)).then_inc(ph["attr"][s].sem, 16)
                    need(sp, ph["same"], 2 * (j - SL + 1))
                    sp.sem_inc(sp_turn, 1)
                    sp.dma_start(dst_row[:, s, :], dstp[bass.ds(j * GE, GE + 1)].partition_broadcast(P))\
                        .then_inc(ph["dst"][s].sem, 16)

                def edge_store(j, s):
                    need(sp, ph["upd"], last * (j + 1))
                    sp.sem_inc(sp_turn, 1)
                    sp.dma_start(edge_view(t, j * GE), xo[:, s, :, :]).then_inc(ph["x_out"][s].sem, 16)

                pipelined(sp, EG, [(edge_load, 0), (edge_store, 4)])

            for s in range(SL):
                need(sp, dn["x2_out"][s], ended(NG, s))
            edge_phase(e0, t1, 6)
            need(sp, e0["upd"], 6 * EG)
            edge_phase(e1, t2, 1)

            for k, ph in enumerate(conv):
                if k == 0:
                    for s in range(SL):
                        need(sp, e1["x_out"][s], ended(EG, s))
                if k == 3:
                    for s in range(SL):
                        need(sp, conv[0]["x_out"][s], ended(EG, s))

                def conv_load(j, s):
                    need(sp, ph["same"], 2 * (j - SL + 1))
                    sp.sem_inc(sp_turn, 1)
                    sp.dma_start(dst_row[:, s, :], dstp[bass.ds(j * GE, GE + 1)].partition_broadcast(P))\
                        .then_inc(ph["dst"][s].sem, 16)
                    if k in (0, 3):
                        need(sp, ph["upd"], 3 * (j - SL + 1))
                        first = j * GE + (E_PAD + N if k == 3 else 0)
                        sp.sem_inc(sp_turn, 1)
                        sp.dma_start(xd[:, s, :, :], edge_view(t2, first)).then_inc(ph["res"][s].sem, 16)

                def conv_store(j, s):
                    need(sp, ph["upd"], 3 * (j + 1))
                    t, first = ((t2, E_PAD + N), (c1, 0), (c2, 0))[k]
                    sp.sem_inc(sp_turn, 1)
                    sp.dma_start(edge_view(t, j * GE + first), xo[:, s, :, :]).then_inc(ph["x_out"][s].sem, 16)

                need(sp, e1["same"] if k == 0 else conv[k - 1]["same"], 2 * EG)
                pipelined(sp, EG, [(conv_load, 0)] + ([(conv_store, 3)] if k < 3 else []))
            for s in range(SL):
                need(sp, conv[1]["x_out"][s], ended(EG, s))
                need(sp, conv[2]["x_out"][s], ended(EG, s))
                need(sp, conv[3]["scattered"][s], ended(EG, s, G))
                need(sp, dn["o_out"][s], ended(NG, s))
            sp.wait_ge(rows_ready, 32)

        @block.gpsimd
        def _(pool):
            nc.gpsimd.memset(ident[:], 0.0).then_inc(consts, 1)
            nc.gpsimd.memset(before[:], 0.0).then_inc(consts, 1)
            pool.wait_ge(consts, 2)
            nc.gpsimd.affine_select(out=ident[:], in_=ident[:], compare_op=ALU.not_equal, fill=1.0, base=0,
                                    pattern=[[-1, P]], channel_multiplier=1).then_inc(consts, 1)
            nc.gpsimd.affine_select(out=before[:], in_=before[:], compare_op=ALU.is_ge, fill=1.0, base=0,
                                    pattern=[[-1, HI]], channel_multiplier=1).then_inc(consts, 1)
            nc.gpsimd.iota(iota_lo_i[:], pattern=[[1, LO]], base=0, channel_multiplier=0).then_inc(consts, 1)
            nc.gpsimd.iota(iota_hi_i[:], pattern=[[1, P]], base=0, channel_multiplier=0).then_inc(consts, 1)
            nc.gpsimd.iota(home_i[:], pattern=[[1, LO]], base=E_PAD, channel_multiplier=LO).then_inc(consts, 1)

            def gather(into, table, s, which, c, done):
                nc.gpsimd.indirect_dma_start(
                    out=into, out_offset=None, in_=table,
                    in_offset=bass.IndirectOffsetOnAxis(ap=idx[:, s, which, c:c + 1], axis=0)).then_inc(done.sem, 16)

            def root(into, of, done):
                shape = list(of.shape)
                e = neg_half[0:shape[0], 0:1]
                if len(shape) == 3:
                    e = e.unsqueeze(2)
                nc.gpsimd.tensor_tensor(into, of, e.broadcast_to(shape), ALU.pow).then_inc(done, 1)

            pool.wait_ge(table_step, 1)
            pool.wait_ge(const_step, 1)
            root(info[:, :, 1], dego, ns_made)

            def root_of(count, step, per, at, q0, q1):
                def stage(j, s):
                    need(pool, step, per * j + at)
                    pool.sem_inc(pool_turn, 1)
                    root(rstd[:, s, q0:q1, :], var[:, s, q0:q1, :], count.sem)
                return stage

            pool.wait_ge(info_out, 16)

            def info_gather(j, s):
                need(pool, info_p["kept"], j - SL + 1)
                need(pool, info_p["idx"], j + 1)
                pool.sem_inc(pool_turn, 1)
                for which in range(2):
                    for c in range(G):
                        gather(got[:, s, which, c, :], info_d[:, :], s, which, c, info_p["got"][s])

            pipelined(pool, EG, [(info_gather, 0)])

            pipelined(pool, NG, [(root_of(dn["root_a"], dn["norm"], 4, 3, 0, 1), 0),
                                 (root_of(dn["root_y"], dn["upd"], 10, 4, 2, 3), 1),
                                 (root_of(dn["root_x"], dn["upd"], 10, 9, 1, 2), 1)])

            for ph, t in ((e0, a["x"]), (e1, t1)):
                if ph is e1:
                    for s in range(SL):
                        need(pool, dn["x1_out"][s], ended(NG, s))
                        need(pool, e0["x_out"][s], ended(EG, s))
                    need(pool, e0["upd"], 6 * EG)
                else:
                    need(pool, dn["upd"], 10 * NG)

                def edge_gather(j, s):
                    need(pool, ph["norm"], 4 * (j - SL + 1))
                    need(pool, ph["upd"], (6 if ph is e0 else 1) * (j - SL + 1))
                    need(pool, ph["idx"], j + 1)
                    pool.sem_inc(pool_turn, 1)
                    for c in range(G):
                        gather(xs[:, s, c, :], t[:, :], s, 0, c, ph["xs"][s])

                def edge_gather_dst(j, s):
                    for c in range(G):
                        gather(xd[:, s, c, :], t[:, :], s, 1, c, ph["xd"][s])

                pipelined(pool, EG, [(edge_gather, 0)]
                          + ([(root_of(ph["root_y"], ph["upd"], 6, 4, 2, 3), 3)] if ph is e0 else [])
                          + [(root_of(ph["root_a"], ph["norm"], 4, 3, 0, 2), 1), (edge_gather_dst, 0)])

            for k, ph in enumerate(conv):
                before_ph = e1 if k == 0 else conv[k - 1]
                for s in range(SL):
                    if k == 0:
                        need(pool, dn["x2_out"][s], ended(NG, s))
                    need(pool, before_ph["x_out"][s], ended(EG, s))
                if k == 1:
                    pool.wait_ge(rows_ready, 32)
                if k == 3:
                    for s in range(SL):
                        need(pool, dn["o_out"][s], ended(NG, s))
                t = (t2[0:E_PAD + N, :], t2, c1, c2)[k]

                def conv_gather(j, s):
                    need(pool, ph["h"], j - SL + 1)
                    need(pool, ph["idx"], j + 1)
                    pool.sem_inc(pool_turn, 1)
                    for c in range(G):
                        gather(xs[:, s, c, :], t[:, :], s, 0, c, ph["xs"][s])

                def scatter(j, s):
                    need(pool, ph["upd"], 3 * (j + 1))
                    pool.sem_inc(pool_turn, 1)
                    for c in range(G):
                        nc.gpsimd.indirect_dma_start(
                            out=out[:, :], out_offset=bass.IndirectOffsetOnAxis(ap=idx[:, s, 1, c:c + 1], axis=0),
                            in_=xo[:, s, c, :], in_offset=None, bounds_check=N - 1, oob_is_err=False)\
                            .then_inc(ph["scattered"][s].sem, 16)

                pipelined(pool, EG, [(conv_gather, 0)] + ([(root_of(ph["root_a"], ph["norm"], 4, 3, 0, 1), 1)] if k < 2 else [])
                          + ([(scatter, 3)] if k == 3 else []))
                if k == 0:
                    need(pool, ph["upd"], 3 * EG)
                    root(nd[:], deg[:], nd_made)

        @block.scalar
        def _(act):
            act.wait_ge(weights_in, 16 * n_weights[0])

            def relu1(j, s):
                need(act, dn["t1"], j + 1)
                need(act, dn["z1"], j - 1)
                nc.scalar.activation(hdT[:, s % 2, :], bank[0][0:D, :], ACT.Relu).then_inc(dn["r1"].sem, 1)

            def gelu1(j, s):
                need(act, dn["z1"], j + 1)
                need(act, dn["u1"], j - 1)
                nc.scalar.activation(u1[0:D, s % 2, :], bank[1][0:D, :], ACT.Gelu, bias=bias[:, 2:3])\
                    .then_inc(dn["g1"].sem, 1)

            def relu2(j, s):
                need(act, dn["t2"], j + 1)
                need(act, dn["z2"], j - 1)
                nc.scalar.activation(hsT[0:D, s % 2, :], bank[3][0:D, :], ACT.Relu).then_inc(dn["r2"].sem, 1)

            def relu3(j, s):
                need(act, dn["z2"], j + 1)
                need(act, dn["u2"], j - 1)
                nc.scalar.activation(v1[0:D, s % 2, :], bank[4][0:D, :], ACT.Relu, bias=bias[:, 4:5])\
                    .then_inc(dn["g2"].sem, 1)

            act.wait_ge(const_step, 1)
            pipelined(act, NG, [(relu1, 0), (relu2, 2), (gelu1, 0), (relu3, 2)])

            for ph in (e0, e1):
                first = ph is e0

                def trr(j, s):
                    need(act, ph["tr"], j + 1)
                    need(act, ph["hid"], j - 1)
                    nc.scalar.activation(hsT[0:D, s % 2, :], bank[0][0:D, :], ACT.Relu)
                    if first:
                        nc.scalar.activation(hsT[D:P, s % 2, :], bank[0][D:P, :], ACT.Copy)
                    need(act, ph["z"], j - 1)
                    nc.scalar.activation(hdT[:, s % 2, :], bank[1][0:D, :], ACT.Relu).then_inc(ph["trr"].sem, 1)

                def hidden(j, s):
                    need(act, ph["hid"], j + 1)
                    need(act, ph["tok"], j - 1)
                    if first:
                        nc.scalar.activation(m1[0:D, s % 2, :], bank[2][0:D, :], ACT.Gelu, bias=bias[:, 0:1])
                        nc.scalar.activation(g1[0:D, s % 2, :], bank[3][0:D, :], ACT.Gelu, bias=bias[:, 1:2])\
                            .then_inc(ph["act"].sem, 1)
                    else:
                        nc.scalar.activation(m1[0:D, s % 2, :], bank[2][0:D, :], ACT.Relu, bias=bias[:, 3:4])\
                            .then_inc(ph["act"].sem, 1)

                def message(j, s):
                    mg = tok(bank[4], D + 1)
                    need(act, ph["tok"], j + 1)
                    nc.scalar.activation(gate[:, s, 0, :], mg[:, :, D], ACT.Tanh, scale=0.5).then_inc(ph["msg"].sem, 1)
                    need(act, ph["msg"], 3 * j + 1)
                    nc.scalar.activation(gate[:, s, 1, :], gate[:, s, 0, :], ACT.Copy, scale=0.5, bias=0.5)\
                        .then_inc(ph["msg"].sem, 1)
                    need(act, ph["seg"], j - 1)
                    need(act, ph["msg"], 3 * j + 2)
                    for c in range(G):
                        ins = nc.scalar.activation(msg[:, s % 2, c, 0:D], mg[:, c, 0:D], ACT.Copy,
                                                   scale=gate[:, s, 1, c:c + 1])
                    ins.then_inc(ph["msg"].sem, 1)

                def update_act(j, s):
                    need(act, ph["z"], j + 1)
                    need(act, ph["u"], j - 1)
                    nc.scalar.activation(u1[0:D, s % 2, :], bank[6][0:D, :], ACT.Gelu if first else ACT.Relu,
                                         bias=bias[:, 2:3] if first else bias[:, 4:5]).then_inc(ph["g"].sem, 1)

                pipelined(act, EG, [(update_act, 2), (trr, 1), (hidden, 1)] + ([(message, 1)] if first else []))

            for k, ph in enumerate(conv):
                def rows_in(j, s):
                    if k in (0, 1):
                        need(act, ph["norm"], 4 * (j + 1))
                    else:
                        need(act, ph["xs"][s], landed(j, s, G))
                    need(act, ph["seg"], j - 1)
                    if k == 0:
                        ins = nc.scalar.activation(msg[:, s % 2, :, 0:D], hd[:, s, :, :], ACT.Relu)
                    else:
                        need(act, ph["norm"] if k == 1 else ph["xs"][s], 4 * (j + 1) if k == 1 else landed(j, s, G))
                        for c in range(G):
                            ins = nc.scalar.activation(
                                msg[:, s % 2, c, 0:D], hd[:, s, c, :] if k == 1 else xs[:, s, c, :], ACT.Relu,
                                scale=ns_now[:, s, c:c + 1])
                    ins.then_inc(ph["h"].sem, 1)

                pipelined(act, EG, [(rows_in, 1)])

        @block.tensor
        def _(pe):
            pe.wait_ge(weights_in, 16 * n_weights[0])
            pe.wait_ge(consts, 7)

            for k in range(3):
                pe.wait_ge(blk_f, k + 1)
                if k >= 1:
                    pe.wait_ge(col_step, k)
                for b in range(4):
                    ins = nc.tensor.transpose(bank[0][:, b * LB:(b + 1) * LB], blk[:, k, b, :], ident[0:LB, 0:LB])
                ins.then_inc(blk_t, 1)

            def count(j, s):
                need(pe, hot, 2 * (j + 1))
                for which in range(2):
                    for half in range(2):
                        ins = nc.tensor.matmul(
                            bank[1 + 2 * which + half][0:HI, :], hot_hi[:, (s % 2), which, 0:HI],
                            hot_lo[:, (s % 2), which, half * 512:half * 512 + 512],
                            start=isinstance(j, int) and j == 0, stop=isinstance(j, int) and j == ET - 1)
                ins.then_inc(counted, 1)

            pipelined(pe, ET, [(count, 0)])
            pe.wait_ge(table_step, 2)
            nc.tensor.matmul(bank[5][0:HI, 0:1], before[:], cum[:, LO - 1:LO], start=True, stop=True)\
                .then_inc(offs, 1)

            def products(into, w, x, done):
                nc.tensor.matmul(into, w, x, start=True, stop=True).then_inc(done.sem, 1)

            def tr1(j, s):
                need(pe, dn["norm"], 4 * (j + 1))
                need(pe, dn["r1"], j)
                for c in range(G):
                    ins = nc.tensor.transpose(bank[0][0:D, c * P:(c + 1) * P], hd[:, s, c, :], ident[:])
                ins.then_inc(dn["t1"].sem, 1)

            def z1(j, s):
                need(pe, dn["r1"], j + 1)
                need(pe, dn["g1"], j)
                products(bank[1][0:D, :], uw1[:, 0, :], hdT[:, s % 2, :], dn["z1"])

            def out1(j, s):
                need(pe, dn["g1"], j + 1)
                need(pe, dn["upd"], 10 * (j - 1) + 1)
                for c in range(G):
                    ins = nc.tensor.matmul(tok(bank[2])[:, c, :], u1[:, s % 2, c * P:(c + 1) * P], uw2[:],
                                           start=True, stop=True)
                ins.then_inc(dn["u1"].sem, 1)

            def tr2(j, s):
                need(pe, dn["upd"], 10 * (j + 1))
                need(pe, dn["r2"], j)
                for c in range(G):
                    ins = nc.tensor.transpose(bank[3][0:D, c * P:(c + 1) * P], hs[:, s, c, 0:D], ident[:])
                ins.then_inc(dn["t2"].sem, 1)

            def z2(j, s):
                need(pe, dn["r2"], j + 1)
                need(pe, dn["g2"], j)
                products(bank[4][0:D, :], wu1[:, 0, :], hsT[0:D, s % 2, :], dn["z2"])

            def out2(j, s):
                need(pe, dn["g2"], j + 1)
                need(pe, dn["fin"], 2 * (j - 1) + 1)
                for c in range(G):
                    ins = nc.tensor.matmul(tok(bank[5])[:, c, :], v1[:, s % 2, c * P:(c + 1) * P], wu2[:],
                                           start=True, stop=True)
                ins.then_inc(dn["u2"].sem, 1)

            pe.wait_ge(col_step, 3)
            pe.wait_ge(table_step, 7)
            pe.wait_ge(const_step, 1)
            pipelined(pe, NG, [(tr1, 0), (tr2, 2), (z1, 0), (z2, 2), (out1, 0), (out2, 2)])

            need(pe, dn["fin"], 2 * NG)
            for ph in (e0, e1):
                first = ph is e0

                def tr(j, s):
                    need(pe, ph["norm"], 4 * (j + 1))
                    if first:
                        need(pe, ph["attr"][s], attr_landed(j, s))
                    need(pe, ph["trr"], j)
                    w = P if first else D
                    for c in range(G):
                        nc.tensor.transpose(bank[0][0:w, c * P:(c + 1) * P], hs[:, s, c, 0:w], ident[:])
                    for c in range(G):
                        ins = nc.tensor.transpose(bank[1][0:D, c * P:(c + 1) * P], hd[:, s, c, :], ident[:])
                    ins.then_inc(ph["tr"].sem, 1)

                def hid(j, s):
                    need(pe, ph["trr"], j + 1)
                    need(pe, ph["act"], j)
                    if first:
                        nc.tensor.matmul(bank[2][0:D, :], mw1[:], hsT[:, s % 2, :], start=True, stop=True)
                        products(bank[3][0:D, :], gw1[:], hsT[:, s % 2, :], ph["hid"])
                    else:
                        nc.tensor.matmul(bank[2][0:D, :], wm1[:, 0, :], hsT[0:D, s % 2, :], start=True, stop=False)
                        nc.tensor.matmul(bank[2][0:D, :], wm1[:, 1, :], hdT[:, s % 2, :], start=False, stop=True)\
                            .then_inc(ph["hid"].sem, 1)

                def tokens(j, s):
                    need(pe, ph["act"], j + 1)
                    need(pe, ph["msg"], 3 * j if first else j)
                    mg = tok(bank[4], D + 1)
                    for c in range(G):
                        ins = nc.tensor.matmul(mg[:, c, 0:D], m1[:, s % 2, c * P:(c + 1) * P],
                                               (mw2 if first else wm2)[:], start=True, stop=True)
                        if first:
                            ins = nc.tensor.matmul(mg[:, c, D:D + 1], g1[:, s % 2, c * P:(c + 1) * P], gw2[:],
                                                   start=True, stop=True)
                    ins.then_inc(ph["tok"].sem, 1)

                def seg(j, s):
                    need(pe, ph["msg"], 3 * (j + 1) if first else j + 1)
                    need(pe, ph["same"], 2 * (j + 1))
                    need(pe, ph["agg"], G * j)
                    for c in range(G):
                        ins = nc.tensor.matmul(bank[5][0:D, c * P:(c + 1) * P], msg[:, s % 2, c, 0:D],
                                               same[:, s % 2, c, :], start=True, stop=True)
                    ins.then_inc(ph["seg"].sem, 1)

                def upd_z(j, s):
                    w = uw1 if first else wu1
                    need(pe, ph["agg"], G * (j + 1))
                    need(pe, ph["g"], j)
                    nc.tensor.matmul(bank[6][0:D, :], w[:, 0, :], hdT[:, s % 2, :], start=True, stop=False)
                    nc.tensor.matmul(bank[6][0:D, :], w[:, 1, :], aggT[0:D, s, :], start=False, stop=True)\
                        .then_inc(ph["z"].sem, 1)

                def upd_u(j, s):
                    need(pe, ph["g"], j + 1)
                    need(pe, ph["upd"], 6 * (j - 1) + 1 if first else j)
                    for c in range(G):
                        ins = nc.tensor.matmul(tok(bank[7])[:, c, :], u1[:, s % 2, c * P:(c + 1) * P],
                                               (uw2 if first else wu2)[:], start=True, stop=True)
                    ins.then_inc(ph["u"].sem, 1)

                pipelined(pe, EG, [(upd_z, 2), (tr, 1), (upd_u, 2), (hid, 1), (tokens, 1), (seg, 1)])
                need(pe, ph["upd"], (6 if first else 1) * EG)

            for k, ph in enumerate(conv):
                m = D + 1 if k == 0 else D

                def seg(j, s):
                    need(pe, ph["h"], j + 1)
                    need(pe, ph["same"], 2 * (j + 1))
                    need(pe, ph["agg"], G * (j - 1))
                    for c in range(G):
                        ins = nc.tensor.matmul(bank[s % 2][0:m, c * P:(c + 1) * P], msg[:, s % 2, c, 0:m],
                                               same[:, s % 2, c, :], start=True, stop=True)
                    ins.then_inc(ph["seg"].sem, 1)

                def apply_w(j, s):
                    need(pe, ph["agg"], G * (j + 1))
                    need(pe, ph["upd"], 3 * (j - 1))
                    for c in range(G):
                        ins = nc.tensor.matmul(tok(bank[2 + s % 2], m)[:, c, :], aggT[0:m, s, c * P:(c + 1) * P],
                                               w2[:] if k == 0 else w3[:, k - 1, :], start=True, stop=True)
                    ins.then_inc(ph["u"].sem, 1)

                pipelined(pe, EG, [(apply_w, 2), (seg, 1)])
                need(pe, ph["upd"], 3 * EG)

        @block.vector
        def _(dve):
            nc.vector.memset(st_s[:], NO_NODE).then_inc(pad_set, 1)
            nc.vector.memset(st_d[:], NO_NODE).then_inc(pad_set, 1)
            nc.vector.memset(edge_pad[:], NO_EDGE).then_inc(pad_set, 1)
            nc.vector.memset(neg_half[:], -0.5)
            nc.vector.memset(w2[D:D + 1, :], 1.0)
            nc.vector.memset(w2[0:D, D:D + 1], 0.0)
            for b in (m1, g1, u1, v1):
                nc.vector.memset(b[D:D + 1, :, :], 1.0)
            nc.vector.memset(hs[:, :, :, D:P], 0.0)
            nc.vector.memset(drop[:], 0.0)
            nc.vector.memset(msg[:, :, :, D:D + 1], 1.0)
            nc.vector.memset(aggT[:, SL - 1, :], 0.0).then_inc(const_step, 1)

            dve.wait_ge(blocks_in, 48)
            for k in range(3):
                nc.vector.tensor_copy(blk[:, k, :, :], blk_i[:, k, :, :]).then_inc(blk_f, 1)
            dve.wait_ge(consts, 7)
            nc.vector.tensor_copy(iota_lo[:], iota_lo_i[:])
            nc.vector.tensor_copy(iota_hi[:], iota_hi_i[:])
            nc.vector.tensor_copy(home[:], home_i[:])
            for k in range(3):
                dve.wait_ge(blk_t, k + 1)
                nc.vector.tensor_copy(cols[:, k, :], bank[0][:, 0:ET]).then_inc(col_step, 1)
            dve.wait_ge(col_step, 3)
            nc.vector.tensor_scalar(src_at[:], cols[:, 0, :], 0.0, None, ALU.max)
            nc.vector.tensor_scalar(dst_at[:], cols[:, 1, :], 0.0, None, ALU.max)
            nc.vector.tensor_copy(st_s[:], cols[:, 0, :])
            nc.vector.tensor_copy(st_d[:], cols[:, 1, :])
            nc.vector.tensor_tensor(is_last[:], cols[:, 1, :], cols[:, 2, :], ALU.not_equal)
            nc.vector.tensor_scalar(out_at[:], cols[:, 1, :], -FAR, None, ALU.add)
            nc.vector.tensor_scalar(in_tab[:], cols[:, 1, :], 0.0, None, ALU.is_ge).then_inc(col_step, 1)
            dve.wait_ge(col_step, 4)
            for st, lo, hi in ((st_s, row_src, row_src3), (st_d, row_dst, row_srcc)):
                nc.vector.tensor_single_scalar(lo[:].bitcast(I32), st[:], LO - 1, ALU.bitwise_and)
                nc.vector.tensor_single_scalar(hi[:].bitcast(I32), st[:], LO.bit_length() - 1, ALU.arith_shift_right)
            nc.vector.tensor_tensor(is_last[:], is_last[:], in_tab[:], ALU.mult).then_inc(col_step, 1)
            dve.wait_ge(col_step, 5)
            for which, (lo, hi) in enumerate(((row_src, row_src3), (row_dst, row_srcc))):
                nc.vector.tensor_copy(lo_of[:, which, :], lo[:].bitcast(I32))
                nc.vector.tensor_copy(hi_of[:, which, :], hi[:].bitcast(I32))
            nc.vector.tensor_tensor(out_at[:], out_at[:], is_last[:], ALU.mult).then_inc(col_step, 1)
            dve.wait_ge(col_step, 6)
            nc.vector.tensor_scalar(out_at[:], out_at[:], FAR, None, ALU.add).then_inc(col_step, 1)
            dve.wait_ge(col_step, 7)

            def one_hot(j, s):
                need(dve, counted, j - 1)
                dve.sem_inc(dve_turn, 1)
                for which in range(2):
                    nc.vector.tensor_scalar(hot_hi[:, s % 2, which, :], iota_hi[:],
                                            hi_of[:, which, bass.ds(j, 1)], None, ALU.is_equal)
                    nc.vector.tensor_scalar(hot_lo[:, s % 2, which, :], iota_lo[:],
                                            lo_of[:, which, bass.ds(j, 1)], None, ALU.is_equal).then_inc(hot, 1)

            pipelined(dve, ET, [(one_hot, 0)])

            dve.wait_ge(counted, ET)
            for half in range(2):
                cut = slice(half * 512, half * 512 + 512)
                nc.vector.tensor_copy(degi[:, cut], bank[3 + half][0:HI, :])
                nc.vector.tensor_scalar(dego[:, cut], bank[1 + half][0:HI, :], 1.0, None, ALU.max)
            nc.vector.memset(has[:], 1.0).then_inc(table_step, 1)
            dve.wait_ge(table_step, 1)
            nc.vector.tensor_tensor_scan(cum[:], has[:], degi[:], 0.0, ALU.mult, ALU.add).then_inc(table_step, 1)
            dve.wait_ge(offs, 1)
            nc.vector.tensor_copy(off[:], bank[5][0:HI, 0:1])
            nc.vector.tensor_scalar(has[:], degi[:], 0.0, None, ALU.is_gt).then_inc(table_step, 1)
            dve.wait_ge(table_step, 3)
            nc.vector.tensor_scalar(cum[:], cum[:], off[:, 0:1], -1.0, ALU.add, ALU.add).then_inc(table_step, 1)
            dve.wait_ge(table_step, 4)
            nc.vector.tensor_tensor(cum[:], cum[:], home[:], ALU.subtract).then_inc(table_step, 1)
            dve.wait_ge(table_step, 5)
            nc.vector.tensor_tensor(cum[:], cum[:], has[:], ALU.mult).then_inc(table_step, 1)
            dve.wait_ge(table_step, 6)
            nc.vector.tensor_tensor(info[:, :, 0], cum[:], home[:], ALU.add).then_inc(table_step, 1)

            def info_idx(j, s):
                if not isinstance(j, int) or j >= SL:
                    need(dve, info_p["got"][s], landed(j - SL, s, 2 * G))
                    dve.sem_inc(dve_turn, 1)
                nc.vector.tensor_copy(idx[:, s, 0, :], src_at[:, bass.ds(j * G, G)])
                nc.vector.tensor_copy(idx[:, s, 1, :], dst_at[:, bass.ds(j * G, G)]).then_inc(info_p["idx"].sem, 1)

            def info_keep(j, s):
                need(dve, info_p["got"][s], landed(j, s, 2 * G))
                dve.sem_inc(dve_turn, 1)
                nc.vector.tensor_copy(row_src[:, bass.ds(j * G, G)], got[:, s, 0, :, 0])
                nc.vector.tensor_copy(ns[:, bass.ds(j * G, G)], got[:, s, 0, :, 1])
                nc.vector.tensor_copy(row_dst[:, bass.ds(j * G, G)], got[:, s, 1, :, 0]).then_inc(info_p["kept"].sem, 1)

            pipelined(dve, EG, [(info_idx, 0), (info_keep, 2)])
            need(dve, info_p["kept"], EG)
            nc.vector.tensor_scalar(row_srcc[:], row_src[:], float(E_PAD), None, ALU.min)
            nc.vector.tensor_scalar(in_tab[:], row_src[:], float(E_PAD), float(E_PAD + N), ALU.is_lt, ALU.mult)\
                .then_inc(idx_step, 1)
            dve.wait_ge(idx_step, 1)
            nc.vector.tensor_tensor(row_src3[:], row_src[:], in_tab[:], ALU.add).then_inc(idx_step, 1)
            dve.wait_ge(weights_in, 16 * n_weights[0])
            nc.vector.tensor_scalar(relu_b2[:], rows[:, 4, :], 0.0, None, ALU.max).then_inc(idx_step, 1)
            dve.wait_ge(idx_step, 3)

            def moments(xq, s, step, at):
                for q, x in xq.items():
                    for c in range(G):
                        ins = nc.vector.bn_stats(stats[:, q, c, :], x[:, c, :])
                ins.then_inc(step.sem, 1)
                need(dve, step, at + 1)
                dve.sem_inc(dve_turn, 1)
                for q in xq:
                    for c in range(G):
                        ins = nc.vector.bn_aggr(mv[:, s, q, c, :], stats[:, q, c, :])
                ins.then_inc(step.sem, 1)
                need(dve, step, at + 2)
                q0, q1 = min(xq), max(xq) + 1
                nc.vector.tensor_scalar(var[:, s, q0:q1, :], mv[:, s, q0:q1, :, 1], EPS, None, ALU.add)\
                    .then_inc(step.sem, 1)

            def normalise(into, x, q, s):
                for c in range(G):
                    ins = nc.vector.tensor_scalar(into[:, c, :], x[:, c, :], mv[:, s, q, c, 0:1],
                                                  rstd[:, s, q, c:c + 1], ALU.subtract, ALU.mult)
                return ins

            def wide(row):
                return row.unsqueeze(1).broadcast_to([P, G, D])

            def dense_moments(j, s):
                need(dve, dn["x_in"][s], landed(j, s))
                dve.sem_inc(dve_turn, 1)
                moments({0: xd[:, s, :, :]}, s, dn["norm"], 4 * j)

            def dense_norm(j, s):
                need(dve, dn["root_a"], j + 1)
                need(dve, dn["upd"], 10 * (j - SL + 1))
                dve.sem_inc(dve_turn, 1)
                normalise(hd[:, s, :, :], xd[:, s, :, :], 0, s).then_inc(dn["norm"].sem, 1)

            def update_y(ph, j, s, u_bank, per):
                nc.vector.scalar_tensor_tensor(out=y[:, s, :, :], in0=hd[:, s, :, :], scalar=0.0,
                                               in1=tok(u_bank), op0=ALU.max, op1=ALU.add).then_inc(ph["upd"].sem, 1)
                need(dve, ph["upd"], per * j + 1)
                moments({2: y[:, s, :, :]}, s, ph["upd"], per * j + 1)

            def update_x(ph, j, s, per, into):
                need(dve, ph["root_y"], j + 1)
                dve.sem_inc(dve_turn, 1)
                nc.vector.tensor_tensor(xb[:, s, :, :], xd[:, s, :, :], wide(rows[:, 1, :]), ALU.add)
                for c in range(G):
                    ins = nc.vector.scalar_tensor_tensor(out=yg[:, s, c, :], in0=y[:, s, c, :],
                                                         scalar=mv[:, s, 2, c, 0:1], in1=rows[:, 0, :],
                                                         op0=ALU.subtract, op1=ALU.mult)
                ins.then_inc(ph["upd"].sem, 1)
                need(dve, ph["upd"], per * j + 5)
                for c in range(G):
                    ins = nc.vector.scalar_tensor_tensor(out=into[:, s, c, :], in0=yg[:, s, c, :],
                                                         scalar=rstd[:, s, 2, c:c + 1], in1=xb[:, s, c, :],
                                                         op0=ALU.mult, op1=ALU.add)
                ins.then_inc(ph["upd"].sem, 1)

            def dense_y(j, s):
                need(dve, dn["u1"], j + 1)
                dve.sem_inc(dve_turn, 1)
                update_y(dn, j, s, bank[2], 10)

            def dense_x(j, s):
                if not isinstance(j, int) or j >= SL:
                    need(dve, dn["x1_out"][s], landed(j - SL, s))
                    need(dve, dn["o_out"][s], landed(j - SL, s))
                    dve.sem_inc(dve_turn, 1)
                update_x(dn, j, s, 10, xn)
                need(dve, dn["upd"], 10 * j + 6)
                moments({1: xn[:, s, :, :]}, s, dn["upd"], 10 * j + 6)

            def dense_norm2(j, s):
                need(dve, dn["root_x"], j + 1)
                need(dve, dn["t2"], j - SL + 1)
                dve.sem_inc(dve_turn, 1)
                normalise(hs[:, s, :, 0:D], xn[:, s, :, :], 1, s).then_inc(dn["upd"].sem, 1)

            def dense_finish(j, s):
                need(dve, dn["u2"], j + 1)
                need(dve, dn["upd"], 10 * (j + 1))
                if not isinstance(j, int) or j >= SL:
                    need(dve, dn["x2_out"][s], landed(j - SL, s))
                dve.sem_inc(dve_turn, 1)
                nc.vector.tensor_tensor(xo[:, s, :, :], xn[:, s, :, :], tok(bank[5]), ALU.add).then_inc(dn["fin"].sem, 1)
                need(dve, dn["fin"], 2 * j + 1)
                nc.vector.tensor_tensor(yg[:, s, :, :], xo[:, s, :, :], wide(relu_b2[:]), ALU.add).then_inc(dn["fin"].sem, 1)

            pipelined(dve, NG, [(dense_moments, 0), (dense_y, 1), (dense_norm, 0), (dense_x, 1), (dense_finish, 3),
                                (dense_norm2, 1)])
            need(dve, dn["fin"], 2 * NG)
            for s in range(SL):
                need(dve, dn["o_out"][s], ended(NG, s))

            def compare(ph, j, s):
                need(dve, ph["dst"][s], landed(j, s))
                need(dve, ph["seg"], j - 1)
                need(dve, ph["agg"], G * (j - 1))
                dve.sem_inc(dve_turn, 1)
                for c in range(G):
                    ins = nc.vector.tensor_scalar(same[:, s % 2, c, :], dst_row[:, s, 1 + c * P:1 + (c + 1) * P],
                                                  cols[:, 1, bass.ds(j * G + c, 1)], None, ALU.is_equal)
                ins.then_inc(ph["same"].sem, 1)
                nc.vector.tensor_tensor(
                    goes_on[:, s % 2, :, :], dst_row[:, s, 1:1 + GE].rearrange("p (c e) -> p c e", e=P),
                    dst_row[:, s, 0:GE].rearrange("p (c e) -> p c e", e=P)[:, :, 0:1].broadcast_to([P, G, P]),
                    ALU.is_equal).then_inc(ph["same"].sem, 1)

            def carry_on(ph, j, s, b, m, done):
                need(dve, ph["seg"], j + 1)
                need(dve, ph["same"], 2 * (j + 1))
                need(dve, done, j - SL + 1)
                need(dve, ph["agg"], G * j)
                dve.sem_inc(dve_turn, 1)
                for c in range(G):
                    carried = aggT[0:m, s, c * P - 1:c * P] if c else aggT[0:m, (s - 1) % SL, GE - 1:GE]
                    if c:
                        need(dve, ph["agg"], G * j + c)
                    nc.vector.scalar_tensor_tensor(
                        out=aggT[0:m, s, c * P:(c + 1) * P], in0=goes_on[0:m, s % 2, c, :], scalar=carried,
                        in1=b[0:m, c * P:(c + 1) * P], op0=ALU.mult, op1=ALU.add).then_inc(ph["agg"].sem, 1)

            for ph in (e0, e1):
                first = ph is e0

                def take_idx(j, s):
                    if not isinstance(j, int) or j >= SL:
                        need(dve, ph["xs"][s], landed(j - SL, s, G))
                        need(dve, ph["xd"][s], landed(j - SL, s, G))
                        dve.sem_inc(dve_turn, 1)
                    nc.vector.tensor_copy(idx[:, s, 0, :], (src_at if first else row_src)[:, bass.ds(j * G, G)])
                    nc.vector.tensor_copy(idx[:, s, 1, :], (dst_at if first else row_dst)[:, bass.ds(j * G, G)])\
                        .then_inc(ph["idx"].sem, 1)

                def edge_moments(j, s):
                    need(dve, ph["xs"][s], landed(j, s, G))
                    need(dve, ph["xd"][s], landed(j, s, G))
                    dve.sem_inc(dve_turn, 1)
                    moments({0: xs[:, s, :, :], 1: xd[:, s, :, :]}, s, ph["norm"], 4 * j)

                def norms(j, s):
                    need(dve, ph["root_a"], j + 1)
                    need(dve, ph["tr"], j - SL + 1)
                    dve.sem_inc(dve_turn, 1)
                    normalise(hs[:, s, :, 0:D], xs[:, s, :, :], 0, s)
                    normalise(hd[:, s, :, :], xd[:, s, :, :], 1, s).then_inc(ph["norm"].sem, 1)

                def match(j, s):
                    compare(ph, j, s)

                def times_drop(j, s):
                    need(dve, ph["tok"], j + 1)
                    need(dve, ph["attr"][s], attr_landed(j, s))
                    need(dve, ph["seg"], j - 1)
                    nc.vector.tensor_tensor(msg[:, s % 2, :, 0:D], tok(bank[4], D + 1)[:, :, 0:D],
                                            drop[:, s, :, :], ALU.mult).then_inc(ph["msg"].sem, 1)

                def sums(j, s):
                    carry_on(ph, j, s, bank[5], D, ph["z"])

                def new_y(j, s):
                    need(dve, ph["u"], j + 1)
                    dve.sem_inc(dve_turn, 1)
                    update_y(ph, j, s, bank[7], 6)

                def new_x(j, s):
                    if not isinstance(j, int) or j >= SL:
                        need(dve, ph["x_out"][s], landed(j - SL, s))
                        dve.sem_inc(dve_turn, 1)
                    if first:
                        update_x(ph, j, s, 6, xo)
                    else:
                        need(dve, ph["u"], j + 1)
                        nc.vector.tensor_tensor(xo[:, s, :, :], xd[:, s, :, :], tok(bank[7]), ALU.add)\
                            .then_inc(ph["upd"].sem, 1)

                if not first:
                    for s in range(SL):
                        need(dve, e0["x_out"][s], ended(EG, s))
                    nc.vector.memset(aggT[:, SL - 1, GE - 1:GE], 0.0).then_inc(idx_step, 1)
                    dve.wait_ge(idx_step, 4)
                pipelined(dve, EG, [(take_idx, 0), (sums, 2)] + ([(new_y, 3)] if first else [])
                          + [(edge_moments, 1), (match, 1), (new_x, 3), (norms, 1)]
                          + ([] if first else [(times_drop, 1)]))
                need(dve, ph["z"], EG)

            for k, ph in enumerate(conv):
                m = D + 1 if k == 0 else D
                where = (row_src, row_src3, row_srcc, row_srcc)[k]
                before_ph = e1 if k == 0 else conv[k - 1]
                for s in range(SL):
                    need(dve, before_ph["x_out"][s], ended(EG, s))
                nc.vector.memset(aggT[:, SL - 1, GE - 1:GE], 0.0).then_inc(idx_step, 1)
                dve.wait_ge(idx_step, 5 + k)

                def take_idx(j, s):
                    if not isinstance(j, int) or j >= SL:
                        need(dve, ph["xs"][s], landed(j - SL, s, G))
                        if k == 3:
                            need(dve, ph["scattered"][s], landed(j - SL, s, G))
                        else:
                            need(dve, ph["h"], j - SL + 1)
                        need(dve, ph["h"], j - SL + 1)
                        need(dve, ph["upd"], 3 * (j - SL + 1))
                        dve.sem_inc(dve_turn, 1)
                    if k == 3:
                        nc.vector.tensor_copy(idx[:, s, 1, :], out_at[:, bass.ds(j * G, G)])
                    if k:
                        nc.vector.tensor_copy(ns_now[:, s, :], ns[:, bass.ds(j * G, G)])
                        nc.vector.tensor_copy(nd_now[:, s, :], nd[:, bass.ds(j * G, G)])
                    nc.vector.tensor_copy(idx[:, s, 0, :], where[:, bass.ds(j * G, G)]).then_inc(ph["idx"].sem, 1)

                def row_moments(j, s):
                    need(dve, ph["xs"][s], landed(j, s, G))
                    dve.sem_inc(dve_turn, 1)
                    moments({0: xs[:, s, :, :]}, s, ph["norm"], 4 * j)

                def norms(j, s):
                    need(dve, ph["root_a"], j + 1)
                    need(dve, ph["h"], j - SL + 1)
                    dve.sem_inc(dve_turn, 1)
                    normalise(hd[:, s, :, :], xs[:, s, :, :], 0, s).then_inc(ph["norm"].sem, 1)

                def match(j, s):
                    compare(ph, j, s)

                def sums(j, s):
                    carry_on(ph, j, s, bank[s % 2], m, ph["u"])

                def finish(j, s):
                    u = tok(bank[2 + s % 2], m)
                    need(dve, ph["u"], j + 1)
                    if k in (0, 3):
                        need(dve, ph["res"][s], landed(j, s))
                    if not isinstance(j, int) or j >= SL:
                        need(dve, ph["scattered"][s] if k == 3 else ph["x_out"][s], landed(j - SL, s, G if k == 3 else 1))
                    dve.sem_inc(dve_turn, 1)
                    if k == 0:
                        nc.vector.reciprocal(rstd[:, s, 2, :], u[:, :, D])
                        nc.vector.tensor_copy(deg[:, bass.ds(j * G, G)], u[:, :, D])\
                            .then_inc(ph["upd"].sem, 1)
                        need(dve, ph["upd"], 3 * j + 1)
                        for c in range(G):
                            ins = nc.vector.scalar_tensor_tensor(
                                out=xo[:, s, c, :], in0=u[:, c, 0:D], scalar=rstd[:, s, 2, c:c + 1],
                                in1=xd[:, s, c, :], op0=ALU.mult, op1=ALU.add)
                        ins.then_inc(ph["upd"].sem, 2)
                        return
                    to = y if k == 3 else xo
                    for c in range(G):
                        ins = nc.vector.scalar_tensor_tensor(
                            out=to[:, s, c, :], in0=u[:, c, 0:D], scalar=nd_now[:, s, c:c + 1],
                            in1=rows[:, 1 + k, :], op0=ALU.mult, op1=ALU.add)
                    if k < 3:
                        ins.then_inc(ph["upd"].sem, 3)
                        return
                    ins.then_inc(ph["upd"].sem, 1)
                    need(dve, ph["upd"], 3 * j + 1)
                    nc.vector.scalar_tensor_tensor(out=xo[:, s, :, :], in0=y[:, s, :, :], scalar=0.0,
                                                   in1=xd[:, s, :, :], op0=ALU.max, op1=ALU.add)\
                        .then_inc(ph["upd"].sem, 2)

                pipelined(dve, EG, [(take_idx, 0)] + ([(row_moments, 1)] if k < 2 else [])
                          + [(sums, 2), (match, 1), (finish, 3)] + ([(norms, 1)] if k < 2 else []))
                if k == 0:
                    need(dve, ph["upd"], 3 * EG)
                    dve.wait_ge(nd_made, 1)


_INS = ['x', 'src', 'dst', 'edge_attr_32', 'edge_attr_96',
        'L0_gnn_mW1', 'L0_gnn_mb1', 'L0_gnn_mW2', 'L0_gnn_mb2', 'L0_gnn_gW1', 'L0_gnn_gb1', 'L0_gnn_gW2',
        'L0_gnn_gb2', 'L0_gnn_uW1', 'L0_gnn_ub1', 'L0_gnn_uW2', 'L0_gnn_ub2', 'L0_gnn_ln_g', 'L0_gnn_ln_b',
        'L1_gnn_Wm1', 'L1_gnn_bm1', 'L1_gnn_Wm2', 'L1_gnn_bm2', 'L1_gnn_Wu1', 'L1_gnn_bu1', 'L1_gnn_Wu2',
        'L1_gnn_bu2', 'L2_gnn_W', 'L2_gnn_b', 'L3_gnn_W0', 'L3_gnn_b0', 'L3_gnn_W1', 'L3_gnn_b1',
        'L3_gnn_W2', 'L3_gnn_b2']
_OUTS = [((100000, 96), 'float32')]


def kernel(**inputs):
    import numpy as _np
    import concourse.bacc as _bacc
    from concourse import mybir as _mybir
    from concourse.bass_utils import run_bass_kernel_spmd as _run

    nc = _bacc.Bacc("TRN2", target_bir_lowering=False, num_devices=1)
    arrays, aps = {}, {}
    for name in _INS:
        arr = _np.ascontiguousarray(inputs[name])
        arrays[f"in_{name}_dram"] = arr
        aps[name] = nc.dram_tensor(f"in_{name}_dram", arr.shape, _mybir.dt.from_np(arr.dtype), kind="ExternalInput").ap()
    out = nc.dram_tensor("out_0_dram", _OUTS[0][0], _mybir.dt.float32, kind="ExternalOutput").ap()
    build(nc, aps, out)
    r = _run(nc, [arrays], core_ids=[0])
    return r.results[0]["out_0_dram"]
```

```python
from contextlib import ExitStack

import concourse.bass as bass
from concourse import mybir

F32 = mybir.dt.float32
F16 = mybir.dt.float16
I32 = mybir.dt.int32
ALU = mybir.AluOpType
ACT = mybir.ActivationFunctionType

P = 128
D = 96
DA = 32
N = 100000
E = 50000
G = 4
GE = G * P
EG = 98
ET = EG * G
E_PAD = EG * GE
NG = (N + GE - 1) // GE
UNROLL = 6
GI = 2
HI, LO = 98, 1024
LB = EG
FAR = float(1 << 20)
EPS = 1e-5
GUESS = float(0x5F1FFFF9)
NEWTON = 2.38924456
SCALE = 0.703952253
CUBE = (-3 / 8 * SCALE ** 5, 10 / 8 * SCALE ** 3, -15 / 8 * SCALE)
ROOT = 12
NO_NODE, NO_EDGE = -1, -2
assert HI * LO >= N and E_PAD >= E


class Count:

    def __init__(self, sem, base=0):
        self.sem, self.base = sem, base


def need(eng, count, value):
    sem, base = (count.sem, count.base) if isinstance(count, Count) else (count, 0)
    if not isinstance(value, int) or value > 0:
        eng.wait_ge(sem, value + base)


class Group:

    def __init__(self, turn, c):
        self.turn, self.c = turn, c
        self.j = c if turn is None else turn * UNROLL + c

    def shift(self, by):
        return Group(self.turn, self.c + by)

    def at(self, slots):
        return self.c % slots

    def use(self, slots):
        return self.c // slots if self.turn is None else self.turn * (UNROLL // slots) + self.c // slots


def landed(g, slots, dmas=1):
    return 16 * dmas * (g.use(slots) + 1)


def freed(g, slots, dmas=1):
    return 16 * dmas * g.use(slots)


def ended(n, slots, s, dmas=1):
    return 16 * dmas * ((n - s + slots - 1) // slots)


def rounds(n, stages):
    return n + max(stage[1] for stage in stages)


def pipelined(eng, n, stages):
    most = max(stage[1] for stage in stages)
    last = max([n + most] + [stage[2] for stage in stages if len(stage) > 2])
    first = (most + 2 * UNROLL - 1) // UNROLL * UNROLL
    turns = (n - 1 - first) // UNROLL

    def step(g):
        for stage, lag, *always in stages:
            if g.turn is not None or (always and g.c < always[0]) or (not always and 0 <= g.c - lag < n):
                stage(g.shift(-lag))

    for i in range(first):
        step(Group(None, i))
    with eng.Fori(0, turns) as turn:
        for c in range(UNROLL):
            step(Group(turn, first + c))
    for i in range(first + turns * UNROLL, last):
        step(Group(None, i))


def build(nc, a, out):
    with ExitStack() as ctx:
        def sb(name, shape, dt=F32):
            return ctx.enter_context(nc.sbuf_tensor(name, shape, dt))

        def sem(name):
            return ctx.enter_context(nc.semaphore(name))

        def dram(name, shape, dt=F32):
            return nc.dram_tensor(name, shape, dt, kind="Internal").ap()

        srcp = dram("srcp", (E_PAD,), I32)
        dstp = dram("dstp", (E_PAD + 2,), I32)
        info_d = dram("info_d", (HI * LO, 2))
        t1 = dram("t1", (E_PAD + N, D))
        t2 = dram("t2", (E_PAD + N + E_PAD, D))
        c1 = dram("c1", (E_PAD + 1, D))
        c2 = dram("c2", (E_PAD + 1, D))

        ident = sb("ident", [P, P])
        before = sb("before", [HI, HI])
        iota_lo = sb("iota_lo", [P, LO], F16)
        iota_hi_i = sb("iota_hi_i", [P, P], I32)
        iota_hi = sb("iota_hi", [P, P], F16)
        home_i = sb("home_i", [HI, LO], I32)
        mw1 = sb("mw1", [D + DA, D])
        gw1 = sb("gw1", [D + DA, D])
        mw2 = sb("mw2", [D + 1, D])
        gw2 = sb("gw2", [D + 1, 1])
        uw1 = sb("uw1", [D, 2, D])
        uw2 = sb("uw2", [D + 1, D])
        wm1 = sb("wm1", [D, 2, D])
        wm2 = sb("wm2", [D + 1, D])
        wu1 = sb("wu1", [D, 2, D])
        wu2 = sb("wu2", [D + 1, D])
        w2 = sb("w2", [D + 1, D + 1])
        w3 = sb("w3", [D, 3, D])
        bias = sb("bias", [D, 5])
        rows = sb("rows", [P, 5, D])
        relu_b2 = sb("relu_b2", [P, D])

        st_s = sb("st_s", [P, ET], I32)
        st_d = sb("st_d", [P, ET], I32)
        edge_pad = sb("edge_pad", [1, 2], I32)
        blk_i = sb("blk_i", [LB, 3, 4, P], I32)
        cols = sb("cols", [P, 3, ET])
        src_at = sb("src_at", [P, ET])
        dst_at = sb("dst_at", [P, ET])
        out_at = sb("out_at", [P, ET])
        is_last = sb("is_last", [P, ET])
        in_tab = sb("in_tab", [P, ET])
        lo_of = sb("lo_of", [P, 2, ET])
        hi_of = sb("hi_of", [P, 2, ET])
        row_src = sb("row_src", [P, ET])
        row_dst = sb("row_dst", [P, ET])
        row_src3 = sb("row_src3", [P, ET])
        row_srcc = sb("row_srcc", [P, ET])
        ns = sb("ns", [P, ET])
        nd = sb("nd", [P, ET])
        hot_hi = sb("hot_hi", [P, 2, 2, P], F16)
        hot_lo = sb("hot_lo", [P, 2, 2, LO], F16)
        degi = sb("degi", [HI, LO])
        deg = sb("deg", [P, ET])
        cum = sb("cum", [HI, LO])
        home = sb("home", [HI, LO])
        has = sb("has", [HI, LO])
        off = sb("off", [HI, 1])
        info = sb("info", [HI, LO, 2])

        idx = sb("idx", [P, 6, 2, G], I32)
        idx_out = sb("idx_out", [P, 3, G], I32)
        got = sb("got", [P, 3, 2, GI, 2])
        xs = sb("xs", [P, 6, G, D])
        xd = sb("xd", [P, 6, G, D])
        hs = sb("hs", [P, 3, G, P])
        hd = sb("hd", [P, 6, G, D])
        stats = sb("stats", [P, 3, G, 6])
        mv = sb("mv", [P, 3, 3, G, 2])
        var = sb("var", [P, 3 * G])
        half = sb("half", [P, 3 * G], I32)
        guess = sb("guess", [P, 3 * G])
        sq = sb("sq", [P, 2, 3 * G])
        res = sb("res", [P, 2, 3 * G])
        root1 = sb("root1", [P, 3 * G])
        rstd = sb("rstd", [P, 3, 3, G])
        nmr = sb("nmr", [P, 3, 3, G])
        scaled = sb("scaled", [P, 3, 2, G])
        neg_half = sb("neg_half", [P, 1])
        hsT = sb("hsT", [P, 2, GE])
        hdT = sb("hdT", [D, 3, GE])
        m1 = sb("m1", [D + 1, 2, GE])
        g1 = sb("g1", [D + 1, 2, GE])
        u1 = sb("u1", [D + 1, 2, GE])
        v1 = g1
        gate = sb("gate", [P, 2, 2, G])
        now = sb("now", [P, 6, 2, G])
        msg = sb("msg", [P, 2, G, D + 1])
        same = sb("same", [P, 3, G, P])
        iota_lo_i = same[:, 0:2, :, :].rearrange("p s c e -> p (s c e)").bitcast(I32)
        goes_on = sb("goes_on", [P, 3, G, P])
        dst_row = sb("dst_row", [P, 3, GE + 1], I32)
        drop = sb("drop", [P, 3, G, D])
        aggT = sb("aggT", [D + 1, 3, GE])
        y = sb("y", [P, 2, G, D])
        yg = sb("yg", [P, 2, G, D])
        xb = sb("xb", [P, 3, G, D])
        dego = xb[0:HI, :, :, :].rearrange("p s c d -> p (s c d)")[:, 0:LO]
        xn = sb("xn", [P, 6, G, D])
        blk = xn[0:LB, 0:4, :, :].rearrange("p s c d -> p (s c d)").rearrange("p (k b e) -> p k b e", k=3, b=4)
        xo = sb("xo", [P, 3, G, D])
        oo = sb("oo", [P, 3, G, D])

        bank = [ctx.enter_context(nc.psum_tensor(f"bank{i}", [P, 512], F32)) for i in range(8)]

        def tok(b, w=D):
            return b[:, 0:G * w].rearrange("p (a c) -> p a c", c=w)

        weights_in = sem("weights_in")
        consts = sem("consts")
        const_step = sem("const_step")
        pad_set = sem("pad_set")
        staged = sem("staged")
        scratch_out = sem("scratch_out")
        blocks_in = sem("blocks_in")
        blk_f = sem("blk_f")
        blk_t = sem("blk_t")
        col_step = sem("col_step")
        hot = sem("hot")
        counted = sem("counted")
        table_step = sem("table_step")
        offs = sem("offs")
        info_out = sem("info_out")
        pool_turn = sem("pool_turn")
        sp_turn = sem("sp_turn")
        nd_made = sem("nd_made")
        ns_made = sem("ns_made")
        dve_turn = sem("dve_turn")
        rows_ready = sem("rows_ready")
        idx_step = sem("idx_step")
        n_weights = [0]

        def Phase(tag, n, counts, slots, own=(), after=None):
            made = {}
            for name in counts:
                made[name] = Count(sem(f"{tag}_{name}")) if after is None else \
                    Count(after[name].sem, after[name].base + after["n"] * after["counts"][name])
            for name, (many, dmas) in slots.items():
                made[name] = []
                for s in range(many):
                    if after is None:
                        made[name].append(Count(sem(f"{tag}_{name}{s}")))
                        continue
                    extra = 16 if name == "attr" and s == (EG - 1) % many else 0
                    last = after[name][s]
                    base = last.base + ended(after["n"], many, s, after["slots"][name][1]) + extra
                    made[name].append(Count(last.sem, base))
            for name in own:
                made[name] = Count(sem(f"{tag}_{name}"))
            return dict(made, n=n, counts=counts, slots=slots)

        dn = Phase("dense", NG, dict(norm=1, mom=2, t1=1, r1=1, z1=1, g1=1, u1=1, upd=7, t2=1, r2=1, z2=1, g2=1,
                                     u2=1, fin=1, norm2=1, xb=1, oo=1, idx=1, kept=1),
                   dict(x_in=(6, 1), x1_out=(6, 1), x2_out=(3, 1), o_out=(3, 1), got=(3, 2 * GI)), ["root"])
        e0 = Phase("edge", EG, dict(idx=1, mom=2, norm=1, same=2, tr=1, trr=1, hid=1, act=1, tok=1, msg=3, seg=1,
                                    agg=G, z=1, g=1, u=1, upd=5),
                   dict(xs=(6, G), xd=(6, G), attr=(3, 1), dst=(3, 1), x_out=(3, 1)), ["root0"])
        e1 = Phase("edge", EG, dict(e0["counts"], msg=1, upd=1), e0["slots"], ["root1"], after=e0)
        e0["root"], e1["root"] = e0["root0"], e1["root1"]
        conv = []
        for k in range(4):
            conv.append(Phase(
                "conv", EG, dict(idx=1, mom=2 if k < 2 else 0, scaled=1 if k == 1 else 0, same=2, h=1, seg=1,
                                 agg=G, u=1, upd=2),
                dict(xs=(6, G), dst=(3, 1), res=(6, 1 if k in (0, 3) else 0), x_out=(3, 1 if k < 3 else 0),
                     scattered=(3, G if k == 3 else 0)),
                [f"root{k}"], after=conv[k - 1] if k else None))
            conv[k]["root"] = conv[k][f"root{k}"]

        def node_start(j):
            return min(j * GE, N - GE) if isinstance(j, int) else j * GE

        def is_last_group(g, n):
            return g.turn is None and g.c == n - 1

        def node_view(t, first):
            return t[bass.ds(first, GE), :].rearrange("(p c) d -> p c d", c=G)

        def edge_view(t, first):
            return t[bass.ds(first, GE), :].rearrange("(c p) d -> p c d", p=P)

        attr_dmas_last = 2

        def attr_landed(g):
            both = 16 * (attr_dmas_last - 1) if g.turn is None and g.c == EG - 1 else 0
            return landed(g, 3) + both

        block = ctx.enter_context(nc.Block())

        @block.sync
        def _(sp):
            def load(dst, src):
                sp.dma_start(dst, src).then_inc(weights_in, 16)
                n_weights[0] += 1

            sp.wait_ge(pad_set, 3)
            whole = E // ET
            for st, name in ((st_s, "src"), (st_d, "dst")):
                sp.dma_start(st[0:whole, :], a[name][0:whole * ET].rearrange("(p t) -> p t", t=ET)).then_inc(staged, 16)
                sp.dma_start(st[whole:whole + 1, 0:E - whole * ET],
                             a[name][whole * ET:E].rearrange("(p t) -> p t", p=1)).then_inc(staged, 16)
            sp.wait_ge(staged, 64)
            sp.dma_start(srcp.rearrange("(p t) -> p t", t=ET), st_s[:]).then_inc(scratch_out, 16)
            sp.dma_start(dstp[1:1 + E_PAD].rearrange("(p t) -> p t", t=ET), st_d[:]).then_inc(scratch_out, 16)
            sp.dma_start(dstp[0:1].rearrange("(p t) -> p t", p=1), edge_pad[:, 0:1]).then_inc(scratch_out, 16)
            sp.dma_start(dstp[E_PAD + 1:E_PAD + 2].rearrange("(p t) -> p t", p=1), edge_pad[:, 1:2]).then_inc(scratch_out, 16)
            sp.wait_ge(scratch_out, 64)
            for k, flat in enumerate((srcp, dstp[1:1 + E_PAD], dstp[2:2 + E_PAD])):
                sp.dma_start(blk_i[:, k, :, :], flat.rearrange("(b t p) -> t b p", t=LB, p=P)).then_inc(blocks_in, 16)

            load(mw1[:], a["L0_gnn_mW1"][:, :])
            load(gw1[:], a["L0_gnn_gW1"][:, :])
            for w, name, b in ((mw2, "L0_gnn_mW2", "L0_gnn_mb2"), (gw2, "L0_gnn_gW2", "L0_gnn_gb2"),
                               (uw2, "L0_gnn_uW2", "L0_gnn_ub2"), (wm2, "L1_gnn_Wm2", "L1_gnn_bm2"),
                               (wu2, "L1_gnn_Wu2", "L1_gnn_bu2")):
                load(w[0:D, :], a[name][:, :])
                load(w[D:D + 1, :], a[b].rearrange("(p c) -> p c", p=1))
            for w, name in ((uw1, "L0_gnn_uW1"), (wm1, "L1_gnn_Wm1"), (wu1, "L1_gnn_Wu1")):
                load(w[:], a[name].rearrange("(h p) c -> p h c", p=D))
            sp.wait_ge(const_step, 1)
            load(w2[0:D, 0:D], a["L2_gnn_W"][:, :])
            load(w2[D:D + 1, 0:D], a["L2_gnn_b"].rearrange("(p c) -> p c", p=1))
            for k in range(3):
                load(w3[:, k, :], a[f"L3_gnn_W{k}"][:, :])
            for k, name in enumerate(("L0_gnn_mb1", "L0_gnn_gb1", "L0_gnn_ub1", "L1_gnn_bm1", "L1_gnn_bu1")):
                load(bias[:, k:k + 1], a[name].rearrange("(p c) -> p c", c=1))
            for k, name in enumerate(("L0_gnn_ln_g", "L0_gnn_ln_b", "L3_gnn_b0", "L3_gnn_b1", "L3_gnn_b2")):
                load(rows[:, k, :], a[name].partition_broadcast(P))
            sp.wait_ge(weights_in, 16 * n_weights[0])
            for c, k in ((c1, 2), (c2, 3)):
                sp.dma_start(c[E_PAD:E_PAD + 1, :], rows[0:1, k, :]).then_inc(rows_ready, 16)

            sp.wait_ge(table_step, 7)
            sp.wait_ge(ns_made, 1)
            sp.dma_start(info_d.rearrange("(h l) c -> h (l c)", l=LO), info[:].rearrange("h l c -> h (l c)"))\
                .then_inc(info_out, 16)

            def dense_load(g):
                need(sp, dn["upd"], 7 * (g.j - 5))
                sp.sem_inc(sp_turn, 1)
                need(sp, dn["xb"], g.j - 5)
                sp.sem_inc(sp_turn, 1)
                sp.dma_start(xd[:, g.at(6), :, :], node_view(a["x"], node_start(g.j))).then_inc(dn["x_in"][g.at(6)].sem, 16)

            def dense_store_x1(g):
                need(sp, dn["upd"], 7 * (g.j + 1))
                if is_last_group(g, NG):
                    before = g.shift(-1)
                    need(sp, dn["x1_out"][before.at(6)], landed(before, 6))
                sp.sem_inc(sp_turn, 1)
                sp.dma_start(node_view(t1, node_start(g.j) + E_PAD), xn[:, g.at(6), :, :])\
                    .then_inc(dn["x1_out"][g.at(6)].sem, 16)

            def dense_store_x2(g):
                need(sp, dn["fin"], g.j + 1)
                sp.sem_inc(sp_turn, 1)
                need(sp, dn["oo"], g.j + 1)
                if is_last_group(g, NG):
                    before = g.shift(-1)
                    need(sp, dn["x2_out"][before.at(3)], landed(before, 3))
                    need(sp, dn["o_out"][before.at(3)], landed(before, 3))
                sp.sem_inc(sp_turn, 1)
                sp.dma_start(node_view(t2, node_start(g.j) + E_PAD), xo[:, g.at(3), :, :])\
                    .then_inc(dn["x2_out"][g.at(3)].sem, 16)
                sp.dma_start(node_view(out, node_start(g.j)), oo[:, g.at(3), :, :]).then_inc(dn["o_out"][g.at(3)].sem, 16)

            pipelined(sp, NG, [(dense_load, 0), (dense_store_x1, 5), (dense_store_x2, 8)])

            def edge_phase(ph, t, last):
                attr = a["edge_attr_32"] if ph is e0 else a["edge_attr_96"]
                into = hs[:, :, :, D:D + DA] if ph is e0 else drop[:, :, :, :]

                def edge_load(g):
                    s = g.at(3)
                    if ph is e0:
                        need(sp, ph["tr"], g.j - 2)
                        sp.sem_inc(sp_turn, 1)
                    else:
                        need(sp, ph["msg"], g.j - 2)
                        sp.sem_inc(sp_turn, 1)
                    need(sp, ph["same"], 2 * (g.j - 2))
                    sp.sem_inc(sp_turn, 1)
                    first = g.j * GE
                    if is_last_group(g, EG):
                        full = (E - first) // P
                        rest = E - first - full * P
                        sp.dma_start(into[:, s, 0:full, :], attr[first:first + full * P, :]
                                     .rearrange("(c p) d -> p c d", p=P)).then_inc(ph["attr"][s].sem, 16)
                        sp.dma_start(into[0:rest, s, full, :], attr[E - rest:E, :]).then_inc(ph["attr"][s].sem, 16)
                    else:
                        sp.dma_start(into[:, s, :, :], edge_view(attr, first)).then_inc(ph["attr"][s].sem, 16)
                    sp.dma_start(dst_row[:, s, :], dstp[bass.ds(first, GE + 1)].partition_broadcast(P))\
                        .then_inc(ph["dst"][s].sem, 16)

                def edge_store(g):
                    need(sp, ph["upd"], last * (g.j + 1))
                    sp.sem_inc(sp_turn, 1)
                    sp.dma_start(edge_view(t, g.j * GE), xo[:, g.at(3), :, :]).then_inc(ph["x_out"][g.at(3)].sem, 16)

                pipelined(sp, EG, [(edge_load, 1), (edge_store, 7)])

            need(sp, dn["t2"], NG)
            edge_phase(e0, t1, 5)
            edge_phase(e1, t2, 1)

            for k, ph in enumerate(conv):
                if k in (0, 3):
                    source = e1 if k == 0 else conv[0]
                    for s in range(3):
                        need(sp, source["x_out"][s], ended(EG, 3, s))
                if k == 0:
                    need(sp, e1["upd"], EG)

                def conv_load(g):
                    need(sp, ph["same"], 2 * (g.j - 2))
                    if k in (0, 3):
                        sp.sem_inc(sp_turn, 1)
                        need(sp, ph["upd"], 2 * (g.j - 5))
                    sp.sem_inc(sp_turn, 1)
                    sp.dma_start(dst_row[:, g.at(3), :], dstp[bass.ds(g.j * GE, GE + 1)].partition_broadcast(P))\
                        .then_inc(ph["dst"][g.at(3)].sem, 16)
                    if k in (0, 3):
                        first = g.j * GE + (E_PAD + N if k == 3 else 0)
                        sp.dma_start(xd[:, g.at(6), :, :], edge_view(t2, first)).then_inc(ph["res"][g.at(6)].sem, 16)

                def conv_store(g):
                    need(sp, ph["upd"], 2 * (g.j + 1))
                    sp.sem_inc(sp_turn, 1)
                    t, first = ((t2, E_PAD + N), (c1, 0), (c2, 0))[k]
                    sp.dma_start(edge_view(t, g.j * GE + first), xo[:, g.at(3), :, :])\
                        .then_inc(ph["x_out"][g.at(3)].sem, 16)

                need(sp, e1["same"] if k == 0 else conv[k - 1]["same"], 2 * EG)
                pipelined(sp, EG, [(conv_load, 1)] + ([(conv_store, 6)] if k < 3 else []))
            for s in range(3):
                need(sp, conv[1]["x_out"][s], ended(EG, 3, s))
                need(sp, conv[2]["x_out"][s], ended(EG, 3, s))
                need(sp, conv[3]["scattered"][s], ended(EG, 3, s, G))
                need(sp, dn["o_out"][s], ended(NG, 3, s))
            sp.wait_ge(rows_ready, 32)

        @block.gpsimd
        def _(pool):
            nc.gpsimd.memset(ident[:], 0.0).then_inc(consts, 1)
            nc.gpsimd.memset(before[:], 0.0).then_inc(consts, 1)
            pool.wait_ge(consts, 2)
            nc.gpsimd.affine_select(out=ident[:], in_=ident[:], compare_op=ALU.not_equal, fill=1.0, base=0,
                                    pattern=[[-1, P]], channel_multiplier=1).then_inc(consts, 1)
            nc.gpsimd.affine_select(out=before[:], in_=before[:], compare_op=ALU.is_ge, fill=1.0, base=0,
                                    pattern=[[-1, HI]], channel_multiplier=1).then_inc(consts, 1)
            nc.gpsimd.iota(iota_lo_i[:], pattern=[[1, LO]], base=0, channel_multiplier=0).then_inc(consts, 1)
            nc.gpsimd.iota(iota_hi_i[:], pattern=[[1, P]], base=0, channel_multiplier=0).then_inc(consts, 1)
            nc.gpsimd.iota(home_i[:], pattern=[[1, LO]], base=E_PAD, channel_multiplier=LO).then_inc(consts, 1)

            def gather(into, table, indices, done):
                nc.gpsimd.indirect_dma_start(
                    out=into, out_offset=None, in_=table,
                    in_offset=bass.IndirectOffsetOnAxis(ap=indices, axis=0)).then_inc(done.sem, 16)

            def root(into, of, done):
                nc.gpsimd.tensor_tensor(into, of, neg_half[0:of.shape[0], 0:1].broadcast_to(list(of.shape)), ALU.pow)\
                    .then_inc(done, 1)

            pool.wait_ge(table_step, 1)
            pool.wait_ge(const_step, 1)
            root(info[:, :, 1], dego, ns_made)
            pool.wait_ge(info_out, 16)
            pool.wait_ge(weights_in, 16 * n_weights[0])
            pool.wait_ge(idx_step, 1)

            def info_gather(g):
                need(pool, dn["kept"], g.j - 2)
                need(pool, dn["idx"], g.j + 1)
                pool.sem_inc(pool_turn, 1)
                for which in range(2):
                    for c in range(GI):
                        gather(got[:, g.at(3), which, c, :], info_d[:, :], idx[:, g.at(6), which, c:c + 1],
                               dn["got"][g.at(3)])

            def wide(row):
                return row.unsqueeze(1).broadcast_to([P, G, D])

            def dense_xb(g):
                need(pool, dn["x_in"][g.at(6)], landed(g, 6))
                need(pool, dn["upd"], 7 * (g.j - 2))
                pool.sem_inc(pool_turn, 1)
                nc.gpsimd.tensor_tensor(xb[:, g.at(3), :, :], xd[:, g.at(6), :, :], wide(rows[:, 1, :]), ALU.add)\
                    .then_inc(dn["xb"].sem, 1)

            def dense_oo(g):
                need(pool, dn["fin"], g.j + 1)
                need(pool, dn["o_out"][g.at(3)], freed(g, 3))
                pool.sem_inc(pool_turn, 1)
                nc.gpsimd.tensor_tensor(oo[:, g.at(3), :, :], xo[:, g.at(3), :, :], wide(relu_b2[:]), ALU.add)\
                    .then_inc(dn["oo"].sem, 1)

            pipelined(pool, NG, [(dense_xb, 1), (info_gather, 0), (dense_oo, 6)])

            for ph, t in ((e0, a["x"]), (e1, t1)):
                if ph is e1:
                    for s in range(6):
                        need(pool, dn["x1_out"][s], ended(NG, 6, s))
                    for s in range(3):
                        need(pool, e0["x_out"][s], ended(EG, 3, s))
                else:
                    need(pool, dn["upd"], 7 * NG)

                def edge_gather(g):
                    need(pool, ph["norm"], g.j - 5)
                    need(pool, ph["upd"], (5 if ph is e0 else 1) * (g.j - 5))
                    need(pool, ph["idx"], g.j + 1)
                    pool.sem_inc(pool_turn, 1)
                    for c in range(G):
                        gather(xs[:, g.at(6), c, :], t[:, :], idx[:, g.at(6), 0, c:c + 1], ph["xs"][g.at(6)])
                    for c in range(G):
                        gather(xd[:, g.at(6), c, :], t[:, :], idx[:, g.at(6), 1, c:c + 1], ph["xd"][g.at(6)])

                pipelined(pool, EG, [(edge_gather, 0)])

            for k, ph in enumerate(conv):
                before_ph = e1 if k == 0 else conv[k - 1]
                for s in range(3):
                    if k == 0:
                        need(pool, dn["x2_out"][s], ended(NG, 3, s))
                    need(pool, before_ph["x_out"][s], ended(EG, 3, s))
                    if k == 3:
                        need(pool, dn["o_out"][s], ended(NG, 3, s))
                if k == 0:
                    need(pool, e1["norm"], EG)
                if k == 1:
                    pool.wait_ge(rows_ready, 32)
                t = (t2[0:E_PAD + N, :], t2, c1, c2)[k]

                def conv_gather(g):
                    need(pool, ph["h"], g.j - 5)
                    need(pool, ph["idx"], g.j + 1)
                    pool.sem_inc(pool_turn, 1)
                    for c in range(G):
                        gather(xs[:, g.at(6), c, :], t[:, :], idx[:, g.at(6), 0, c:c + 1], ph["xs"][g.at(6)])

                def scatter(g):
                    need(pool, ph["upd"], 2 * (g.j + 1))
                    pool.sem_inc(pool_turn, 1)
                    for c in range(G):
                        nc.gpsimd.indirect_dma_start(
                            out=out[:, :], out_offset=bass.IndirectOffsetOnAxis(ap=idx_out[:, g.at(3), c:c + 1], axis=0),
                            in_=xo[:, g.at(3), c, :], in_offset=None, bounds_check=N - 1, oob_is_err=False)\
                            .then_inc(ph["scattered"][g.at(3)].sem, 16)

                pipelined(pool, EG, [(conv_gather, 0)] + ([(scatter, 5)] if k == 3 else []))
                if k == 0:
                    need(pool, ph["upd"], 2 * EG)
                    root(nd[:], deg[:], nd_made)

        @block.scalar
        def _(act):
            act.wait_ge(weights_in, 16 * n_weights[0])

            def normed(into, x, b, q):
                for c in range(G):
                    ins = nc.scalar.activation(into[:, c, :], x[:, c, :], ACT.Relu, bias=nmr[:, b, q, c:c + 1],
                                               scale=rstd[:, b, q, c:c + 1])
                return ins

            def norm1(g):
                need(act, dn["root"], ROOT * (g.j + 1))
                need(act, dn["upd"], 7 * (g.j - 3) + 1)
                normed(hd[:, g.at(3), :, :], xd[:, g.at(6), :, :], g.at(3), 0).then_inc(dn["norm"].sem, 1)

            def norm2(g):
                need(act, dn["root"], ROOT * (g.j + 3 + 1))
                need(act, dn["t2"], g.j - 2)
                normed(hs[:, g.at(3), :, 0:D], xn[:, g.at(6), :, :], g.shift(3).at(3), 2).then_inc(dn["norm2"].sem, 1)

            def evac1(g):
                need(act, dn["t1"], g.j + 1)
                need(act, dn["z1"], g.j - 1)
                nc.scalar.activation(hdT[:, g.at(2), :], bank[0][0:D, :], ACT.Copy).then_inc(dn["r1"].sem, 1)

            def gelu1(g):
                need(act, dn["z1"], g.j + 1)
                need(act, dn["u1"], g.j - 1)
                nc.scalar.activation(u1[0:D, g.at(2), :], bank[1][0:D, :], ACT.Gelu, bias=bias[:, 2:3])\
                    .then_inc(dn["g1"].sem, 1)

            def evac2(g):
                need(act, dn["t2"], g.j + 1)
                need(act, dn["z2"], g.j - 1)
                nc.scalar.activation(hsT[0:D, g.at(2), :], bank[3][0:D, :], ACT.Copy).then_inc(dn["r2"].sem, 1)

            def relu2(g):
                need(act, dn["z2"], g.j + 1)
                need(act, dn["u2"], g.j - 1)
                nc.scalar.activation(v1[0:D, g.at(2), :], bank[4][0:D, :], ACT.Relu, bias=bias[:, 4:5])\
                    .then_inc(dn["g2"].sem, 1)

            act.wait_ge(const_step, 1)
            pipelined(act, NG, [(gelu1, 1), (relu2, 4), (norm1, 0), (norm2, 3), (evac1, 0), (evac2, 3)])

            for ph in (e0, e1):
                first = ph is e0

                def norms(g):
                    b = g.shift(2).at(3)
                    need(act, ph["root"], ROOT * (g.j + 2 + 1))
                    need(act, ph["tr"], g.j - 2)
                    normed(hs[:, g.at(3), :, 0:D], xs[:, g.at(6), :, :], b, 0)
                    if first:
                        need(act, ph["upd"], 5 * (g.j - 6) + 1)
                    normed(hd[:, g.at(6), :, :], xd[:, g.at(6), :, :], b, 1).then_inc(ph["norm"].sem, 1)

                def evac(g):
                    need(act, ph["tr"], g.j + 1)
                    need(act, ph["hid"], g.j - 1)
                    nc.scalar.activation(hsT[0:P if first else D, g.at(2), :], bank[0][0:P if first else D, :], ACT.Copy)
                    need(act, ph["z"], g.j - 2)
                    nc.scalar.activation(hdT[:, g.at(3), :], bank[1][0:D, :], ACT.Copy).then_inc(ph["trr"].sem, 1)

                def hidden(g):
                    need(act, ph["hid"], g.j + 1)
                    need(act, ph["tok"], g.j - 1)
                    if first:
                        nc.scalar.activation(m1[0:D, g.at(2), :], bank[2][0:D, :], ACT.Gelu, bias=bias[:, 0:1])
                        nc.scalar.activation(g1[0:D, g.at(2), :], bank[3][0:D, :], ACT.Gelu, bias=bias[:, 1:2])\
                            .then_inc(ph["act"].sem, 1)
                    else:
                        nc.scalar.activation(m1[0:D, g.at(2), :], bank[2][0:D, :], ACT.Relu, bias=bias[:, 3:4])\
                            .then_inc(ph["act"].sem, 1)

                def message(g):
                    mg = tok(bank[4], D + 1)
                    need(act, ph["tok"], g.j + 1)
                    nc.scalar.activation(gate[:, g.at(2), 0, :], mg[:, :, D], ACT.Tanh, scale=0.5)\
                        .then_inc(ph["msg"].sem, 1)
                    need(act, ph["msg"], 3 * g.j + 1)
                    nc.scalar.activation(gate[:, g.at(2), 1, :], gate[:, g.at(2), 0, :], ACT.Copy, scale=0.5, bias=0.5)\
                        .then_inc(ph["msg"].sem, 1)
                    need(act, ph["seg"], g.j - 1)
                    need(act, ph["msg"], 3 * g.j + 2)
                    for c in range(G):
                        ins = nc.scalar.activation(msg[:, g.at(2), c, 0:D], mg[:, c, 0:D], ACT.Copy,
                                                   scale=gate[:, g.at(2), 1, c:c + 1])
                    ins.then_inc(ph["msg"].sem, 1)

                def update_act(g):
                    need(act, ph["z"], g.j + 1)
                    need(act, ph["u"], g.j - 1)
                    nc.scalar.activation(u1[0:D, g.at(2), :], bank[6][0:D, :], ACT.Gelu if first else ACT.Relu,
                                         bias=bias[:, 2:3] if first else bias[:, 4:5]).then_inc(ph["g"].sem, 1)

                pipelined(act, EG, ([(message, 3)] if first else []) + [(update_act, 4), (norms, 2), (evac, 2), (hidden, 2)])

            for k, ph in enumerate(conv):
                def rows_in(g):
                    b = g.shift(2).at(3)
                    need(act, ph["seg"], g.j - 1)
                    if k == 0:
                        need(act, ph["root"], ROOT * (g.j + 2 + 1))
                        normed(msg[:, g.at(2), :, 0:D], xs[:, g.at(6), :, :], b, 0).then_inc(ph["h"].sem, 1)
                        return
                    if k == 1:
                        need(act, ph["scaled"], g.j + 1)
                    else:
                        need(act, ph["xs"][g.at(6)], landed(g, 6, G))
                    for c in range(G):
                        if k == 1:
                            ins = nc.scalar.activation(msg[:, g.at(2), c, 0:D], xs[:, g.at(6), c, :], ACT.Relu,
                                                       bias=scaled[:, b, 1, c:c + 1], scale=scaled[:, b, 0, c:c + 1])
                        else:
                            ins = nc.scalar.activation(msg[:, g.at(2), c, 0:D], xs[:, g.at(6), c, :], ACT.Relu,
                                                       scale=now[:, g.at(6), 0, c:c + 1])
                    ins.then_inc(ph["h"].sem, 1)

                if k >= 2:
                    need(act, ph["idx"], 1)
                pipelined(act, EG, [(rows_in, 2)])

        @block.tensor
        def _(pe):
            pe.wait_ge(weights_in, 16 * n_weights[0])
            pe.wait_ge(consts, 7)

            for k in range(3):
                pe.wait_ge(blk_f, k + 1)
                if k >= 1:
                    pe.wait_ge(col_step, k)
                for b in range(4):
                    ins = nc.tensor.transpose(bank[0][:, b * LB:(b + 1) * LB], blk[:, k, b, :], ident[0:LB, 0:LB])
                ins.then_inc(blk_t, 1)

            def count(g):
                need(pe, hot, 2 * (g.j + 1))
                for which in range(2):
                    for side in range(2):
                        ins = nc.tensor.matmul(
                            bank[1 + 2 * which + side][0:HI, :], hot_hi[:, g.at(2), which, 0:HI],
                            hot_lo[:, g.at(2), which, side * 512:side * 512 + 512],
                            start=g.turn is None and g.c == 0, stop=g.turn is None and g.c == ET - 1)
                ins.then_inc(counted, 1)

            pipelined(pe, ET, [(count, 0)])
            pe.wait_ge(table_step, 2)
            nc.tensor.matmul(bank[5][0:HI, 0:1], before[:], cum[:, LO - 1:LO], start=True, stop=True)\
                .then_inc(offs, 1)

            def products(into, w, x, done):
                nc.tensor.matmul(into, w, x, start=True, stop=True).then_inc(done.sem, 1)

            def tr1(g):
                need(pe, dn["norm"], g.j + 1)
                need(pe, dn["r1"], g.j)
                for c in range(G):
                    ins = nc.tensor.transpose(bank[0][0:D, c * P:(c + 1) * P], hd[:, g.at(3), c, :], ident[:])
                ins.then_inc(dn["t1"].sem, 1)

            def z1(g):
                need(pe, dn["r1"], g.j + 1)
                need(pe, dn["g1"], g.j)
                products(bank[1][0:D, :], uw1[:, 0, :], hdT[:, g.at(2), :], dn["z1"])

            def out1(g):
                need(pe, dn["g1"], g.j + 1)
                need(pe, dn["upd"], 7 * (g.j - 2) + 1)
                for c in range(G):
                    ins = nc.tensor.matmul(tok(bank[2 + 4 * g.at(2)])[:, c, :], u1[:, g.at(2), c * P:(c + 1) * P],
                                           uw2[:], start=True, stop=True)
                ins.then_inc(dn["u1"].sem, 1)

            def tr2(g):
                need(pe, dn["norm2"], g.j + 1)
                need(pe, dn["r2"], g.j)
                for c in range(G):
                    ins = nc.tensor.transpose(bank[3][0:D, c * P:(c + 1) * P], hs[:, g.at(3), c, 0:D], ident[:])
                ins.then_inc(dn["t2"].sem, 1)

            def z2(g):
                need(pe, dn["r2"], g.j + 1)
                need(pe, dn["g2"], g.j)
                products(bank[4][0:D, :], wu1[:, 0, :], hsT[0:D, g.at(2), :], dn["z2"])

            def out2(g):
                need(pe, dn["g2"], g.j + 1)
                need(pe, dn["fin"], g.j - 1)
                for c in range(G):
                    ins = nc.tensor.matmul(tok(bank[5 + 2 * g.at(2)])[:, c, :], v1[:, g.at(2), c * P:(c + 1) * P],
                                           wu2[:], start=True, stop=True)
                ins.then_inc(dn["u2"].sem, 1)

            pe.wait_ge(col_step, 3)
            pe.wait_ge(table_step, 7)
            pe.wait_ge(const_step, 1)
            pipelined(pe, NG, [(z1, 1), (z2, 4), (out1, 1), (out2, 4), (tr1, 0), (tr2, 3)])

            need(pe, dn["fin"], NG)
            for ph in (e0, e1):
                first = ph is e0

                def tr(g):
                    w = P if first else D
                    need(pe, ph["norm"], g.j + 1)
                    if first:
                        need(pe, ph["attr"][g.at(3)], attr_landed(g))
                    need(pe, ph["trr"], g.j)
                    for c in range(G):
                        nc.tensor.transpose(bank[0][0:w, c * P:(c + 1) * P], hs[:, g.at(3), c, 0:w], ident[:])
                    for c in range(G):
                        ins = nc.tensor.transpose(bank[1][0:D, c * P:(c + 1) * P], hd[:, g.at(6), c, :], ident[:])
                    ins.then_inc(ph["tr"].sem, 1)

                def hid(g):
                    need(pe, ph["trr"], g.j + 1)
                    need(pe, ph["act"], g.j)
                    if first:
                        nc.tensor.matmul(bank[2][0:D, :], mw1[:], hsT[:, g.at(2), :], start=True, stop=True)
                        products(bank[3][0:D, :], gw1[:], hsT[:, g.at(2), :], ph["hid"])
                    else:
                        nc.tensor.matmul(bank[2][0:D, :], wm1[:, 0, :], hsT[0:D, g.at(2), :], start=True, stop=False)
                        nc.tensor.matmul(bank[2][0:D, :], wm1[:, 1, :], hdT[:, g.at(3), :], start=False, stop=True)\
                            .then_inc(ph["hid"].sem, 1)

                def tokens(g):
                    need(pe, ph["act"], g.j + 1)
                    need(pe, ph["msg"], 3 * g.j if first else g.j)
                    mg = tok(bank[4], D + 1)
                    for c in range(G):
                        ins = nc.tensor.matmul(mg[:, c, 0:D], m1[:, g.at(2), c * P:(c + 1) * P],
                                               (mw2 if first else wm2)[:], start=True, stop=True)
                        if first:
                            ins = nc.tensor.matmul(mg[:, c, D:D + 1], g1[:, g.at(2), c * P:(c + 1) * P], gw2[:],
                                                   start=True, stop=True)
                    ins.then_inc(ph["tok"].sem, 1)

                def seg(g):
                    need(pe, ph["msg"], 3 * (g.j + 1) if first else g.j + 1)
                    need(pe, ph["same"], 2 * (g.j + 1))
                    need(pe, ph["agg"], G * g.j)
                    for c in range(G):
                        ins = nc.tensor.matmul(bank[5][0:D, c * P:(c + 1) * P], msg[:, g.at(2), c, 0:D],
                                               same[:, g.at(3), c, :], start=True, stop=True)
                    ins.then_inc(ph["seg"].sem, 1)

                def upd_z(g):
                    w = uw1 if first else wu1
                    need(pe, ph["agg"], G * (g.j + 1))
                    need(pe, ph["g"], g.j)
                    nc.tensor.matmul(bank[6][0:D, :], w[:, 0, :], hdT[:, g.at(3), :], start=True, stop=False)
                    nc.tensor.matmul(bank[6][0:D, :], w[:, 1, :], aggT[0:D, g.at(3), :], start=False, stop=True)\
                        .then_inc(ph["z"].sem, 1)

                def upd_u(g):
                    need(pe, ph["g"], g.j + 1)
                    need(pe, ph["upd"], 5 * (g.j - 1) + 1 if first else g.j)
                    for c in range(G):
                        ins = nc.tensor.matmul(tok(bank[7])[:, c, :], u1[:, g.at(2), c * P:(c + 1) * P],
                                               (uw2 if first else wu2)[:], start=True, stop=True)
                    ins.then_inc(ph["u"].sem, 1)

                pipelined(pe, EG, [(seg, 4), (tokens, 3), (upd_z, 4), (tr, 2), (upd_u, 4), (hid, 2)])
                need(pe, ph["upd"], (5 if first else 1) * EG)

            for k, ph in enumerate(conv):
                m = D + 1 if k == 0 else D

                def seg(g):
                    need(pe, ph["h"], g.j + 1)
                    need(pe, ph["same"], 2 * (g.j + 1))
                    need(pe, ph["agg"], G * (g.j - 1))
                    for c in range(G):
                        ins = nc.tensor.matmul(bank[g.at(2)][0:m, c * P:(c + 1) * P], msg[:, g.at(2), c, 0:m],
                                               same[:, g.at(3), c, :], start=True, stop=True)
                    ins.then_inc(ph["seg"].sem, 1)

                def apply_w(g):
                    need(pe, ph["agg"], G * (g.j + 1))
                    need(pe, ph["upd"], 2 * (g.j - 1))
                    for c in range(G):
                        ins = nc.tensor.matmul(tok(bank[2 + g.at(2)], m)[:, c, :], aggT[0:m, g.at(3), c * P:(c + 1) * P],
                                               w2[:] if k == 0 else w3[:, k - 1, :], start=True, stop=True)
                    ins.then_inc(ph["u"].sem, 1)

                pipelined(pe, EG, [(apply_w, 4), (seg, 3)])
                need(pe, ph["upd"], 2 * EG)

        @block.vector
        def _(dve):
            nc.vector.memset(st_s[:], NO_NODE).then_inc(pad_set, 1)
            nc.vector.memset(st_d[:], NO_NODE).then_inc(pad_set, 1)
            nc.vector.memset(edge_pad[:], NO_EDGE).then_inc(pad_set, 1)
            nc.vector.memset(neg_half[:], -0.5)
            nc.vector.memset(w2[D:D + 1, :], 1.0)
            nc.vector.memset(w2[0:D, D:D + 1], 0.0)
            for b in (m1, g1, u1):
                nc.vector.memset(b[D:D + 1, :, :], 1.0)
            nc.vector.memset(hs[:, :, :, D:P], 0.0)
            nc.vector.memset(drop[:], 0.0)
            nc.vector.memset(msg[:, :, :, D:D + 1], 1.0)
            nc.vector.memset(mv[:], 1.0)
            nc.vector.memset(aggT[:, 2, :], 0.0).then_inc(const_step, 1)

            dve.wait_ge(blocks_in, 48)
            for k in range(3):
                nc.vector.tensor_copy(blk[:, k, :, :], blk_i[:, k, :, :]).then_inc(blk_f, 1)
            dve.wait_ge(consts, 7)
            nc.vector.tensor_copy(iota_lo[:], iota_lo_i[:])
            nc.vector.tensor_copy(iota_hi[:], iota_hi_i[:])
            nc.vector.tensor_copy(home[:], home_i[:])
            for k in range(3):
                dve.wait_ge(blk_t, k + 1)
                nc.vector.tensor_copy(cols[:, k, :], bank[0][:, 0:ET]).then_inc(col_step, 1)
            dve.wait_ge(col_step, 3)
            nc.vector.tensor_scalar(src_at[:], cols[:, 0, :], 0.0, None, ALU.max)
            nc.vector.tensor_scalar(dst_at[:], cols[:, 1, :], 0.0, None, ALU.max)
            nc.vector.tensor_copy(st_s[:], cols[:, 0, :])
            nc.vector.tensor_copy(st_d[:], cols[:, 1, :])
            nc.vector.tensor_tensor(is_last[:], cols[:, 1, :], cols[:, 2, :], ALU.not_equal)
            nc.vector.tensor_scalar(out_at[:], cols[:, 1, :], -FAR, None, ALU.add)
            nc.vector.tensor_scalar(in_tab[:], cols[:, 1, :], 0.0, None, ALU.is_ge).then_inc(col_step, 1)
            dve.wait_ge(col_step, 4)
            for st, lo, hi in ((st_s, row_src, row_src3), (st_d, row_dst, row_srcc)):
                nc.vector.tensor_single_scalar(lo[:].bitcast(I32), st[:], LO - 1, ALU.bitwise_and)
                nc.vector.tensor_single_scalar(hi[:].bitcast(I32), st[:], LO.bit_length() - 1, ALU.arith_shift_right)
            nc.vector.tensor_tensor(is_last[:], is_last[:], in_tab[:], ALU.mult).then_inc(col_step, 1)
            dve.wait_ge(col_step, 5)
            for which, (lo, hi) in enumerate(((row_src, row_src3), (row_dst, row_srcc))):
                nc.vector.tensor_copy(lo_of[:, which, :], lo[:].bitcast(I32))
                nc.vector.tensor_copy(hi_of[:, which, :], hi[:].bitcast(I32))
            nc.vector.tensor_tensor(out_at[:], out_at[:], is_last[:], ALU.mult).then_inc(col_step, 1)
            dve.wait_ge(col_step, 6)
            nc.vector.tensor_scalar(out_at[:], out_at[:], FAR, None, ALU.add).then_inc(col_step, 1)
            dve.wait_ge(col_step, 7)

            def one_hot(g):
                need(dve, counted, g.j - 1)
                dve.sem_inc(dve_turn, 1)
                for which in range(2):
                    nc.vector.tensor_scalar(hot_hi[:, g.at(2), which, :], iota_hi[:],
                                            hi_of[:, which, bass.ds(g.j, 1)], None, ALU.is_equal)
                    nc.vector.tensor_scalar(hot_lo[:, g.at(2), which, :], iota_lo[:],
                                            lo_of[:, which, bass.ds(g.j, 1)], None, ALU.is_equal).then_inc(hot, 1)

            pipelined(dve, ET, [(one_hot, 0)])

            dve.wait_ge(counted, ET)
            for side in range(2):
                cut = slice(side * 512, side * 512 + 512)
                nc.vector.tensor_copy(degi[:, cut], bank[3 + side][0:HI, :])
                nc.vector.tensor_scalar(dego[:, cut], bank[1 + side][0:HI, :], 1.0, None, ALU.max)
            nc.vector.memset(has[:], 1.0).then_inc(table_step, 1)
            dve.wait_ge(table_step, 1)
            nc.vector.tensor_tensor_scan(cum[:], has[:], degi[:], 0.0, ALU.mult, ALU.add).then_inc(table_step, 1)
            dve.wait_ge(offs, 1)
            nc.vector.tensor_copy(off[:], bank[5][0:HI, 0:1])
            nc.vector.tensor_scalar(has[:], degi[:], 0.0, None, ALU.is_gt).then_inc(table_step, 1)
            dve.wait_ge(table_step, 3)
            nc.vector.tensor_scalar(cum[:], cum[:], off[:, 0:1], -1.0, ALU.add, ALU.add).then_inc(table_step, 1)
            dve.wait_ge(table_step, 4)
            nc.vector.tensor_tensor(cum[:], cum[:], home[:], ALU.subtract).then_inc(table_step, 1)
            dve.wait_ge(table_step, 5)
            nc.vector.tensor_tensor(cum[:], cum[:], has[:], ALU.mult).then_inc(table_step, 1)
            dve.wait_ge(table_step, 6)
            nc.vector.tensor_tensor(info[:, :, 0], cum[:], home[:], ALU.add).then_inc(table_step, 1)

            dve.wait_ge(weights_in, 16 * n_weights[0])
            nc.vector.tensor_scalar(relu_b2[:], rows[:, 4, :], 0.0, None, ALU.max).then_inc(idx_step, 1)

            def moments(x, into, q, step, at):
                for c in range(G):
                    ins = nc.vector.bn_stats(stats[:, q, c, :], x[:, c, :])
                ins.then_inc(step.sem, 1)
                need(dve, step, at + 1)
                dve.sem_inc(dve_turn, 1)
                for c in range(G):
                    ins = nc.vector.bn_aggr(into[:, c, :], stats[:, q, c, :])
                ins.then_inc(step.sem, 1)
                need(dve, step, at + 2)
                dve.sem_inc(dve_turn, 1)

            def roots_of(ph, readers):
                def roots(g):
                    b, at = g.at(3), ROOT * g.j
                    for count, value in readers(g):
                        need(dve, count, value)
                    v = nc.vector
                    v.tensor_scalar(var[:], mv[:, b, :, :, 1].rearrange("p q c -> p (q c)"), EPS, None, ALU.add)\
                        .then_inc(ph["root"].sem, 1)
                    need(dve, ph["root"], at + 1)
                    v.tensor_single_scalar(half[:], var[:].bitcast(I32), 1, ALU.arith_shift_right)\
                        .then_inc(ph["root"].sem, 1)
                    need(dve, ph["root"], at + 2)
                    v.tensor_scalar(guess[:].bitcast(I32), half[:], -1.0, GUESS, ALU.mult, ALU.add)\
                        .then_inc(ph["root"].sem, 1)
                    need(dve, ph["root"], at + 3)
                    v.tensor_tensor(sq[:, 0, :], guess[:], guess[:], ALU.mult).then_inc(ph["root"].sem, 1)
                    need(dve, ph["root"], at + 4)
                    v.tensor_tensor(res[:, 0, :], sq[:, 0, :], var[:], ALU.mult).then_inc(ph["root"].sem, 1)
                    need(dve, ph["root"], at + 5)
                    v.scalar_tensor_tensor(out=root1[:], in0=res[:, 0, :], scalar=-NEWTON, in1=guess[:],
                                           op0=ALU.add, op1=ALU.mult).then_inc(ph["root"].sem, 1)
                    need(dve, ph["root"], at + 6)
                    v.tensor_tensor(sq[:, 1, :], root1[:], root1[:], ALU.mult).then_inc(ph["root"].sem, 1)
                    need(dve, ph["root"], at + 7)
                    v.tensor_tensor(res[:, 1, :], sq[:, 1, :], var[:], ALU.mult).then_inc(ph["root"].sem, 1)
                    need(dve, ph["root"], at + 8)
                    v.tensor_scalar(sq[:, 0, :], res[:, 1, :], CUBE[0], CUBE[1], ALU.mult, ALU.add)\
                        .then_inc(ph["root"].sem, 1)
                    need(dve, ph["root"], at + 9)
                    v.tensor_tensor(sq[:, 1, :], sq[:, 0, :], res[:, 1, :], ALU.mult).then_inc(ph["root"].sem, 1)
                    need(dve, ph["root"], at + 10)
                    r = rstd[:, b, :, :].rearrange("p q c -> p (q c)")
                    v.scalar_tensor_tensor(out=r, in0=sq[:, 1, :], scalar=CUBE[2], in1=root1[:],
                                           op0=ALU.add, op1=ALU.mult).then_inc(ph["root"].sem, 1)
                    need(dve, ph["root"], at + 11)
                    v.scalar_tensor_tensor(out=nmr[:, b, :, :].rearrange("p q c -> p (q c)"),
                                           in0=mv[:, b, :, :, 0].rearrange("p q c -> p (q c)"), scalar=-1.0, in1=r,
                                           op0=ALU.mult, op1=ALU.mult).then_inc(ph["root"].sem, 1)
                return roots

            def wide(row):
                return row.unsqueeze(1).broadcast_to([P, G, D])

            def dense_moments(g):
                need(dve, dn["x_in"][g.at(6)], landed(g, 6))
                dve.sem_inc(dve_turn, 1)
                moments(xd[:, g.at(6), :, :], mv[:, g.at(3), 0, :, :], 0, dn["mom"], 2 * g.j)

            def update_y(ph, g, hd_slot, u_bank, per, b, q):
                nc.vector.tensor_tensor(y[:, g.at(2), :, :], hd[:, hd_slot, :, :], tok(u_bank), ALU.add)\
                    .then_inc(ph["upd"].sem, 1)
                need(dve, ph["upd"], per * g.j + 1)
                moments(y[:, g.at(2), :, :], mv[:, b, q, :, :], q, ph["upd"], per * g.j + 1)

            def update_x(ph, g, lag, per, q, into):
                b = g.shift(lag).at(3)
                need(dve, ph["root"], ROOT * (g.j + lag + 1))
                dve.sem_inc(dve_turn, 1)
                for c in range(G):
                    ins = nc.vector.scalar_tensor_tensor(out=yg[:, g.at(2), c, :], in0=y[:, g.at(2), c, :],
                                                         scalar=mv[:, b, q, c, 0:1], in1=rows[:, 0, :],
                                                         op0=ALU.subtract, op1=ALU.mult)
                ins.then_inc(ph["upd"].sem, 1)
                need(dve, ph["upd"], per * g.j + 4)
                for c in range(G):
                    ins = nc.vector.scalar_tensor_tensor(out=into[:, c, :], in0=yg[:, g.at(2), c, :],
                                                         scalar=rstd[:, b, q, c:c + 1], in1=xb[:, g.at(3), c, :],
                                                         op0=ALU.mult, op1=ALU.add)
                ins.then_inc(ph["upd"].sem, 1)

            def dense_y(g):
                need(dve, dn["u1"], g.j + 1)
                dve.sem_inc(dve_turn, 1)
                update_y(dn, g, g.at(3), bank[2 + 4 * g.at(2)], 7, g.shift(2).at(3), 1)

            def dense_x(g):
                need(dve, dn["xb"], g.j + 1)
                need(dve, dn["x1_out"][g.at(6)], freed(g, 6))
                need(dve, dn["fin"], g.j - 5)
                dve.sem_inc(dve_turn, 1)
                update_x(dn, g, 2, 7, 1, xn[:, g.at(6), :, :])
                need(dve, dn["upd"], 7 * g.j + 5)
                moments(xn[:, g.at(6), :, :], mv[:, g.shift(3).at(3), 2, :, :], 2, dn["upd"], 7 * g.j + 5)

            def dense_finish(g):
                need(dve, dn["u2"], g.j + 1)
                need(dve, dn["x2_out"][g.at(3)], freed(g, 3))
                need(dve, dn["oo"], g.j - 2)
                dve.sem_inc(dve_turn, 1)
                nc.vector.tensor_tensor(xo[:, g.at(3), :, :], xn[:, g.at(6), :, :], tok(bank[5 + 2 * g.at(2)]), ALU.add)\
                    .then_inc(dn["fin"].sem, 1)

            def info_idx(g):
                need(dve, dn["got"][g.at(3)], freed(g, 3, 2 * GI))
                dve.sem_inc(dve_turn, 1)
                nc.vector.tensor_copy(idx[:, g.at(6), 0, 0:GI], src_at[:, bass.ds(g.j * GI, GI)])
                nc.vector.tensor_copy(idx[:, g.at(6), 1, 0:GI], dst_at[:, bass.ds(g.j * GI, GI)])\
                    .then_inc(dn["idx"].sem, 1)

            def info_keep(g):
                need(dve, dn["got"][g.at(3)], landed(g, 3, 2 * GI))
                dve.sem_inc(dve_turn, 1)
                nc.vector.tensor_copy(row_src[:, bass.ds(g.j * GI, GI)], got[:, g.at(3), 0, :, 0])
                nc.vector.tensor_copy(ns[:, bass.ds(g.j * GI, GI)], got[:, g.at(3), 0, :, 1])
                nc.vector.tensor_copy(row_dst[:, bass.ds(g.j * GI, GI)], got[:, g.at(3), 1, :, 0])\
                    .then_inc(dn["kept"].sem, 1)

            def read_dense(g):
                return ((dn["norm"], g.j - 2), (dn["norm2"], g.j - 5))

            dve.wait_ge(info_out, 16)
            pipelined(dve, NG, [(info_idx, 0), (dense_moments, 0), (dense_y, 2), (roots_of(dn, read_dense), 0, NG + 3),
                                (dense_x, 2), (info_keep, 2), (dense_finish, 5)])
            need(dve, dn["fin"], NG)
            for s in range(3):
                need(dve, dn["x2_out"][s], ended(NG, 3, s))
            need(dve, dn["oo"], NG)
            need(dve, dn["kept"], NG)
            need(dve, dn["norm2"], NG)
            nc.vector.tensor_scalar(row_srcc[:], row_src[:], float(E_PAD), None, ALU.min)
            nc.vector.tensor_scalar(in_tab[:], row_src[:], float(E_PAD), float(E_PAD + N), ALU.is_lt, ALU.mult)\
                .then_inc(idx_step, 1)
            dve.wait_ge(idx_step, 2)
            nc.vector.tensor_tensor(row_src3[:], row_src[:], in_tab[:], ALU.add).then_inc(idx_step, 1)
            dve.wait_ge(idx_step, 3)

            def match_of(ph):
                def match(g):
                    s = g.at(3)
                    need(dve, ph["dst"][s], landed(g, 3))
                    need(dve, ph["seg"], g.j - 2)
                    need(dve, ph["agg"], G * (g.j - 2))
                    dve.sem_inc(dve_turn, 1)
                    here = dst_row[:, s, 1:1 + GE].rearrange("p (c e) -> p c e", e=P)
                    nc.vector.tensor_tensor(
                        same[:, s, :, :], here,
                        cols[:, 1, bass.ds(g.j * G, G)].unsqueeze(2).broadcast_to([P, G, P]),
                        ALU.is_equal).then_inc(ph["same"].sem, 1)
                    nc.vector.tensor_tensor(
                        goes_on[:, s, :, :], here,
                        dst_row[:, s, 0:GE].rearrange("p (c e) -> p c e", e=P)[:, :, 0:1].broadcast_to([P, G, P]),
                        ALU.is_equal).then_inc(ph["same"].sem, 1)
                return match

            def sums_of(ph, b, m, done):
                def sums(g):
                    s = g.at(3)
                    need(dve, ph["seg"], g.j + 1)
                    need(dve, ph["same"], 2 * (g.j + 1))
                    need(dve, done, g.j - 2)
                    need(dve, ph["agg"], G * g.j)
                    dve.sem_inc(dve_turn, 1)
                    for c in range(G):
                        carried = aggT[0:m, s, c * P - 1:c * P] if c else aggT[0:m, (s + 2) % 3, GE - 1:GE]
                        if c:
                            need(dve, ph["agg"], G * g.j + c)
                        nc.vector.scalar_tensor_tensor(
                            out=aggT[0:m, s, c * P:(c + 1) * P], in0=goes_on[0:m, s, c, :], scalar=carried,
                            in1=b(g)[0:m, c * P:(c + 1) * P], op0=ALU.mult, op1=ALU.add).then_inc(ph["agg"].sem, 1)
                return sums

            for ph in (e0, e1):
                first = ph is e0

                def take_idx(g):
                    s = g.at(6)
                    need(dve, ph["xs"][s], freed(g, 6, G))
                    need(dve, ph["xd"][s], freed(g, 6, G))
                    dve.sem_inc(dve_turn, 1)
                    nc.vector.tensor_copy(idx[:, s, 0, :], (src_at if first else row_src)[:, bass.ds(g.j * G, G)])
                    nc.vector.tensor_copy(idx[:, s, 1, :], (dst_at if first else row_dst)[:, bass.ds(g.j * G, G)])\
                        .then_inc(ph["idx"].sem, 1)

                def edge_moments(g):
                    b = g.shift(2).at(3)
                    need(dve, ph["xs"][g.at(6)], landed(g, 6, G))
                    need(dve, ph["xd"][g.at(6)], landed(g, 6, G))
                    dve.sem_inc(dve_turn, 1)
                    for q, x in ((0, xs), (1, xd)):
                        for c in range(G):
                            ins = nc.vector.bn_stats(stats[:, q, c, :], x[:, g.at(6), c, :])
                    ins.then_inc(ph["mom"].sem, 1)
                    need(dve, ph["mom"], 2 * g.j + 1)
                    dve.sem_inc(dve_turn, 1)
                    for q in range(2):
                        for c in range(G):
                            ins = nc.vector.bn_aggr(mv[:, b, q, c, :], stats[:, q, c, :])
                    ins.then_inc(ph["mom"].sem, 1)
                    need(dve, ph["mom"], 2 * g.j + 2)

                def times_drop(g):
                    need(dve, ph["tok"], g.j + 1)
                    need(dve, ph["attr"][g.at(3)], attr_landed(g))
                    need(dve, ph["seg"], g.j - 1)
                    nc.vector.tensor_tensor(msg[:, g.at(2), :, 0:D], tok(bank[4], D + 1)[:, :, 0:D],
                                            drop[:, g.at(3), :, :], ALU.mult).then_inc(ph["msg"].sem, 1)

                def new_y(g):
                    need(dve, ph["u"], g.j + 1)
                    dve.sem_inc(dve_turn, 1)
                    nc.vector.tensor_tensor(xb[:, g.at(3), :, :], xd[:, g.at(6), :, :], wide(rows[:, 1, :]), ALU.add)
                    update_y(ph, g, g.at(6), bank[7], 5, g.shift(5).at(3), 2)

                def new_x(g):
                    need(dve, ph["x_out"][g.at(3)], freed(g, 3))
                    if first:
                        update_x(ph, g, 5, 5, 2, xo[:, g.at(3), :, :])
                        return
                    need(dve, ph["u"], g.j + 1)
                    nc.vector.tensor_tensor(xo[:, g.at(3), :, :], xd[:, g.at(6), :, :], tok(bank[7]), ALU.add)\
                        .then_inc(ph["upd"].sem, 1)

                def read_rows(g):
                    return ((ph["norm"], g.j - 4),)

                if not first:
                    for s in range(3):
                        need(dve, e0["x_out"][s], ended(EG, 3, s))
                    nc.vector.memset(aggT[:, 2, GE - 1:GE], 0.0).then_inc(idx_step, 1)
                    dve.wait_ge(idx_step, 4)
                sums = sums_of(ph, lambda g: bank[5], D, ph["z"])
                roots = (roots_of(ph, read_rows), 0, EG + 5)
                if first:
                    stages = [(take_idx, 0), (edge_moments, 2), (match_of(ph), 2), (new_y, 5), roots, (sums, 4), (new_x, 5)]
                else:
                    stages = [(take_idx, 0), (edge_moments, 2), roots, (match_of(ph), 2), (times_drop, 3),
                              (sums, 4), (new_x, 5)]
                pipelined(dve, EG, stages)
                need(dve, ph["z"], EG)
                need(dve, ph["norm"], EG)

            for k, ph in enumerate(conv):
                m = D + 1 if k == 0 else D
                where = (row_src, row_src3, row_srcc, row_srcc)[k]
                before_ph = e1 if k == 0 else conv[k - 1]
                for s in range(3):
                    need(dve, before_ph["x_out"][s], ended(EG, 3, s))
                nc.vector.memset(aggT[:, 2, GE - 1:GE], 0.0).then_inc(idx_step, 1)
                dve.wait_ge(idx_step, 5 + k)

                def take_idx(g):
                    s = g.at(6)
                    need(dve, ph["xs"][s], freed(g, 6, G))
                    need(dve, ph["h"], g.j - 5)
                    need(dve, ph["upd"], 2 * (g.j - 5))
                    dve.sem_inc(dve_turn, 1)
                    if k:
                        nc.vector.tensor_copy(now[:, s, 0, :], ns[:, bass.ds(g.j * G, G)])
                        nc.vector.tensor_copy(now[:, s, 1, :], nd[:, bass.ds(g.j * G, G)])
                    nc.vector.tensor_copy(idx[:, s, 0, :], where[:, bass.ds(g.j * G, G)]).then_inc(ph["idx"].sem, 1)

                def row_moments(g):
                    need(dve, ph["xs"][g.at(6)], landed(g, 6, G))
                    dve.sem_inc(dve_turn, 1)
                    moments(xs[:, g.at(6), :, :], mv[:, g.shift(2).at(3), 0, :, :], 0, ph["mom"], 2 * g.j)

                def read_rows(g):
                    return ((ph["h"], g.j - 4),)

                def times_ns(g):
                    b = g.shift(2).at(3)
                    need(dve, ph["root"], ROOT * (g.j + 2 + 1))
                    need(dve, ph["h"], g.j - 2)
                    nc.vector.tensor_tensor(scaled[:, b, 0, :], rstd[:, b, 0, :], now[:, g.at(6), 0, :], ALU.mult)
                    nc.vector.tensor_tensor(scaled[:, b, 1, :], nmr[:, b, 0, :], now[:, g.at(6), 0, :], ALU.mult)\
                        .then_inc(ph["scaled"].sem, 1)

                def finish(g):
                    u = tok(bank[2 + g.at(2)], m)
                    s, o = g.at(6), g.at(3)
                    need(dve, ph["u"], g.j + 1)
                    if k in (0, 3):
                        need(dve, ph["res"][s], landed(g, 6))
                    if k == 3:
                        need(dve, ph["scattered"][o], freed(g, 3, G))
                    else:
                        need(dve, ph["x_out"][o], freed(g, 3))
                    dve.sem_inc(dve_turn, 1)
                    if k == 0:
                        nc.vector.reciprocal(gate[:, g.at(2), 0, :], u[:, :, D])
                        nc.vector.tensor_copy(deg[:, bass.ds(g.j * G, G)], u[:, :, D]).then_inc(ph["upd"].sem, 1)
                        need(dve, ph["upd"], 2 * g.j + 1)
                        for c in range(G):
                            ins = nc.vector.scalar_tensor_tensor(
                                out=xo[:, o, c, :], in0=u[:, c, 0:D], scalar=gate[:, g.at(2), 0, c:c + 1],
                                in1=xd[:, s, c, :], op0=ALU.mult, op1=ALU.add)
                        ins.then_inc(ph["upd"].sem, 1)
                        return
                    for c in range(G):
                        to = y[:, g.at(2), c, :] if k == 3 else xo[:, o, c, :]
                        ins = nc.vector.scalar_tensor_tensor(
                            out=to, in0=u[:, c, 0:D], scalar=now[:, s, 1, c:c + 1],
                            in1=rows[:, 1 + k, :], op0=ALU.mult, op1=ALU.add)
                    if k < 3:
                        ins.then_inc(ph["upd"].sem, 2)
                        return
                    ins.then_inc(ph["upd"].sem, 1)
                    nc.vector.tensor_copy(idx_out[:, o, :], out_at[:, bass.ds(g.j * G, G)])
                    need(dve, ph["upd"], 2 * g.j + 1)
                    nc.vector.scalar_tensor_tensor(out=xo[:, o, :, :], in0=y[:, g.at(2), :, :], scalar=0.0,
                                                   in1=xd[:, s, :, :], op0=ALU.max, op1=ALU.add)\
                        .then_inc(ph["upd"].sem, 1)

                sums = sums_of(ph, lambda g: bank[g.at(2)], m, ph["u"])
                stages = [(take_idx, 0)]
                if k < 2:
                    stages += [(row_moments, 2), (roots_of(ph, read_rows), 0, EG + 2)]
                if k == 1:
                    stages += [(times_ns, 2)]
                pipelined(dve, EG, stages + [(match_of(ph), 2), (sums, 3), (finish, 4)])
                if k == 0:
                    need(dve, ph["upd"], 2 * EG)
                    dve.wait_ge(nd_made, 1)


_INS = ['x', 'src', 'dst', 'edge_attr_32', 'edge_attr_96',
        'L0_gnn_mW1', 'L0_gnn_mb1', 'L0_gnn_mW2', 'L0_gnn_mb2', 'L0_gnn_gW1', 'L0_gnn_gb1', 'L0_gnn_gW2',
        'L0_gnn_gb2', 'L0_gnn_uW1', 'L0_gnn_ub1', 'L0_gnn_uW2', 'L0_gnn_ub2', 'L0_gnn_ln_g', 'L0_gnn_ln_b',
        'L1_gnn_Wm1', 'L1_gnn_bm1', 'L1_gnn_Wm2', 'L1_gnn_bm2', 'L1_gnn_Wu1', 'L1_gnn_bu1', 'L1_gnn_Wu2',
        'L1_gnn_bu2', 'L2_gnn_W', 'L2_gnn_b', 'L3_gnn_W0', 'L3_gnn_b0', 'L3_gnn_W1', 'L3_gnn_b1',
        'L3_gnn_W2', 'L3_gnn_b2']
_OUTS = [((100000, 96), 'float32')]


def kernel(**inputs):
    import numpy as _np
    import concourse.bacc as _bacc
    from concourse import mybir as _mybir
    from concourse.bass_utils import run_bass_kernel_spmd as _run

    nc = _bacc.Bacc("TRN2", target_bir_lowering=False, num_devices=1)
    arrays, aps = {}, {}
    for name in _INS:
        arr = _np.ascontiguousarray(inputs[name])
        arrays[f"in_{name}_dram"] = arr
        aps[name] = nc.dram_tensor(f"in_{name}_dram", arr.shape, _mybir.dt.from_np(arr.dtype), kind="ExternalInput").ap()
    out = nc.dram_tensor("out_0_dram", _OUTS[0][0], _mybir.dt.float32, kind="ExternalOutput").ap()
    build(nc, aps, out)
    r = _run(nc, [arrays], core_ids=[0])
    return r.results[0]["out_0_dram"]
```

```python
from contextlib import ExitStack

import concourse.bass as bass
from concourse import mybir

F32 = mybir.dt.float32
F16 = mybir.dt.float16
I32 = mybir.dt.int32
ALU = mybir.AluOpType
ACT = mybir.ActivationFunctionType

P = 128
D = 96
DA = 32
N = 100000
E = 50000
G = 4
GE = G * P
EG = 98
ET = EG * G
E_PAD = EG * GE
NG = (N + GE - 1) // GE
UNROLL = 6
GI = 2
HI, LO = 98, 1024
LB = EG
FAR = float(1 << 20)
EPS = 1e-5
GUESS = float(0x5F1FFFF9)
NEWTON = 2.38924456
SCALE = 0.703952253
CUBE = (-3 / 8 * SCALE ** 5, 10 / 8 * SCALE ** 3, -15 / 8 * SCALE)
ROOT = 12
NO_NODE, NO_EDGE = -1, -2
assert HI * LO >= N and E_PAD >= E


class Count:

    def __init__(self, sem, base=0):
        self.sem, self.base = sem, base


def need(eng, count, value):
    sem, base = (count.sem, count.base) if isinstance(count, Count) else (count, 0)
    if not isinstance(value, int) or value > 0:
        eng.wait_ge(sem, value + base)


class Group:

    def __init__(self, turn, c):
        self.turn, self.c = turn, c
        self.j = c if turn is None else turn * UNROLL + c

    def shift(self, by):
        return Group(self.turn, self.c + by)

    def at(self, slots):
        return self.c % slots

    def use(self, slots):
        return self.c // slots if self.turn is None else self.turn * (UNROLL // slots) + self.c // slots


def landed(g, slots, dmas=1):
    return 16 * dmas * (g.use(slots) + 1)


def freed(g, slots, dmas=1):
    return 16 * dmas * g.use(slots)


def ended(n, slots, s, dmas=1):
    return 16 * dmas * ((n - s + slots - 1) // slots)


def rounds(n, stages):
    return n + max(stage[1] for stage in stages)


def pipelined(eng, n, stages):
    most = max(stage[1] for stage in stages)
    last = max([n + most] + [stage[2] for stage in stages if len(stage) > 2])
    first = (most + 2 * UNROLL - 1) // UNROLL * UNROLL
    turns = (n - 1 - first) // UNROLL

    def step(g):
        for stage, lag, *always in stages:
            if g.turn is not None or (always and g.c < always[0]) or (not always and 0 <= g.c - lag < n):
                stage(g.shift(-lag))

    for i in range(first):
        step(Group(None, i))
    with eng.Fori(0, turns) as turn:
        for c in range(UNROLL):
            step(Group(turn, first + c))
    for i in range(first + turns * UNROLL, last):
        step(Group(None, i))


def build(nc, a, out):
    with ExitStack() as ctx:
        def sb(name, shape, dt=F32):
            return ctx.enter_context(nc.sbuf_tensor(name, shape, dt))

        def sem(name):
            return ctx.enter_context(nc.semaphore(name))

        def dram(name, shape, dt=F32):
            return nc.dram_tensor(name, shape, dt, kind="Internal").ap()

        srcp = dram("srcp", (E_PAD,), I32)
        dstp = dram("dstp", (E_PAD + 2,), I32)
        info_d = dram("info_d", (HI * LO, 2))
        t1 = dram("t1", (E_PAD + N, D))
        t2 = dram("t2", (E_PAD + N + E_PAD, D))
        c1 = dram("c1", (E_PAD + 1, D))
        c2 = dram("c2", (E_PAD + 1, D))

        ident = sb("ident", [P, P])
        before = sb("before", [HI, HI])
        iota_lo = sb("iota_lo", [P, LO], F16)
        iota_hi_i = sb("iota_hi_i", [P, P], I32)
        iota_hi = sb("iota_hi", [P, P], F16)
        home_i = sb("home_i", [HI, LO], I32)
        mw1 = sb("mw1", [D + DA, D])
        gw1 = sb("gw1", [D + DA, D])
        mw2 = sb("mw2", [D + 1, D])
        gw2 = sb("gw2", [D + 1, 1])
        uw1 = sb("uw1", [D, 2, D])
        uw2 = sb("uw2", [D + 1, D])
        wm1 = sb("wm1", [D, 2, D])
        wm2 = sb("wm2", [D + 1, D])
        wu1 = sb("wu1", [D, 2, D])
        wu2 = sb("wu2", [D + 1, D])
        w2 = sb("w2", [D + 1, D + 1])
        w3 = sb("w3", [D, 3, D])
        bias = sb("bias", [D, 5])
        rows = sb("rows", [P, 5, D])
        relu_b2 = sb("relu_b2", [P, D])

        st_s = sb("st_s", [P, ET], I32)
        st_d = sb("st_d", [P, ET], I32)
        edge_pad = sb("edge_pad", [1, 2], I32)
        blk_i = sb("blk_i", [LB, 3, 4, P], I32)
        cols = sb("cols", [P, 3, ET])
        src_at = sb("src_at", [P, ET])
        dst_at = sb("dst_at", [P, ET])
        out_at = sb("out_at", [P, ET])
        is_last = sb("is_last", [P, ET])
        in_tab = sb("in_tab", [P, ET])
        lo_of = sb("lo_of", [P, 2, ET])
        hi_of = sb("hi_of", [P, 2, ET])
        row_src = sb("row_src", [P, ET])
        row_dst = sb("row_dst", [P, ET])
        row_src3 = sb("row_src3", [P, ET])
        row_srcc = sb("row_srcc", [P, ET])
        ns = sb("ns", [P, ET])
        nd = sb("nd", [P, ET])
        hot_hi = sb("hot_hi", [P, 2, 2, P], F16)
        apart = sb("apart", [P, 2, 2, P])
        degi = sb("degi", [HI, LO])
        deg = sb("deg", [P, ET])
        cum = sb("cum", [HI, LO])
        home = sb("home", [HI, LO])
        has = sb("has", [HI, LO])
        off = sb("off", [HI, 1])
        info = sb("info", [HI, LO, 2])

        idx = sb("idx", [P, 6, 2, G], I32)
        idx_out = sb("idx_out", [P, 3, G], I32)
        got = sb("got", [P, 3, 2, GI, 2])
        xs = sb("xs", [P, 6, G, D])
        xd = sb("xd", [P, 6, G, D])
        hot_lo = xd[:].rearrange("p s c d -> p (s c d)")[:, 0:2 * LO].bitcast(F16)\
            .rearrange("p (s w n) -> p s w n", s=2, w=2)
        hs = sb("hs", [P, 3, G, P])
        hd = sb("hd", [P, 6, G, D])
        stats = sb("stats", [P, 3, G, 6])
        mv = sb("mv", [P, 3, 3, G, 2])
        var = sb("var", [P, 3 * G])
        mve = sb("mve", [P, 3, G])
        half = sb("half", [P, 3 * G], I32)
        guess = sb("guess", [P, 3 * G])
        sq = sb("sq", [P, 2, 3 * G])
        res = sb("res", [P, 2, 3 * G])
        root1 = sb("root1", [P, 3 * G])
        rstd = sb("rstd", [P, 3, 3, G])
        nmr = sb("nmr", [P, 3, 3, G])
        scaled = sb("scaled", [P, 3, 2, G])
        neg_half = sb("neg_half", [P, 1])
        hsT = sb("hsT", [P, 2, GE])
        hdT = sb("hdT", [D, 6, GE])
        m1 = sb("m1", [D + 1, 2, GE])
        g1 = sb("g1", [D + 1, 2, GE])
        u1 = sb("u1", [D + 1, 2, GE])
        v1 = g1
        gate = sb("gate", [P, 2, 2, G])
        now = sb("now", [P, 6, 2, G])
        msg = sb("msg", [P, 2, G, D + 1])
        same = sb("same", [P, 3, G, P])
        iota_lo_i = same[:, 0:2, :, :].rearrange("p s c e -> p (s c e)").bitcast(I32)
        goes_on = sb("goes_on", [P, 3, G, P])
        minus_prev = sb("minus_prev", [P, 3, G])
        dst_row = sb("dst_row", [P, 3, GE + 1], I32)
        drop = sb("drop", [P, 3, G, D])
        aggT = sb("aggT", [D + 1, 3, GE])
        y = sb("y", [P, 2, G, D])
        yg = sb("yg", [P, 2, G, D])
        yx = sb("yx", [P, G, D])
        xb = sb("xb", [P, 3, G, D])
        dego = xb[0:HI, :, :, :].rearrange("p s c d -> p (s c d)")[:, 0:LO]
        xn = sb("xn", [P, 6, G, D])
        blk = xn[0:LB, 0:4, :, :].rearrange("p s c d -> p (s c d)").rearrange("p (k b e) -> p k b e", k=3, b=4)
        xo = sb("xo", [P, 3, G, D])
        oo = sb("oo", [P, 3, G, D])

        bank = [ctx.enter_context(nc.psum_tensor(f"bank{i}", [P, 512], F32)) for i in range(8)]

        def tok(b, w=D):
            return b[:, 0:G * w].rearrange("p (a c) -> p a c", c=w)

        weights_in = sem("weights_in")
        consts = sem("consts")
        const_step = sem("const_step")
        pad_set = sem("pad_set")
        staged = sem("staged")
        scratch_out = sem("scratch_out")
        blocks_in = sem("blocks_in")
        blk_f = sem("blk_f")
        blk_t = sem("blk_t")
        col_step = sem("col_step")
        hot = sem("hot")
        hot_his = sem("hot_his")
        counted = sem("counted")
        table_step = sem("table_step")
        offs = sem("offs")
        info_out = sem("info_out")
        pool_turn = sem("pool_turn")
        sp_turn = sem("sp_turn")
        nd_made = sem("nd_made")
        ns_made = sem("ns_made")
        dve_turn = sem("dve_turn")
        rows_ready = sem("rows_ready")
        idx_step = sem("idx_step")
        n_weights = [0]

        def Phase(tag, n, counts, slots, own=(), after=None):
            made = {}
            for name in counts:
                made[name] = Count(sem(f"{tag}_{name}")) if after is None else \
                    Count(after[name].sem, after[name].base + after["n"] * after["counts"][name])
            for name, (many, dmas) in slots.items():
                made[name] = []
                for s in range(many):
                    if after is None:
                        made[name].append(Count(sem(f"{tag}_{name}{s}")))
                        continue
                    extra = 16 if name == "attr" and s == (EG - 1) % many else 0
                    last = after[name][s]
                    base = last.base + ended(after["n"], many, s, after["slots"][name][1]) + extra
                    made[name].append(Count(last.sem, base))
            for name in own:
                made[name] = Count(sem(f"{tag}_{name}"))
            return dict(made, n=n, counts=counts, slots=slots)

        dn = Phase("dense", NG, dict(norm=1, mom=2, t1=1, r1=1, z1=1, g1=1, u1=1, upd=4, yu=3, t2=1, r2=1, z2=1, g2=1,
                                     u2=1, fin=1, norm2=1, norm_y=1, xb=1, oo=1, idx=1, kept=1),
                   dict(x_in=(6, 1), x1_out=(6, 1), x2_out=(3, 1), o_out=(3, 1), got=(3, 2 * GI)), ["root"])
        e0 = Phase("edge", EG, dict(idx=1, mom=2, norm=1, same=2, on=2, tr=1, trr=1, hid=1, act=1, tok=1, msg=3, seg=1,
                                    agg=G, z=1, g=1, u=1, upd=5, xb=1),
                   dict(xs=(6, G), xd=(6, G), attr=(3, 1), dst=(3, 1), x_out=(3, 1)), ["root0"])
        e1 = Phase("edge", EG, dict(e0["counts"], on=0, msg=1, upd=1, xb=0), e0["slots"], ["root1"], after=e0)
        e0["by_act"], e1["by_act"] = True, False
        e0["root"], e1["root"] = e0["root0"], e1["root1"]
        conv = []
        for k in range(4):
            conv.append(Phase(
                "conv", EG, dict(idx=1, mom=2 if k < 2 else 0, var=k < 2, std=k < 2, nmr=k < 2, scaled=1 if k == 1 else 0, same=2, on=2 * (k < 2), h=1, seg=1,
                                 agg=G, u=1, upd=2),
                dict(xs=(6, G), dst=(3, 1), res=(6, 1 if k in (0, 3) else 0), x_out=(3, 1 if k < 3 else 0),
                     scattered=(3, G if k == 3 else 0)),
                after=conv[k - 1] if k else None))
            conv[k]["by_act"] = k < 2

        def node_start(j):
            return min(j * GE, N - GE) if isinstance(j, int) else j * GE

        def is_last_group(g, n):
            return g.turn is None and g.c == n - 1

        def node_view(t, first):
            return t[bass.ds(first, GE), :].rearrange("(p c) d -> p c d", c=G)

        def edge_view(t, first):
            return t[bass.ds(first, GE), :].rearrange("(c p) d -> p c d", p=P)

        attr_dmas_last = 2

        def attr_landed(g):
            both = 16 * (attr_dmas_last - 1) if g.turn is None and g.c == EG - 1 else 0
            return landed(g, 3) + both

        block = ctx.enter_context(nc.Block())

        @block.sync
        def _(sp):
            def load(dst, src):
                sp.dma_start(dst, src).then_inc(weights_in, 16)
                n_weights[0] += 1

            sp.wait_ge(pad_set, 3)
            whole = E // ET
            for st, name in ((st_s, "src"), (st_d, "dst")):
                sp.dma_start(st[0:whole, :], a[name][0:whole * ET].rearrange("(p t) -> p t", t=ET)).then_inc(staged, 16)
                sp.dma_start(st[whole:whole + 1, 0:E - whole * ET],
                             a[name][whole * ET:E].rearrange("(p t) -> p t", p=1)).then_inc(staged, 16)
            sp.wait_ge(staged, 64)
            sp.dma_start(srcp.rearrange("(p t) -> p t", t=ET), st_s[:]).then_inc(scratch_out, 16)
            sp.dma_start(dstp[1:1 + E_PAD].rearrange("(p t) -> p t", t=ET), st_d[:]).then_inc(scratch_out, 16)
            sp.dma_start(dstp[0:1].rearrange("(p t) -> p t", p=1), edge_pad[:, 0:1]).then_inc(scratch_out, 16)
            sp.dma_start(dstp[E_PAD + 1:E_PAD + 2].rearrange("(p t) -> p t", p=1), edge_pad[:, 1:2]).then_inc(scratch_out, 16)
            sp.wait_ge(scratch_out, 64)
            for k, flat in enumerate((srcp, dstp[1:1 + E_PAD], dstp[2:2 + E_PAD])):
                sp.dma_start(blk_i[:, k, :, :], flat.rearrange("(b t p) -> t b p", t=LB, p=P)).then_inc(blocks_in, 16)

            load(mw1[:], a["L0_gnn_mW1"][:, :])
            load(gw1[:], a["L0_gnn_gW1"][:, :])
            for w, name, b in ((mw2, "L0_gnn_mW2", "L0_gnn_mb2"), (gw2, "L0_gnn_gW2", "L0_gnn_gb2"),
                               (uw2, "L0_gnn_uW2", "L0_gnn_ub2"), (wm2, "L1_gnn_Wm2", "L1_gnn_bm2"),
                               (wu2, "L1_gnn_Wu2", "L1_gnn_bu2")):
                load(w[0:D, :], a[name][:, :])
                load(w[D:D + 1, :], a[b].rearrange("(p c) -> p c", p=1))
            for w, name in ((uw1, "L0_gnn_uW1"), (wm1, "L1_gnn_Wm1"), (wu1, "L1_gnn_Wu1")):
                load(w[:], a[name].rearrange("(h p) c -> p h c", p=D))
            sp.wait_ge(const_step, 1)
            load(w2[0:D, 0:D], a["L2_gnn_W"][:, :])
            load(w2[D:D + 1, 0:D], a["L2_gnn_b"].rearrange("(p c) -> p c", p=1))
            for k in range(3):
                load(w3[:, k, :], a[f"L3_gnn_W{k}"][:, :])
            for k, name in enumerate(("L0_gnn_mb1", "L0_gnn_gb1", "L0_gnn_ub1", "L1_gnn_bm1", "L1_gnn_bu1")):
                load(bias[:, k:k + 1], a[name].rearrange("(p c) -> p c", c=1))
            for k, name in enumerate(("L0_gnn_ln_g", "L0_gnn_ln_b", "L3_gnn_b0", "L3_gnn_b1", "L3_gnn_b2")):
                load(rows[:, k, :], a[name].partition_broadcast(P))
            sp.wait_ge(weights_in, 16 * n_weights[0])
            for c, k in ((c1, 2), (c2, 3)):
                sp.dma_start(c[E_PAD:E_PAD + 1, :], rows[0:1, k, :]).then_inc(rows_ready, 16)

            sp.wait_ge(table_step, 7)
            sp.wait_ge(ns_made, 10)
            sp.dma_start(info_d.rearrange("(h l) c -> h (l c)", l=LO), info[:].rearrange("h l c -> h (l c)"))\
                .then_inc(info_out, 16)

            def dense_load(g):
                need(sp, dn["upd"], 4 * (g.j - 5))
                sp.sem_inc(sp_turn, 1)
                need(sp, dn["xb"], g.j - 5)
                sp.sem_inc(sp_turn, 1)
                sp.dma_start(xd[:, g.at(6), :, :], node_view(a["x"], node_start(g.j))).then_inc(dn["x_in"][g.at(6)].sem, 16)

            def dense_store_x1(g):
                need(sp, dn["upd"], 4 * (g.j + 1))
                if is_last_group(g, NG):
                    before = g.shift(-1)
                    need(sp, dn["x1_out"][before.at(6)], landed(before, 6))
                sp.sem_inc(sp_turn, 1)
                sp.dma_start(node_view(t1, node_start(g.j) + E_PAD), xn[:, g.at(6), :, :])\
                    .then_inc(dn["x1_out"][g.at(6)].sem, 16)

            def dense_store_x2(g):
                need(sp, dn["fin"], g.j + 1)
                sp.sem_inc(sp_turn, 1)
                need(sp, dn["oo"], g.j + 1)
                if is_last_group(g, NG):
                    before = g.shift(-1)
                    need(sp, dn["x2_out"][before.at(3)], landed(before, 3))
                    need(sp, dn["o_out"][before.at(3)], landed(before, 3))
                sp.sem_inc(sp_turn, 1)
                sp.dma_start(node_view(t2, node_start(g.j) + E_PAD), xo[:, g.at(3), :, :])\
                    .then_inc(dn["x2_out"][g.at(3)].sem, 16)
                sp.dma_start(node_view(out, node_start(g.j)), oo[:, g.at(3), :, :]).then_inc(dn["o_out"][g.at(3)].sem, 16)

            pipelined(sp, NG, [(dense_load, 0), (dense_store_x1, 6), (dense_store_x2, 9)])

            def edge_phase(ph, t, last, behind):
                attr = a["edge_attr_32"] if ph is e0 else a["edge_attr_96"]
                into = hs[:, :, :, D:D + DA] if ph is e0 else drop[:, :, :, :]

                def edge_load(g):
                    s = g.at(3)
                    if ph is e0:
                        need(sp, ph["tr"], g.j - 2)
                        sp.sem_inc(sp_turn, 1)
                    else:
                        need(sp, ph["msg"], g.j - 2)
                        sp.sem_inc(sp_turn, 1)
                    need(sp, ph["same"], 2 * (g.j - 2))
                    sp.sem_inc(sp_turn, 1)
                    if ph["by_act"]:
                        need(sp, ph["on"], 2 * (g.j - 2))
                        sp.sem_inc(sp_turn, 1)
                    first = g.j * GE
                    if is_last_group(g, EG):
                        full = (E - first) // P
                        rest = E - first - full * P
                        sp.dma_start(into[:, s, 0:full, :], attr[first:first + full * P, :]
                                     .rearrange("(c p) d -> p c d", p=P)).then_inc(ph["attr"][s].sem, 16)
                        sp.dma_start(into[0:rest, s, full, :], attr[E - rest:E, :]).then_inc(ph["attr"][s].sem, 16)
                    else:
                        sp.dma_start(into[:, s, :, :], edge_view(attr, first)).then_inc(ph["attr"][s].sem, 16)
                    sp.dma_start(dst_row[:, s, :], dstp[bass.ds(first, GE + 1)].partition_broadcast(P))\
                        .then_inc(ph["dst"][s].sem, 16)

                def edge_store(g):
                    need(sp, ph["upd"], last * (g.j + 1))
                    sp.sem_inc(sp_turn, 1)
                    sp.dma_start(edge_view(t, g.j * GE), xo[:, g.at(3), :, :]).then_inc(ph["x_out"][g.at(3)].sem, 16)

                pipelined(sp, EG, [(edge_load, 1), (edge_store, behind)])

            need(sp, dn["t2"], NG)
            edge_phase(e0, t1, 5, 9)
            need(sp, e0["on"], 2 * EG)
            sp.sem_inc(sp_turn, 1)
            edge_phase(e1, t2, 1, 7)

            for k, ph in enumerate(conv):
                if k in (0, 3):
                    source = e1 if k == 0 else conv[0]
                    for s in range(3):
                        need(sp, source["x_out"][s], ended(EG, 3, s))
                if k == 0:
                    need(sp, e1["upd"], EG)

                def conv_load(g):
                    need(sp, ph["same"], 2 * (g.j - 2))
                    sp.sem_inc(sp_turn, 1)
                    if ph["by_act"]:
                        need(sp, ph["on"], 2 * (g.j - 2))
                        sp.sem_inc(sp_turn, 1)
                    if k in (0, 3):
                        sp.sem_inc(sp_turn, 1)
                        need(sp, ph["upd"], 2 * (g.j - 5))
                    sp.sem_inc(sp_turn, 1)
                    sp.dma_start(dst_row[:, g.at(3), :], dstp[bass.ds(g.j * GE, GE + 1)].partition_broadcast(P))\
                        .then_inc(ph["dst"][g.at(3)].sem, 16)
                    if k in (0, 3):
                        first = g.j * GE + (E_PAD + N if k == 3 else 0)
                        sp.dma_start(xd[:, g.at(6), :, :], edge_view(t2, first)).then_inc(ph["res"][g.at(6)].sem, 16)

                def conv_store(g):
                    need(sp, ph["upd"], 2 * (g.j + 1))
                    sp.sem_inc(sp_turn, 1)
                    t, first = ((t2, E_PAD + N), (c1, 0), (c2, 0))[k]
                    sp.dma_start(edge_view(t, g.j * GE + first), xo[:, g.at(3), :, :])\
                        .then_inc(ph["x_out"][g.at(3)].sem, 16)

                need(sp, e1["same"] if k == 0 else conv[k - 1]["same"], 2 * EG)
                if k in (1, 2):
                    need(sp, conv[k - 1]["on"], 2 * EG)
                pipelined(sp, EG, [(conv_load, 1)] + ([(conv_store, 7)] if k < 3 else []))
            for s in range(3):
                need(sp, conv[1]["x_out"][s], ended(EG, 3, s))
                need(sp, conv[2]["x_out"][s], ended(EG, 3, s))
                need(sp, conv[3]["scattered"][s], ended(EG, 3, s, G))
                need(sp, dn["o_out"][s], ended(NG, 3, s))
            sp.wait_ge(rows_ready, 32)

        @block.gpsimd
        def _(pool):
            nc.gpsimd.memset(ident[:], 0.0).then_inc(consts, 1)
            nc.gpsimd.memset(before[:], 0.0).then_inc(consts, 1)
            pool.wait_ge(consts, 2)
            nc.gpsimd.affine_select(out=ident[:], in_=ident[:], compare_op=ALU.not_equal, fill=1.0, base=0,
                                    pattern=[[-1, P]], channel_multiplier=1).then_inc(consts, 1)
            nc.gpsimd.affine_select(out=before[:], in_=before[:], compare_op=ALU.is_ge, fill=1.0, base=0,
                                    pattern=[[-1, HI]], channel_multiplier=1).then_inc(consts, 1)
            nc.gpsimd.iota(iota_lo_i[:], pattern=[[1, LO]], base=0, channel_multiplier=0).then_inc(consts, 1)
            nc.gpsimd.iota(iota_hi_i[:], pattern=[[1, P]], base=0, channel_multiplier=0).then_inc(consts, 1)
            nc.gpsimd.iota(home_i[:], pattern=[[1, LO]], base=E_PAD, channel_multiplier=LO).then_inc(consts, 1)

            def gather(into, table, indices, done):
                nc.gpsimd.indirect_dma_start(
                    out=into, out_offset=None, in_=table,
                    in_offset=bass.IndirectOffsetOnAxis(ap=indices, axis=0)).then_inc(done.sem, 16)

            pool.wait_ge(const_step, 1)
            pool.wait_ge(info_out, 16)
            pool.wait_ge(weights_in, 16 * n_weights[0])
            pool.wait_ge(idx_step, 1)

            def info_gather(g):
                need(pool, dn["kept"], g.j - 2)
                need(pool, dn["idx"], g.j + 1)
                pool.sem_inc(pool_turn, 1)
                for which in range(2):
                    for c in range(GI):
                        gather(got[:, g.at(3), which, c, :], info_d[:, :], idx[:, g.at(6), which, c:c + 1],
                               dn["got"][g.at(3)])

            def wide(row):
                return row.unsqueeze(1).broadcast_to([P, G, D])

            def dense_xb(g):
                need(pool, dn["x_in"][g.at(6)], landed(g, 6))
                need(pool, dn["upd"], 4 * (g.j - 2))
                pool.sem_inc(pool_turn, 1)
                nc.gpsimd.tensor_tensor(xb[:, g.at(3), :, :], xd[:, g.at(6), :, :], wide(rows[:, 1, :]), ALU.add)\
                    .then_inc(dn["xb"].sem, 1)

            def dense_oo(g):
                need(pool, dn["fin"], g.j + 1)
                need(pool, dn["o_out"][g.at(3)], freed(g, 3))
                pool.sem_inc(pool_turn, 1)
                nc.gpsimd.tensor_tensor(oo[:, g.at(3), :, :], xo[:, g.at(3), :, :], wide(relu_b2[:]), ALU.add)\
                    .then_inc(dn["oo"].sem, 1)

            pipelined(pool, NG, [(dense_xb, 1), (info_gather, 0), (dense_oo, 7)])

            for ph, t in ((e0, a["x"]), (e1, t1)):
                if ph is e1:
                    for s in range(6):
                        need(pool, dn["x1_out"][s], ended(NG, 6, s))
                    for s in range(3):
                        need(pool, e0["x_out"][s], ended(EG, 3, s))
                else:
                    need(pool, dn["upd"], 4 * NG)
                    need(pool, dn["fin"], NG)
                    for s in range(6):
                        need(pool, dn["x1_out"][s], ended(NG, 6, s))

                def edge_gather(g):
                    need(pool, ph["norm"], g.j - 5)
                    if ph is e0:
                        need(pool, ph["xb"], g.j - 5)
                    else:
                        need(pool, ph["upd"], g.j - 5)
                    need(pool, ph["idx"], g.j + 1)
                    pool.sem_inc(pool_turn, 1)
                    for c in range(G):
                        gather(xs[:, g.at(6), c, :], t[:, :], idx[:, g.at(6), 0, c:c + 1], ph["xs"][g.at(6)])
                    for c in range(G):
                        gather(xd[:, g.at(6), c, :], t[:, :], idx[:, g.at(6), 1, c:c + 1], ph["xd"][g.at(6)])

                def edge_xb(g):
                    need(pool, ph["xd"][g.at(6)], landed(g, 6, G))
                    need(pool, ph["upd"], 5 * (g.j - 5))
                    pool.sem_inc(pool_turn, 1)
                    nc.gpsimd.tensor_tensor(xn[:, g.at(6), :, :], xd[:, g.at(6), :, :], wide(rows[:, 1, :]), ALU.add)\
                        .then_inc(ph["xb"].sem, 1)

                pipelined(pool, EG, [(edge_gather, 0)] + ([(edge_xb, 3)] if ph is e0 else []))

            for k, ph in enumerate(conv):
                before_ph = e1 if k == 0 else conv[k - 1]
                for s in range(3):
                    if k == 0:
                        need(pool, dn["x2_out"][s], ended(NG, 3, s))
                    need(pool, before_ph["x_out"][s], ended(EG, 3, s))
                    if k == 3:
                        need(pool, dn["o_out"][s], ended(NG, 3, s))
                if k == 0:
                    need(pool, e1["norm"], EG)
                if k == 1:
                    pool.wait_ge(rows_ready, 32)
                t = (t2[0:E_PAD + N, :], t2, c1, c2)[k]

                def conv_gather(g):
                    need(pool, ph["h"], g.j - 5)
                    need(pool, ph["idx"], g.j + 1)
                    pool.sem_inc(pool_turn, 1)
                    for c in range(G):
                        gather(xs[:, g.at(6), c, :], t[:, :], idx[:, g.at(6), 0, c:c + 1], ph["xs"][g.at(6)])

                def scatter(g):
                    need(pool, ph["upd"], 2 * (g.j + 1))
                    pool.sem_inc(pool_turn, 1)
                    for c in range(G):
                        nc.gpsimd.indirect_dma_start(
                            out=out[:, :], out_offset=bass.IndirectOffsetOnAxis(ap=idx_out[:, g.at(3), c:c + 1], axis=0),
                            in_=xo[:, g.at(3), c, :], in_offset=None, bounds_check=N - 1, oob_is_err=False)\
                            .then_inc(ph["scattered"][g.at(3)].sem, 16)

                def conv_root(g):
                    need(pool, ph["var"], g.j + 1)
                    need(pool, ph["h"], g.j - 2)
                    if k == 1:
                        need(pool, ph["scaled"], g.j - 2)
                    need(pool, ph["nmr"], g.j - 2)
                    pool.sem_inc(pool_turn, 1)
                    nc.gpsimd.tensor_tensor(rstd[:, g.at(3), 0, :], mve[:, g.at(3), :],
                                            neg_half[:, 0:1].broadcast_to([P, G]), ALU.pow).then_inc(ph["std"].sem, 1)

                pipelined(pool, EG, [(conv_gather, 0)] + ([(conv_root, 2)] if k < 2 else []) +
                          ([(scatter, 6)] if k == 3 else []))

        @block.scalar
        def _(act):

            def normed(into, x, b, q):
                for c in range(G):
                    ins = nc.scalar.activation(into[:, c, :], x[:, c, :], ACT.Relu, bias=nmr[:, b, q, c:c + 1],
                                               scale=rstd[:, b, q, c:c + 1])
                return ins

            def hot_rows(g):
                need(act, counted, g.j - 1)
                for which in range(2):
                    ins = nc.scalar.activation(apart[:, g.at(2), which, :], iota_hi[:], ACT.Square,
                                               bias=hi_of[:, which, bass.ds(g.j, 1)], scale=-1.0)
                ins.then_inc(hot_his, 1)
                need(act, hot_his, 2 * g.j + 1)
                nc.scalar.activation(hot_hi[:, g.at(2), :, :], apart[:, g.at(2), :, :], ACT.Relu, bias=1.0, scale=-1.0)\
                    .then_inc(hot_his, 1)

            act.wait_ge(col_step, 7)
            pipelined(act, ET, [(hot_rows, 0)])

            def norm1(g):
                need(act, dn["root"], ROOT * (g.j + 1))
                need(act, dn["yu"], 3 * (g.j - 3) + 1)
                normed(hd[:, g.at(3), :, :], xd[:, g.at(6), :, :], g.at(3), 0).then_inc(dn["norm"].sem, 1)

            def norm2(g):
                need(act, dn["root"], ROOT * (g.j + 4 + 1))
                need(act, dn["t2"], g.j - 2)
                normed(hs[:, g.at(3), :, 0:D], xn[:, g.at(6), :, :], g.shift(4).at(3), 2).then_inc(dn["norm2"].sem, 1)

            def norm_y(g):
                b = g.shift(2).at(3)
                need(act, dn["root"], ROOT * (g.j + 2 + 1))
                need(act, dn["upd"], 4 * (g.j - 2) + 1)
                for c in range(G):
                    ins = nc.scalar.activation(yg[:, g.at(2), c, :], y[:, g.at(2), c, :], ACT.Identity,
                                               bias=nmr[:, b, 1, c:c + 1], scale=rstd[:, b, 1, c:c + 1])
                ins.then_inc(dn["norm_y"].sem, 1)

            def evac1(g):
                need(act, dn["t1"], g.j + 1)
                need(act, dn["z1"], g.j - 1)
                nc.scalar.activation(hdT[:, g.at(2), :], bank[0][0:D, :], ACT.Copy).then_inc(dn["r1"].sem, 1)

            def gelu1(g):
                need(act, dn["z1"], g.j + 1)
                need(act, dn["u1"], g.j - 1)
                nc.scalar.activation(u1[0:D, g.at(2), :], bank[1][0:D, :], ACT.Gelu, bias=bias[:, 2:3])\
                    .then_inc(dn["g1"].sem, 1)

            def evac2(g):
                need(act, dn["t2"], g.j + 1)
                need(act, dn["z2"], g.j - 1)
                nc.scalar.activation(hsT[0:D, g.at(2), :], bank[3][0:D, :], ACT.Copy).then_inc(dn["r2"].sem, 1)

            def relu2(g):
                need(act, dn["z2"], g.j + 1)
                need(act, dn["u2"], g.j - 1)
                nc.scalar.activation(v1[0:D, g.at(2), :], bank[4][0:D, :], ACT.Relu, bias=bias[:, 4:5])\
                    .then_inc(dn["g2"].sem, 1)

            act.wait_ge(const_step, 1)
            act.wait_ge(weights_in, 16 * n_weights[0])
            pipelined(act, NG, [(gelu1, 1), (relu2, 5), (norm1, 0), (norm2, 4), (evac1, 0), (norm_y, 2), (evac2, 4)])

            def goes_on_of(ph):
                def carries(g):
                    s = g.at(3)
                    need(act, ph["same"], 2 * (g.j + 1))
                    need(act, ph["agg"], G * (g.j - 2))
                    for c in range(G):
                        ins = nc.scalar.activation(goes_on[:, s, c, :], dst_row[:, s, 1 + c * P:1 + (c + 1) * P],
                                                   ACT.Square, bias=minus_prev[:, s, c:c + 1])
                    ins.then_inc(ph["on"].sem, 1)
                    need(act, ph["on"], 2 * g.j + 1)
                    nc.scalar.activation(goes_on[:, s, :, :], goes_on[:, s, :, :], ACT.Relu, bias=1.0, scale=-1.0)\
                        .then_inc(ph["on"].sem, 1)
                return carries

            for ph in (e0, e1):
                first = ph is e0

                def norms(g):
                    b = g.shift(2).at(3)
                    need(act, ph["root"], ROOT * (g.j + 2 + 1))
                    need(act, ph["tr"], g.j - 2)
                    normed(hs[:, g.at(3), :, 0:D], xs[:, g.at(6), :, :], b, 0)
                    if first:
                        need(act, ph["upd"], 5 * (g.j - 6) + 1)
                    normed(hd[:, g.at(6), :, :], xd[:, g.at(6), :, :], b, 1).then_inc(ph["norm"].sem, 1)

                def evac(g):
                    need(act, ph["tr"], g.j + 1)
                    need(act, ph["hid"], g.j - 1)
                    nc.scalar.activation(hsT[0:P if first else D, g.at(2), :], bank[0][0:P if first else D, :], ACT.Copy)
                    need(act, ph["z"], g.j - 5)
                    nc.scalar.activation(hdT[:, g.at(6), :], bank[1][0:D, :], ACT.Copy).then_inc(ph["trr"].sem, 1)

                def hidden(g):
                    need(act, ph["hid"], g.j + 1)
                    need(act, ph["tok"], g.j - 1)
                    if first:
                        nc.scalar.activation(m1[0:D, g.at(2), :], bank[2][0:D, :], ACT.Gelu, bias=bias[:, 0:1])
                        nc.scalar.activation(g1[0:D, g.at(2), :], bank[3][0:D, :], ACT.Gelu, bias=bias[:, 1:2])\
                            .then_inc(ph["act"].sem, 1)
                    else:
                        nc.scalar.activation(m1[0:D, g.at(2), :], bank[2][0:D, :], ACT.Relu, bias=bias[:, 3:4])\
                            .then_inc(ph["act"].sem, 1)

                def message(g):
                    mg = tok(bank[4], D + 1)
                    need(act, ph["tok"], g.j + 1)
                    nc.scalar.activation(gate[:, g.at(2), 0, :], mg[:, :, D], ACT.Tanh, scale=0.5)\
                        .then_inc(ph["msg"].sem, 1)
                    need(act, ph["msg"], 3 * g.j + 1)
                    nc.scalar.activation(gate[:, g.at(2), 1, :], gate[:, g.at(2), 0, :], ACT.Copy, scale=0.5, bias=0.5)\
                        .then_inc(ph["msg"].sem, 1)
                    need(act, ph["seg"], g.j - 1)
                    need(act, ph["msg"], 3 * g.j + 2)
                    for c in range(G):
                        ins = nc.scalar.activation(msg[:, g.at(2), c, 0:D], mg[:, c, 0:D], ACT.Copy,
                                                   scale=gate[:, g.at(2), 1, c:c + 1])
                    ins.then_inc(ph["msg"].sem, 1)

                def update_act(g):
                    need(act, ph["z"], g.j + 1)
                    need(act, ph["u"], g.j - 1)
                    nc.scalar.activation(u1[0:D, g.at(2), :], bank[6][0:D, :], ACT.Gelu if first else ACT.Relu,
                                         bias=bias[:, 2:3] if first else bias[:, 4:5]).then_inc(ph["g"].sem, 1)

                if first:
                    pipelined(act, EG, [(norms, 2), (message, 4), (update_act, 6), (hidden, 3), (evac, 2), (goes_on_of(ph), 3)])
                else:
                    pipelined(act, EG, [(norms, 2), (evac, 2), (update_act, 5), (hidden, 2)])

            for k, ph in enumerate(conv):
                def rows_in(g):
                    b = g.at(3)
                    need(act, ph["seg"], g.j - 1)
                    if k == 0:
                        need(act, ph["nmr"], g.j + 1)
                        normed(msg[:, g.at(2), :, 0:D], xs[:, g.at(6), :, :], b, 0).then_inc(ph["h"].sem, 1)
                        return
                    if k == 1:
                        need(act, ph["scaled"], g.j + 1)
                    else:
                        need(act, ph["xs"][g.at(6)], landed(g, 6, G))
                    for c in range(G):
                        if k == 1:
                            ins = nc.scalar.activation(msg[:, g.at(2), c, 0:D], xs[:, g.at(6), c, :], ACT.Relu,
                                                       bias=scaled[:, b, 1, c:c + 1], scale=scaled[:, b, 0, c:c + 1])
                        else:
                            ins = nc.scalar.activation(msg[:, g.at(2), c, 0:D], xs[:, g.at(6), c, :], ACT.Relu,
                                                       scale=now[:, g.at(6), 0, c:c + 1])
                    ins.then_inc(ph["h"].sem, 1)

                if k >= 2:
                    need(act, ph["idx"], 1)
                pipelined(act, EG, [(rows_in, 3), (goes_on_of(ph), 2)] if k < 2 else [(rows_in, 3)])

        @block.tensor
        def _(pe):
            pe.wait_ge(weights_in, 16 * n_weights[0])
            pe.wait_ge(consts, 7)

            for k in range(3):
                pe.wait_ge(blk_f, k + 1)
                if k >= 1:
                    pe.wait_ge(col_step, k)
                for b in range(4):
                    ins = nc.tensor.transpose(bank[0][:, b * LB:(b + 1) * LB], blk[:, k, b, :], ident[0:LB, 0:LB])
                ins.then_inc(blk_t, 1)

            def count(g):
                need(pe, hot, 2 * (g.j + 1))
                need(pe, hot_his, 2 * (g.j + 1))
                for which in range(2):
                    for side in range(2):
                        ins = nc.tensor.matmul(
                            bank[1 + 2 * which + side][0:HI, :], hot_hi[:, g.at(2), which, 0:HI],
                            hot_lo[:, g.at(2), which, side * 512:side * 512 + 512],
                            start=g.turn is None and g.c == 0, stop=g.turn is None and g.c == ET - 1)
                ins.then_inc(counted, 1)

            pipelined(pe, ET, [(count, 0)])
            pe.wait_ge(table_step, 2)
            nc.tensor.matmul(bank[5][0:HI, 0:1], before[:], cum[:, LO - 1:LO], start=True, stop=True)\
                .then_inc(offs, 1)

            def products(into, w, x, done):
                nc.tensor.matmul(into, w, x, start=True, stop=True).then_inc(done.sem, 1)

            def tr1(g):
                need(pe, dn["norm"], g.j + 1)
                need(pe, dn["r1"], g.j)
                for c in range(G):
                    ins = nc.tensor.transpose(bank[0][0:D, c * P:(c + 1) * P], hd[:, g.at(3), c, :], ident[:])
                ins.then_inc(dn["t1"].sem, 1)

            def z1(g):
                need(pe, dn["r1"], g.j + 1)
                need(pe, dn["g1"], g.j)
                products(bank[1][0:D, :], uw1[:, 0, :], hdT[:, g.at(2), :], dn["z1"])

            def out1(g):
                need(pe, dn["g1"], g.j + 1)
                need(pe, dn["yu"], 3 * (g.j - 2) + 1)
                for c in range(G):
                    ins = nc.tensor.matmul(tok(bank[2 + 4 * g.at(2)])[:, c, :], u1[:, g.at(2), c * P:(c + 1) * P],
                                           uw2[:], start=True, stop=True)
                ins.then_inc(dn["u1"].sem, 1)

            def tr2(g):
                need(pe, dn["norm2"], g.j + 1)
                need(pe, dn["r2"], g.j)
                for c in range(G):
                    ins = nc.tensor.transpose(bank[3][0:D, c * P:(c + 1) * P], hs[:, g.at(3), c, 0:D], ident[:])
                ins.then_inc(dn["t2"].sem, 1)

            def z2(g):
                need(pe, dn["r2"], g.j + 1)
                need(pe, dn["g2"], g.j)
                products(bank[4][0:D, :], wu1[:, 0, :], hsT[0:D, g.at(2), :], dn["z2"])

            def out2(g):
                need(pe, dn["g2"], g.j + 1)
                need(pe, dn["fin"], g.j - 1)
                for c in range(G):
                    ins = nc.tensor.matmul(tok(bank[5 + 2 * g.at(2)])[:, c, :], v1[:, g.at(2), c * P:(c + 1) * P],
                                           wu2[:], start=True, stop=True)
                ins.then_inc(dn["u2"].sem, 1)

            pe.wait_ge(col_step, 3)
            pe.wait_ge(table_step, 7)
            pe.wait_ge(const_step, 1)
            pipelined(pe, NG, [(z1, 1), (z2, 5), (out1, 1), (out2, 5), (tr1, 0), (tr2, 4)])

            need(pe, dn["fin"], NG)
            for ph in (e0, e1):
                first = ph is e0

                def tr(g):
                    w = P if first else D
                    need(pe, ph["norm"], g.j + 1)
                    if first:
                        need(pe, ph["attr"][g.at(3)], attr_landed(g))
                    need(pe, ph["trr"], g.j)
                    for c in range(G):
                        nc.tensor.transpose(bank[0][0:w, c * P:(c + 1) * P], hs[:, g.at(3), c, 0:w], ident[:])
                    for c in range(G):
                        ins = nc.tensor.transpose(bank[1][0:D, c * P:(c + 1) * P], hd[:, g.at(6), c, :], ident[:])
                    ins.then_inc(ph["tr"].sem, 1)

                def hid(g):
                    need(pe, ph["trr"], g.j + 1)
                    need(pe, ph["act"], g.j)
                    if first:
                        nc.tensor.matmul(bank[2][0:D, :], mw1[:], hsT[:, g.at(2), :], start=True, stop=True)
                        products(bank[3][0:D, :], gw1[:], hsT[:, g.at(2), :], ph["hid"])
                    else:
                        nc.tensor.matmul(bank[2][0:D, :], wm1[:, 0, :], hsT[0:D, g.at(2), :], start=True, stop=False)
                        nc.tensor.matmul(bank[2][0:D, :], wm1[:, 1, :], hdT[:, g.at(6), :], start=False, stop=True)\
                            .then_inc(ph["hid"].sem, 1)

                def tokens(g):
                    need(pe, ph["act"], g.j + 1)
                    need(pe, ph["msg"], 3 * g.j if first else g.j)
                    mg = tok(bank[4], D + 1)
                    for c in range(G):
                        ins = nc.tensor.matmul(mg[:, c, 0:D], m1[:, g.at(2), c * P:(c + 1) * P],
                                               (mw2 if first else wm2)[:], start=True, stop=True)
                        if first:
                            ins = nc.tensor.matmul(mg[:, c, D:D + 1], g1[:, g.at(2), c * P:(c + 1) * P], gw2[:],
                                                   start=True, stop=True)
                    ins.then_inc(ph["tok"].sem, 1)

                def seg(g):
                    need(pe, ph["msg"], 3 * (g.j + 1) if first else g.j + 1)
                    need(pe, ph["same"], 2 * (g.j + 1))
                    need(pe, ph["agg"], G * g.j)
                    for c in range(G):
                        ins = nc.tensor.matmul(bank[5][0:D, c * P:(c + 1) * P], msg[:, g.at(2), c, 0:D],
                                               same[:, g.at(3), c, :], start=True, stop=True)
                    ins.then_inc(ph["seg"].sem, 1)

                def upd_z(g):
                    w = uw1 if first else wu1
                    need(pe, ph["agg"], G * (g.j + 1))
                    need(pe, ph["g"], g.j)
                    nc.tensor.matmul(bank[6][0:D, :], w[:, 0, :], hdT[:, g.at(6), :], start=True, stop=False)
                    nc.tensor.matmul(bank[6][0:D, :], w[:, 1, :], aggT[0:D, g.at(3), :], start=False, stop=True)\
                        .then_inc(ph["z"].sem, 1)

                def upd_u(g):
                    need(pe, ph["g"], g.j + 1)
                    need(pe, ph["upd"], 5 * (g.j - 1) + 1 if first else g.j)
                    for c in range(G):
                        ins = nc.tensor.matmul(tok(bank[7])[:, c, :], u1[:, g.at(2), c * P:(c + 1) * P],
                                               (uw2 if first else wu2)[:], start=True, stop=True)
                    ins.then_inc(ph["u"].sem, 1)

                if first:
                    pipelined(pe, EG, [(seg, 5), (tokens, 4), (upd_u, 7), (upd_z, 6), (hid, 3), (tr, 2)])
                else:
                    pipelined(pe, EG, [(seg, 4), (tokens, 3), (tr, 2), (upd_z, 5), (hid, 2), (upd_u, 5)])
                need(pe, ph["upd"], (5 if first else 1) * EG)

            for k, ph in enumerate(conv):
                m = D + 1 if k == 0 else D

                def seg(g):
                    need(pe, ph["h"], g.j + 1)
                    need(pe, ph["same"], 2 * (g.j + 1))
                    need(pe, ph["agg"], G * (g.j - 1))
                    for c in range(G):
                        ins = nc.tensor.matmul(bank[g.at(2)][0:m, c * P:(c + 1) * P], msg[:, g.at(2), c, 0:m],
                                               same[:, g.at(3), c, :], start=True, stop=True)
                    ins.then_inc(ph["seg"].sem, 1)

                def apply_w(g):
                    need(pe, ph["agg"], G * (g.j + 1))
                    need(pe, ph["upd"], 2 * (g.j - 1))
                    for c in range(G):
                        ins = nc.tensor.matmul(tok(bank[2 + g.at(2)], m)[:, c, :], aggT[0:m, g.at(3), c * P:(c + 1) * P],
                                               w2[:] if k == 0 else w3[:, k - 1, :], start=True, stop=True)
                    ins.then_inc(ph["u"].sem, 1)

                pipelined(pe, EG, [(seg, 4), (apply_w, 5)])
                need(pe, ph["upd"], 2 * EG)

        @block.vector
        def _(dve):
            nc.vector.memset(st_s[:], NO_NODE).then_inc(pad_set, 1)
            nc.vector.memset(st_d[:], NO_NODE).then_inc(pad_set, 1)
            nc.vector.memset(edge_pad[:], NO_EDGE).then_inc(pad_set, 1)
            nc.vector.memset(neg_half[:], -0.5)
            nc.vector.memset(w2[D:D + 1, :], 1.0)
            nc.vector.memset(w2[0:D, D:D + 1], 0.0)
            for b in (m1, g1, u1):
                nc.vector.memset(b[D:D + 1, :, :], 1.0)
            nc.vector.memset(hs[:, :, :, D:P], 0.0)
            nc.vector.memset(drop[:], 0.0)
            nc.vector.memset(msg[:, :, :, D:D + 1], 1.0)
            nc.vector.memset(mv[:], 1.0)
            nc.vector.memset(aggT[:, 2, :], 0.0).then_inc(const_step, 1)

            dve.wait_ge(blocks_in, 48)
            for k in range(3):
                nc.vector.tensor_copy(blk[:, k, :, :], blk_i[:, k, :, :]).then_inc(blk_f, 1)
            dve.wait_ge(consts, 7)
            nc.vector.tensor_copy(iota_lo[:], iota_lo_i[:])
            nc.vector.tensor_copy(iota_hi[:], iota_hi_i[:])
            nc.vector.tensor_copy(home[:], home_i[:])
            for k in range(3):
                dve.wait_ge(blk_t, k + 1)
                nc.vector.tensor_copy(cols[:, k, :], bank[0][:, 0:ET]).then_inc(col_step, 1)
            dve.wait_ge(col_step, 3)
            nc.vector.tensor_scalar(src_at[:], cols[:, 0, :], 0.0, None, ALU.max)
            nc.vector.tensor_scalar(dst_at[:], cols[:, 1, :], 0.0, None, ALU.max)
            nc.vector.tensor_copy(st_s[:], cols[:, 0, :])
            nc.vector.tensor_copy(st_d[:], cols[:, 1, :])
            nc.vector.tensor_tensor(is_last[:], cols[:, 1, :], cols[:, 2, :], ALU.not_equal)
            nc.vector.tensor_scalar(out_at[:], cols[:, 1, :], -FAR, None, ALU.add)
            nc.vector.tensor_scalar(in_tab[:], cols[:, 1, :], 0.0, None, ALU.is_ge).then_inc(col_step, 1)
            dve.wait_ge(col_step, 4)
            for st, lo, hi in ((st_s, row_src, row_src3), (st_d, row_dst, row_srcc)):
                nc.vector.tensor_single_scalar(lo[:].bitcast(I32), st[:], LO - 1, ALU.bitwise_and)
                nc.vector.tensor_single_scalar(hi[:].bitcast(I32), st[:], LO.bit_length() - 1, ALU.arith_shift_right)
            nc.vector.tensor_tensor(is_last[:], is_last[:], in_tab[:], ALU.mult).then_inc(col_step, 1)
            dve.wait_ge(col_step, 5)
            for which, (lo, hi) in enumerate(((row_src, row_src3), (row_dst, row_srcc))):
                nc.vector.tensor_copy(lo_of[:, which, :], lo[:].bitcast(I32))
                nc.vector.tensor_copy(hi_of[:, which, :], hi[:].bitcast(I32))
            nc.vector.tensor_tensor(out_at[:], out_at[:], is_last[:], ALU.mult).then_inc(col_step, 1)
            dve.wait_ge(col_step, 6)
            nc.vector.tensor_scalar(out_at[:], out_at[:], FAR, None, ALU.add).then_inc(col_step, 1)
            dve.wait_ge(col_step, 7)

            def one_hot(g):
                need(dve, counted, g.j - 1)
                dve.sem_inc(dve_turn, 1)
                for which in range(2):
                    nc.vector.tensor_scalar(hot_lo[:, g.at(2), which, :], iota_lo[:],
                                            lo_of[:, which, bass.ds(g.j, 1)], None, ALU.is_equal).then_inc(hot, 1)

            pipelined(dve, ET, [(one_hot, 0)])

            dve.wait_ge(counted, ET)
            for side in range(2):
                cut = slice(side * 512, side * 512 + 512)
                nc.vector.tensor_copy(degi[:, cut], bank[3 + side][0:HI, :])
                nc.vector.tensor_scalar(dego[:, cut], bank[1 + side][0:HI, :], 1.0, None, ALU.max)
            nc.vector.memset(has[:], 1.0).then_inc(table_step, 1)
            dve.wait_ge(table_step, 1)
            nc.vector.tensor_tensor_scan(cum[:], has[:], degi[:], 0.0, ALU.mult, ALU.add).then_inc(table_step, 1)
            dve.wait_ge(offs, 1)
            nc.vector.tensor_copy(off[:], bank[5][0:HI, 0:1])
            nc.vector.tensor_scalar(has[:], degi[:], 0.0, None, ALU.is_gt).then_inc(table_step, 1)
            dve.wait_ge(table_step, 3)
            nc.vector.tensor_scalar(cum[:], cum[:], off[:, 0:1], -1.0, ALU.add, ALU.add).then_inc(table_step, 1)
            dve.wait_ge(table_step, 4)
            nc.vector.tensor_tensor(cum[:], cum[:], home[:], ALU.subtract).then_inc(table_step, 1)
            dve.wait_ge(table_step, 5)
            nc.vector.tensor_tensor(cum[:], cum[:], has[:], ALU.mult).then_inc(table_step, 1)
            dve.wait_ge(table_step, 6)
            nc.vector.tensor_tensor(info[:, :, 0], cum[:], home[:], ALU.add).then_inc(table_step, 1)

            def degree_roots(into, of, scratch, done):
                p, q, r, t = scratch
                v = nc.vector

                def then(ins, step):
                    ins.then_inc(done, 1)
                    dve.wait_ge(done, step)

                then(v.tensor_single_scalar(p.bitcast(I32), of.bitcast(I32), 1, ALU.arith_shift_right), 1)
                then(v.tensor_scalar(q.bitcast(I32), p.bitcast(I32), -1.0, GUESS, ALU.mult, ALU.add), 2)
                then(v.tensor_tensor(p, q, q, ALU.mult), 3)
                then(v.tensor_tensor(r, p, of, ALU.mult), 4)
                then(v.scalar_tensor_tensor(out=t, in0=r, scalar=-NEWTON, in1=q, op0=ALU.add, op1=ALU.mult), 5)
                then(v.tensor_tensor(p, t, t, ALU.mult), 6)
                then(v.tensor_tensor(r, p, of, ALU.mult), 7)
                then(v.tensor_scalar(p, r, CUBE[0], CUBE[1], ALU.mult, ALU.add), 8)
                then(v.tensor_tensor(q, p, r, ALU.mult), 9)
                then(v.scalar_tensor_tensor(out=into, in0=q, scalar=CUBE[2], in1=t, op0=ALU.add, op1=ALU.mult), 10)

            x_flat = [b[:, :, :, :].rearrange("p s c d -> p (s c d)") for b in (xs, xd, hd)]
            degree_roots(info[:, :, 1], dego,
                         [b[0:HI, i * LO:(i + 1) * LO] for b in x_flat[0:2] for i in range(2)], ns_made)
            dve.wait_ge(weights_in, 16 * n_weights[0])
            nc.vector.tensor_scalar(relu_b2[:], rows[:, 4, :], 0.0, None, ALU.max).then_inc(idx_step, 1)

            def moments(x, into, q, step, at):
                for c in range(G):
                    ins = nc.vector.bn_stats(stats[:, q, c, :], x[:, c, :])
                ins.then_inc(step.sem, 1)
                need(dve, step, at + 1)
                dve.sem_inc(dve_turn, 1)
                for c in range(G):
                    ins = nc.vector.bn_aggr(into[:, c, :], stats[:, q, c, :])
                ins.then_inc(step.sem, 1)
                need(dve, step, at + 2)
                dve.sem_inc(dve_turn, 1)

            def roots_of(ph, readers):
                def roots(g):
                    b, at = g.at(3), ROOT * g.j
                    for count, value in readers(g):
                        need(dve, count, value)
                    v = nc.vector
                    v.tensor_scalar(var[:], mv[:, b, :, :, 1].rearrange("p q c -> p (q c)"), EPS, None, ALU.add)\
                        .then_inc(ph["root"].sem, 1)
                    need(dve, ph["root"], at + 1)
                    v.tensor_single_scalar(half[:], var[:].bitcast(I32), 1, ALU.arith_shift_right)\
                        .then_inc(ph["root"].sem, 1)
                    need(dve, ph["root"], at + 2)
                    v.tensor_scalar(guess[:].bitcast(I32), half[:], -1.0, GUESS, ALU.mult, ALU.add)\
                        .then_inc(ph["root"].sem, 1)
                    need(dve, ph["root"], at + 3)
                    v.tensor_tensor(sq[:, 0, :], guess[:], guess[:], ALU.mult).then_inc(ph["root"].sem, 1)
                    need(dve, ph["root"], at + 4)
                    v.tensor_tensor(res[:, 0, :], sq[:, 0, :], var[:], ALU.mult).then_inc(ph["root"].sem, 1)
                    need(dve, ph["root"], at + 5)
                    v.scalar_tensor_tensor(out=root1[:], in0=res[:, 0, :], scalar=-NEWTON, in1=guess[:],
                                           op0=ALU.add, op1=ALU.mult).then_inc(ph["root"].sem, 1)
                    need(dve, ph["root"], at + 6)
                    v.tensor_tensor(sq[:, 1, :], root1[:], root1[:], ALU.mult).then_inc(ph["root"].sem, 1)
                    need(dve, ph["root"], at + 7)
                    v.tensor_tensor(res[:, 1, :], sq[:, 1, :], var[:], ALU.mult).then_inc(ph["root"].sem, 1)
                    need(dve, ph["root"], at + 8)
                    v.tensor_scalar(sq[:, 0, :], res[:, 1, :], CUBE[0], CUBE[1], ALU.mult, ALU.add)\
                        .then_inc(ph["root"].sem, 1)
                    need(dve, ph["root"], at + 9)
                    v.tensor_tensor(sq[:, 1, :], sq[:, 0, :], res[:, 1, :], ALU.mult).then_inc(ph["root"].sem, 1)
                    need(dve, ph["root"], at + 10)
                    r = rstd[:, b, :, :].rearrange("p q c -> p (q c)")
                    v.scalar_tensor_tensor(out=r, in0=sq[:, 1, :], scalar=CUBE[2], in1=root1[:],
                                           op0=ALU.add, op1=ALU.mult).then_inc(ph["root"].sem, 1)
                    need(dve, ph["root"], at + 11)
                    v.scalar_tensor_tensor(out=nmr[:, b, :, :].rearrange("p q c -> p (q c)"),
                                           in0=mv[:, b, :, :, 0].rearrange("p q c -> p (q c)"), scalar=-1.0, in1=r,
                                           op0=ALU.mult, op1=ALU.mult).then_inc(ph["root"].sem, 1)
                return roots

            def wide(row):
                return row.unsqueeze(1).broadcast_to([P, G, D])

            def dense_moments(g):
                need(dve, dn["x_in"][g.at(6)], landed(g, 6))
                dve.sem_inc(dve_turn, 1)
                moments(xd[:, g.at(6), :, :], mv[:, g.at(3), 0, :, :], 0, dn["mom"], 2 * g.j)

            def update_y(step, g, hd_slot, u_bank, per, b, q):
                nc.vector.tensor_tensor(y[:, g.at(2), :, :], hd[:, hd_slot, :, :], tok(u_bank), ALU.add)\
                    .then_inc(step.sem, 1)
                need(dve, step, per * g.j + 1)
                moments(y[:, g.at(2), :, :], mv[:, b, q, :, :], q, step, per * g.j + 1)

            def update_x(ph, g, lag, per, q, into, shifted):
                b = g.shift(lag).at(3)
                need(dve, ph["root"], ROOT * (g.j + lag + 1))
                dve.sem_inc(dve_turn, 1)
                for c in range(G):
                    ins = nc.vector.scalar_tensor_tensor(out=yg[:, g.at(2), c, :], in0=y[:, g.at(2), c, :],
                                                         scalar=mv[:, b, q, c, 0:1], in1=rows[:, 0, :],
                                                         op0=ALU.subtract, op1=ALU.mult)
                ins.then_inc(ph["upd"].sem, 1)
                need(dve, ph["upd"], per * g.j + 4)
                for c in range(G):
                    ins = nc.vector.scalar_tensor_tensor(out=into[:, c, :], in0=yg[:, g.at(2), c, :],
                                                         scalar=rstd[:, b, q, c:c + 1], in1=shifted[:, c, :],
                                                         op0=ALU.mult, op1=ALU.add)
                ins.then_inc(ph["upd"].sem, 1)

            def dense_y(g):
                need(dve, dn["u1"], g.j + 1)
                dve.sem_inc(dve_turn, 1)
                need(dve, dn["norm_y"], g.j - 1)
                dve.sem_inc(dve_turn, 1)
                update_y(dn["yu"], g, g.at(3), bank[2 + 4 * g.at(2)], 3, g.shift(2).at(3), 1)

            def dense_x(g):
                need(dve, dn["xb"], g.j + 1)
                need(dve, dn["x1_out"][g.at(6)], freed(g, 6))
                need(dve, dn["fin"], g.j - 5)
                dve.sem_inc(dve_turn, 1)
                need(dve, dn["norm_y"], g.j + 1)
                dve.sem_inc(dve_turn, 1)
                nc.vector.tensor_tensor(yx[:], yg[:, g.at(2), :, :], wide(rows[:, 0, :]), ALU.mult)\
                    .then_inc(dn["upd"].sem, 1)
                need(dve, dn["upd"], 4 * g.j + 1)
                nc.vector.tensor_tensor(xn[:, g.at(6), :, :], yx[:], xb[:, g.at(3), :, :], ALU.add)\
                    .then_inc(dn["upd"].sem, 1)
                need(dve, dn["upd"], 4 * g.j + 2)
                moments(xn[:, g.at(6), :, :], mv[:, g.shift(4).at(3), 2, :, :], 2, dn["upd"], 4 * g.j + 2)

            def dense_finish(g):
                need(dve, dn["u2"], g.j + 1)
                need(dve, dn["x2_out"][g.at(3)], freed(g, 3))
                need(dve, dn["oo"], g.j - 2)
                dve.sem_inc(dve_turn, 1)
                nc.vector.tensor_tensor(xo[:, g.at(3), :, :], xn[:, g.at(6), :, :], tok(bank[5 + 2 * g.at(2)]), ALU.add)\
                    .then_inc(dn["fin"].sem, 1)

            def info_idx(g):
                need(dve, dn["got"][g.at(3)], freed(g, 3, 2 * GI))
                dve.sem_inc(dve_turn, 1)
                nc.vector.tensor_copy(idx[:, g.at(6), 0, 0:GI], src_at[:, bass.ds(g.j * GI, GI)])
                nc.vector.tensor_copy(idx[:, g.at(6), 1, 0:GI], dst_at[:, bass.ds(g.j * GI, GI)])\
                    .then_inc(dn["idx"].sem, 1)

            def info_keep(g):
                need(dve, dn["got"][g.at(3)], landed(g, 3, 2 * GI))
                dve.sem_inc(dve_turn, 1)
                nc.vector.tensor_copy(row_src[:, bass.ds(g.j * GI, GI)], got[:, g.at(3), 0, :, 0])
                nc.vector.tensor_copy(ns[:, bass.ds(g.j * GI, GI)], got[:, g.at(3), 0, :, 1])
                nc.vector.tensor_copy(row_dst[:, bass.ds(g.j * GI, GI)], got[:, g.at(3), 1, :, 0])\
                    .then_inc(dn["kept"].sem, 1)

            def read_dense(g):
                done = ((dn["norm"], g.j - 2), (dn["norm_y"], g.j - 4), (dn["norm2"], g.j - 6))
                return done if g.turn is not None else [(count, min(value, NG)) for count, value in done]

            dve.wait_ge(info_out, 16)
            pipelined(dve, NG, [(info_idx, 0), (dense_moments, 0), (dense_y, 2), (roots_of(dn, read_dense), 0, NG + 4),
                                (dense_x, 3), (info_keep, 2), (dense_finish, 6)])
            need(dve, dn["fin"], NG)
            for s in range(3):
                need(dve, dn["x2_out"][s], ended(NG, 3, s))
            need(dve, dn["oo"], NG)
            need(dve, dn["kept"], NG)
            need(dve, dn["norm2"], NG)
            nc.vector.tensor_scalar(row_srcc[:], row_src[:], float(E_PAD), None, ALU.min)
            nc.vector.tensor_scalar(in_tab[:], row_src[:], float(E_PAD), float(E_PAD + N), ALU.is_lt, ALU.mult)\
                .then_inc(idx_step, 1)
            dve.wait_ge(idx_step, 2)
            nc.vector.tensor_tensor(row_src3[:], row_src[:], in_tab[:], ALU.add).then_inc(idx_step, 1)
            dve.wait_ge(idx_step, 3)

            def match_of(ph):
                def match(g):
                    s = g.at(3)
                    need(dve, ph["dst"][s], landed(g, 3))
                    need(dve, ph["seg"], g.j - 2)
                    need(dve, ph["agg"], G * (g.j - 2))
                    dve.sem_inc(dve_turn, 1)
                    here = dst_row[:, s, 1:1 + GE].rearrange("p (c e) -> p c e", e=P)
                    nc.vector.tensor_tensor(
                        same[:, s, :, :], here,
                        cols[:, 1, bass.ds(g.j * G, G)].unsqueeze(2).broadcast_to([P, G, P]),
                        ALU.is_equal).then_inc(ph["same"].sem, 1)
                    if not ph["by_act"]:
                        nc.vector.tensor_tensor(
                            goes_on[:, s, :, :], here,
                            dst_row[:, s, 0:GE].rearrange("p (c e) -> p c e", e=P)[:, :, 0:1].broadcast_to([P, G, P]),
                            ALU.is_equal).then_inc(ph["same"].sem, 1)
                        return
                    need(dve, ph["on"], 2 * (g.j - 2))
                    dve.sem_inc(dve_turn, 1)
                    nc.vector.tensor_scalar(
                        minus_prev[:, s, :], dst_row[:, s, 0:GE].rearrange("p (c e) -> p c e", e=P)[:, :, 0],
                        -1.0, None, ALU.mult).then_inc(ph["same"].sem, 1)
                return match

            def sums_of(ph, b, m, done):
                def sums(g):
                    s = g.at(3)
                    need(dve, ph["seg"], g.j + 1)
                    if ph["by_act"]:
                        need(dve, ph["on"], 2 * (g.j + 1))
                    else:
                        need(dve, ph["same"], 2 * (g.j + 1))
                    need(dve, done, g.j - 2)
                    need(dve, ph["agg"], G * g.j)
                    dve.sem_inc(dve_turn, 1)
                    for c in range(G):
                        carried = aggT[0:m, s, c * P - 1:c * P] if c else aggT[0:m, (s + 2) % 3, GE - 1:GE]
                        if c:
                            need(dve, ph["agg"], G * g.j + c)
                        nc.vector.scalar_tensor_tensor(
                            out=aggT[0:m, s, c * P:(c + 1) * P], in0=goes_on[0:m, s, c, :], scalar=carried,
                            in1=b(g)[0:m, c * P:(c + 1) * P], op0=ALU.mult, op1=ALU.add).then_inc(ph["agg"].sem, 1)
                return sums

            for ph in (e0, e1):
                first = ph is e0

                def take_idx(g):
                    s = g.at(6)
                    need(dve, ph["xs"][s], freed(g, 6, G))
                    need(dve, ph["xd"][s], freed(g, 6, G))
                    dve.sem_inc(dve_turn, 1)
                    nc.vector.tensor_copy(idx[:, s, 0, :], (src_at if first else row_src)[:, bass.ds(g.j * G, G)])
                    nc.vector.tensor_copy(idx[:, s, 1, :], (dst_at if first else row_dst)[:, bass.ds(g.j * G, G)])\
                        .then_inc(ph["idx"].sem, 1)

                def edge_moments(g):
                    b = g.shift(2).at(3)
                    need(dve, ph["xs"][g.at(6)], landed(g, 6, G))
                    need(dve, ph["xd"][g.at(6)], landed(g, 6, G))
                    dve.sem_inc(dve_turn, 1)
                    for q, x in ((0, xs), (1, xd)):
                        for c in range(G):
                            ins = nc.vector.bn_stats(stats[:, q, c, :], x[:, g.at(6), c, :])
                    ins.then_inc(ph["mom"].sem, 1)
                    need(dve, ph["mom"], 2 * g.j + 1)
                    dve.sem_inc(dve_turn, 1)
                    for q in range(2):
                        for c in range(G):
                            ins = nc.vector.bn_aggr(mv[:, b, q, c, :], stats[:, q, c, :])
                    ins.then_inc(ph["mom"].sem, 1)
                    need(dve, ph["mom"], 2 * g.j + 2)

                def times_drop(g):
                    need(dve, ph["tok"], g.j + 1)
                    need(dve, ph["attr"][g.at(3)], attr_landed(g))
                    need(dve, ph["seg"], g.j - 1)
                    nc.vector.tensor_tensor(msg[:, g.at(2), :, 0:D], tok(bank[4], D + 1)[:, :, 0:D],
                                            drop[:, g.at(3), :, :], ALU.mult).then_inc(ph["msg"].sem, 1)

                def new_y(g):
                    need(dve, ph["u"], g.j + 1)
                    dve.sem_inc(dve_turn, 1)
                    update_y(ph["upd"], g, g.at(6), bank[7], 5, g.shift(8).at(3), 2)

                def new_x(g):
                    need(dve, ph["x_out"][g.at(3)], freed(g, 3))
                    if first:
                        need(dve, ph["xb"], g.j + 1)
                        update_x(ph, g, 8, 5, 2, xo[:, g.at(3), :, :], xn[:, g.at(6), :, :])
                        return
                    need(dve, ph["u"], g.j + 1)
                    nc.vector.tensor_tensor(xo[:, g.at(3), :, :], xd[:, g.at(6), :, :], tok(bank[7]), ALU.add)\
                        .then_inc(ph["upd"].sem, 1)

                def read_rows(g):
                    return ((ph["norm"], g.j - 4 if g.turn is not None else min(g.j - 4, EG)),)

                if not first:
                    for s in range(3):
                        need(dve, e0["x_out"][s], ended(EG, 3, s))
                    nc.vector.memset(aggT[:, 2, GE - 1:GE], 0.0).then_inc(idx_step, 1)
                    dve.wait_ge(idx_step, 4)
                sums = sums_of(ph, lambda g: bank[5], D, ph["z"])
                roots = (roots_of(ph, read_rows), 0, EG + (8 if first else 2))
                if first:
                    stages = [(take_idx, 0), (edge_moments, 2), (match_of(ph), 3), (new_y, 8), roots, (sums, 5), (new_x, 8)]
                else:
                    stages = [(take_idx, 0), (edge_moments, 2), roots, (match_of(ph), 2), (new_x, 6),
                              (times_drop, 3), (sums, 4)]
                pipelined(dve, EG, stages)
                need(dve, ph["z"], EG)
                need(dve, ph["norm"], EG)

            for k, ph in enumerate(conv):
                m = D + 1 if k == 0 else D
                where = (row_src, row_src3, row_srcc, row_srcc)[k]
                before_ph = e1 if k == 0 else conv[k - 1]
                for s in range(3):
                    need(dve, before_ph["x_out"][s], ended(EG, 3, s))
                nc.vector.memset(aggT[:, 2, GE - 1:GE], 0.0).then_inc(idx_step, 1)
                dve.wait_ge(idx_step, 5 + k)
                if k in (1, 2):
                    need(dve, conv[k - 1]["on"], 2 * EG)

                def take_idx(g):
                    s = g.at(6)
                    need(dve, ph["xs"][s], freed(g, 6, G))
                    need(dve, ph["h"], g.j - 5)
                    need(dve, ph["upd"], 2 * (g.j - 5))
                    dve.sem_inc(dve_turn, 1)
                    if k:
                        nc.vector.tensor_copy(now[:, s, 0, :], ns[:, bass.ds(g.j * G, G)])
                        nc.vector.tensor_copy(now[:, s, 1, :], nd[:, bass.ds(g.j * G, G)])
                    nc.vector.tensor_copy(idx[:, s, 0, :], where[:, bass.ds(g.j * G, G)]).then_inc(ph["idx"].sem, 1)

                def row_moments(g):
                    need(dve, ph["xs"][g.at(6)], landed(g, 6, G))
                    dve.sem_inc(dve_turn, 1)
                    moments(xs[:, g.at(6), :, :], mv[:, g.at(3), 0, :, :], 0, ph["mom"], 2 * g.j)
                    need(dve, ph["mom"], 2 * g.j + 2)
                    need(dve, ph["std"], g.j - 2)
                    nc.vector.tensor_scalar(mve[:, g.at(3), :], mv[:, g.at(3), 0, :, 1], EPS, None, ALU.add)\
                        .then_inc(ph["var"].sem, 1)

                def minus_mean(g):
                    need(dve, ph["std"], g.j + 1)
                    need(dve, ph["h"], g.j - 2)
                    if k == 1:
                        need(dve, ph["scaled"], g.j - 2)
                    nc.vector.scalar_tensor_tensor(out=nmr[:, g.at(3), 0, :], in0=mv[:, g.at(3), 0, :, 0], scalar=-1.0,
                                                   in1=rstd[:, g.at(3), 0, :], op0=ALU.mult, op1=ALU.mult)\
                        .then_inc(ph["nmr"].sem, 1)

                def times_ns(g):
                    b = g.at(3)
                    need(dve, ph["nmr"], g.j + 1)
                    nc.vector.tensor_tensor(scaled[:, b, 0, :], rstd[:, b, 0, :], now[:, g.at(6), 0, :], ALU.mult)
                    nc.vector.tensor_tensor(scaled[:, b, 1, :], nmr[:, b, 0, :], now[:, g.at(6), 0, :], ALU.mult)\
                        .then_inc(ph["scaled"].sem, 1)

                def finish(g):
                    u = tok(bank[2 + g.at(2)], m)
                    s, o = g.at(6), g.at(3)
                    need(dve, ph["u"], g.j + 1)
                    if k in (0, 3):
                        need(dve, ph["res"][s], landed(g, 6))
                    if k == 3:
                        need(dve, ph["scattered"][o], freed(g, 3, G))
                    else:
                        need(dve, ph["x_out"][o], freed(g, 3))
                    dve.sem_inc(dve_turn, 1)
                    if k == 0:
                        nc.vector.reciprocal(gate[:, g.at(2), 0, :], u[:, :, D])
                        nc.vector.tensor_copy(deg[:, bass.ds(g.j * G, G)], u[:, :, D]).then_inc(ph["upd"].sem, 1)
                        need(dve, ph["upd"], 2 * g.j + 1)
                        for c in range(G):
                            ins = nc.vector.scalar_tensor_tensor(
                                out=xo[:, o, c, :], in0=u[:, c, 0:D], scalar=gate[:, g.at(2), 0, c:c + 1],
                                in1=xd[:, s, c, :], op0=ALU.mult, op1=ALU.add)
                        ins.then_inc(ph["upd"].sem, 1)
                        return
                    for c in range(G):
                        to = y[:, g.at(2), c, :] if k == 3 else xo[:, o, c, :]
                        ins = nc.vector.scalar_tensor_tensor(
                            out=to, in0=u[:, c, 0:D], scalar=now[:, s, 1, c:c + 1],
                            in1=rows[:, 1 + k, :], op0=ALU.mult, op1=ALU.add)
                    if k < 3:
                        ins.then_inc(ph["upd"].sem, 2)
                        return
                    ins.then_inc(ph["upd"].sem, 1)
                    nc.vector.tensor_copy(idx_out[:, o, :], out_at[:, bass.ds(g.j * G, G)])
                    need(dve, ph["upd"], 2 * g.j + 1)
                    nc.vector.scalar_tensor_tensor(out=xo[:, o, :, :], in0=y[:, g.at(2), :, :], scalar=0.0,
                                                   in1=xd[:, s, :, :], op0=ALU.max, op1=ALU.add)\
                        .then_inc(ph["upd"].sem, 1)

                sums = sums_of(ph, lambda g: bank[g.at(2)], m, ph["u"])
                stages = [(minus_mean, 3)] if k < 2 else []
                stages += [(times_ns, 3)] if k == 1 else []
                stages += [(row_moments, 2)] if k < 2 else []
                pipelined(dve, EG, [(take_idx, 0)] + stages + [(match_of(ph), 2), (sums, 4), (finish, 5)])
                if k == 0:
                    need(dve, ph["upd"], 2 * EG)
                    degree_roots(nd[:], deg[:], [x_flat[2][:, i * ET:(i + 1) * ET] for i in range(4)], nd_made)


_INS = ['x', 'src', 'dst', 'edge_attr_32', 'edge_attr_96',
        'L0_gnn_mW1', 'L0_gnn_mb1', 'L0_gnn_mW2', 'L0_gnn_mb2', 'L0_gnn_gW1', 'L0_gnn_gb1', 'L0_gnn_gW2',
        'L0_gnn_gb2', 'L0_gnn_uW1', 'L0_gnn_ub1', 'L0_gnn_uW2', 'L0_gnn_ub2', 'L0_gnn_ln_g', 'L0_gnn_ln_b',
        'L1_gnn_Wm1', 'L1_gnn_bm1', 'L1_gnn_Wm2', 'L1_gnn_bm2', 'L1_gnn_Wu1', 'L1_gnn_bu1', 'L1_gnn_Wu2',
        'L1_gnn_bu2', 'L2_gnn_W', 'L2_gnn_b', 'L3_gnn_W0', 'L3_gnn_b0', 'L3_gnn_W1', 'L3_gnn_b1',
        'L3_gnn_W2', 'L3_gnn_b2']
_OUTS = [((100000, 96), 'float32')]


def kernel(**inputs):
    import numpy as _np
    import concourse.bacc as _bacc
    from concourse import mybir as _mybir
    from concourse.bass_utils import run_bass_kernel_spmd as _run

    nc = _bacc.Bacc("TRN2", target_bir_lowering=False, num_devices=1)
    arrays, aps = {}, {}
    for name in _INS:
        arr = _np.ascontiguousarray(inputs[name])
        arrays[f"in_{name}_dram"] = arr
        aps[name] = nc.dram_tensor(f"in_{name}_dram", arr.shape, _mybir.dt.from_np(arr.dtype), kind="ExternalInput").ap()
    out = nc.dram_tensor("out_0_dram", _OUTS[0][0], _mybir.dt.float32, kind="ExternalOutput").ap()
    build(nc, aps, out)
    r = _run(nc, [arrays], core_ids=[0])
    return r.results[0]["out_0_dram"]
```
